# Optimizing a Trainium2 kernel written in Bass

```python
import numpy as np
import jax
import jax.numpy as jnp

def _softmax(x, axis=-1):
    return jax.nn.softmax(x, axis=axis)

def _gelu(x):
    return jax.nn.gelu(x, approximate=True)

def _silu(x):
    return jax.nn.silu(x)

def _sigmoid(x):
    return jax.nn.sigmoid(x)

def _layernorm(x, axis=-1, eps=1e-05):
    m = jnp.mean(x, axis=axis, keepdims=True)
    v = jnp.var(x, axis=axis, keepdims=True)
    return (x - m) / jnp.sqrt(v + eps)

def _scatter_add(tgt, idx, src, axis=0):
    return tgt.at[idx].add(src)

def _segment_sum(src, seg, n):
    return jax.ops.segment_sum(src, seg, n)
kernel_name = 'mk_pixart_seq_d2_seqx_r4_99753f'

def setup_inputs(seed: int=0):
    np.random.seed(seed)
    _w = jnp.asarray

    def _rec_inputs():
        import jax
        import jax.numpy as jnp
        _rk = jax.random.key(seed)
        x = 7.22e-05 + 1 * jax.random.normal(jax.random.fold_in(_rk, 1), (4, 1024, 256), jnp.float32)
        _lenS = 1024 - jax.random.randint(jax.random.fold_in(_rk, 7), (4,), 0, max(1, 1024 // 4) + 1, jnp.int32)
        _lenS2 = 77 - jax.random.randint(jax.random.fold_in(_rk, 8), (4,), 0, max(1, 77 // 4) + 1, jnp.int32)
        cond_1024 = 0.000887014 + 1.03683 * jax.random.normal(jax.random.fold_in(_rk, 11), (4, 256), jnp.float32)
        _ctx_1024P = jax.random.normal(jax.random.fold_in(_rk, 12), (4, 16, 256), jnp.float32)
        _ctx_1024c = jax.random.dirichlet(jax.random.fold_in(_rk, 512), 0.3 * jnp.ones((16,), jnp.float32), (4, 77))
        _ctx_1024t = jnp.einsum('bsk,bkd->bsd', _ctx_1024c, _ctx_1024P)
        _ctx_1024t = _ctx_1024t * jax.lax.rsqrt(jnp.mean(jnp.square(_ctx_1024t)) + 1e-12) * 0.953939
        ctx_1024 = 0.00086875 + 0.999764 * (_ctx_1024t + 0.3 * jax.random.normal(jax.random.fold_in(_rk, 612), (4, 77, 256), jnp.float32))
        return (x, cond_1024, ctx_1024)
    x, cond_1024, ctx_1024 = _rec_inputs()

    def _L0_xcond_setup():
        import jax, jax.numpy as jnp
        import numpy as np
        C = 256
        H = 16
        D = C // H
        WIN = 128
        SHIFT = 64
        TOPK = 16
        HID = 1024
        EPS = 1e-06

        def _ln(x):
            x32 = x.astype(jnp.float32)
            m = x32.mean(-1, keepdims=True)
            v = jnp.mean((x32 - m) ** 2, axis=-1, keepdims=True)
            return ((x32 - m) * jax.lax.rsqrt(v + EPS)).astype(x.dtype)

        def _self_attn(h, w_qkv, b_qkv, w_so, b_so):
            B, L, _ = h.shape
            qkv = h @ w_qkv + b_qkv
            qkv = jnp.roll(qkv, -SHIFT, axis=1)
            nw = L // WIN
            qkv = qkv.reshape(B, nw, WIN, 3, H, D)
            q, k, v = (qkv[:, :, :, 0], qkv[:, :, :, 1], qkv[:, :, :, 2])
            scores = jnp.einsum('bnqhd,bnkhd->bnhqk', q, k) / jnp.sqrt(jnp.float32(D)).astype(h.dtype)
            attn = jax.nn.softmax(scores, axis=-1)
            o = jnp.einsum('bnhqk,bnkhd->bnqhd', attn, v).reshape(B, L, C)
            o = jnp.roll(o, SHIFT, axis=1)
            return o @ w_so + b_so

        def _topk_cross_attn(h, ctx, w_q, b_q, w_kv, b_kv, w_co, b_co):
            B, L, _ = h.shape
            Lc = ctx.shape[1]
            q = (h @ w_q + b_q).reshape(B, L, H, D)
            kv = (ctx @ w_kv + b_kv).reshape(B, Lc, 2, H, D)
            k, v = (kv[:, :, 0], kv[:, :, 1])
            scores = jnp.einsum('bqhd,bkhd->bhqk', q, k) / jnp.sqrt(jnp.float32(D)).astype(h.dtype)
            top_s, top_i = jax.lax.top_k(scores, TOPK)
            attn = jax.nn.softmax(top_s, axis=-1)
            v_bh = jnp.transpose(v, (0, 2, 1, 3))
            vg = jnp.take_along_axis(v_bh[:, :, None, :, :], top_i[..., None], axis=3)
            o = jnp.einsum('bhqk,bhqkd->bqhd', attn, vg).reshape(B, L, C)
            return o @ w_co + b_co

        def _swiglu(h, w_m1, b_m1, w_m2, b_m2):
            u = h @ w_m1 + b_m1
            a, b = (u[..., :HID], u[..., HID:])
            return jax.nn.silu(a) * b @ w_m2 + b_m2
        key = jax.random.key(seed)
        ks = jax.random.split(key, 24)
        s = 0.02
        inp = {'x': jax.random.normal(ks[0], (2, 1024, C), jnp.float32), 'mod': jax.random.normal(ks[1], (2, C), jnp.float32), 'context': jax.random.normal(ks[2], (2, 256, C), jnp.float32), 'w_ada': jax.random.normal(ks[3], (C, 9 * C), jnp.float32) * s, 'b_ada': jnp.zeros((9 * C,), jnp.float32), 'w_qkv': jax.random.normal(ks[4], (C, 3 * C), jnp.float32) * s, 'b_qkv': jnp.zeros((3 * C,), jnp.float32), 'w_so': jax.random.normal(ks[5], (C, C), jnp.float32) * s, 'b_so': jnp.zeros((C,), jnp.float32), 'w_q': jax.random.normal(ks[6], (C, C), jnp.float32) * s, 'b_q': jnp.zeros((C,), jnp.float32), 'w_kv': jax.random.normal(ks[7], (C, 2 * C), jnp.float32) * s, 'b_kv': jnp.zeros((2 * C,), jnp.float32), 'w_co': jax.random.normal(ks[8], (C, C), jnp.float32) * s, 'b_co': jnp.zeros((C,), jnp.float32), 'w_m1': jax.random.normal(ks[9], (C, 2 * HID), jnp.float32) * s, 'b_m1': jnp.zeros((2 * HID,), jnp.float32), 'w_m2': jax.random.normal(ks[10], (HID, C), jnp.float32) * s, 'b_m2': jnp.zeros((C,), jnp.float32)}
        return inp
    _L0_xcond_all = _L0_xcond_setup()
    _L0_xcond_in = {k: v for k, v in _L0_xcond_all.items() if k in ('w_ada', 'b_ada', 'w_qkv', 'b_qkv', 'w_so', 'b_so', 'w_q', 'b_q', 'w_kv', 'b_kv', 'w_co', 'b_co', 'w_m1', 'b_m1', 'w_m2', 'b_m2')}
    del _L0_xcond_all

    def _L1_xcond_setup():
        import jax, jax.numpy as jnp
        import numpy as np
        H = 256
        RH = 2 * H
        E = 3
        B, T, P = (8, 512, 64)
        LN_EPS = 1e-05

        def _layer_norm(x, gamma, beta):
            mu = jnp.mean(x, axis=-1, keepdims=True)
            var = jnp.mean(jnp.square(x - mu), axis=-1, keepdims=True)
            return (x - mu) * jax.lax.rsqrt(var + LN_EPS) * gamma + beta
        key = jax.random.key(seed)
        ks = jax.random.split(key, 24)
        s = lambda fan_in: 1.0 / np.sqrt(fan_in)
        inp = {'mix_hidden_states': jax.random.normal(ks[0], (B, T, H), jnp.float32), 'global_anchor': jax.random.normal(ks[1], (B, H), jnp.float32), 'prototype_bank': jax.random.normal(ks[2], (B, P, H), jnp.float32), 'ln_gamma': jnp.ones((H,), jnp.float32), 'ln_beta': jnp.zeros((H,), jnp.float32), 'Wq': jax.random.normal(ks[3], (H, H), jnp.float32) * s(H), 'Wk': jax.random.normal(ks[4], (H, H), jnp.float32) * s(H), 'Wv': jax.random.normal(ks[5], (H, H), jnp.float32) * s(H), 'router_W': jax.random.normal(ks[6], (3 * H, E), jnp.float32) * s(3 * H), 'router_b': jnp.zeros((E,), jnp.float32), 'e_w1': jax.random.normal(ks[7], (E, 3 * H, RH), jnp.float32) * s(3 * H), 'e_b1': jnp.zeros((E, RH), jnp.float32), 'e_w2': jax.random.normal(ks[8], (E, RH, H), jnp.float32) * s(RH), 'e_b2': jnp.zeros((E, H), jnp.float32), 'gate_w1': jax.random.normal(ks[9], (3 * H, H), jnp.float32) * s(3 * H), 'gate_b1': jnp.zeros((H,), jnp.float32), 'gate_w2': jax.random.normal(ks[10], (H, H), jnp.float32) * s(H), 'gate_b2': jnp.zeros((H,), jnp.float32), 'out_w': jax.random.normal(ks[11], (H, H), jnp.float32) * s(H), 'out_b': jnp.zeros((H,), jnp.float32)}
        return inp
    _L1_xcond_all = _L1_xcond_setup()
    _L1_xcond_in = {k: v for k, v in _L1_xcond_all.items() if k in ('ln_gamma', 'ln_beta', 'Wq', 'Wk', 'Wv', 'router_W', 'router_b', 'e_w1', 'e_b1', 'e_w2', 'e_b2', 'gate_w1', 'gate_b1', 'gate_w2', 'gate_b2', 'out_w', 'out_b')}
    del _L1_xcond_all
    return {'x': x, 'cond_1024': cond_1024, 'ctx_1024': ctx_1024, 'L0_xcond_w_ada': _L0_xcond_in['w_ada'], 'L0_xcond_b_ada': _L0_xcond_in['b_ada'], 'L0_xcond_w_qkv': _L0_xcond_in['w_qkv'], 'L0_xcond_b_qkv': _L0_xcond_in['b_qkv'], 'L0_xcond_w_so': _L0_xcond_in['w_so'], 'L0_xcond_b_so': _L0_xcond_in['b_so'], 'L0_xcond_w_q': _L0_xcond_in['w_q'], 'L0_xcond_b_q': _L0_xcond_in['b_q'], 'L0_xcond_w_kv': _L0_xcond_in['w_kv'], 'L0_xcond_b_kv': _L0_xcond_in['b_kv'], 'L0_xcond_w_co': _L0_xcond_in['w_co'], 'L0_xcond_b_co': _L0_xcond_in['b_co'], 'L0_xcond_w_m1': _L0_xcond_in['w_m1'], 'L0_xcond_b_m1': _L0_xcond_in['b_m1'], 'L0_xcond_w_m2': _L0_xcond_in['w_m2'], 'L0_xcond_b_m2': _L0_xcond_in['b_m2'], 'L1_xcond_ln_gamma': _L1_xcond_in['ln_gamma'], 'L1_xcond_ln_beta': _L1_xcond_in['ln_beta'], 'L1_xcond_Wq': _L1_xcond_in['Wq'], 'L1_xcond_Wk': _L1_xcond_in['Wk'], 'L1_xcond_Wv': _L1_xcond_in['Wv'], 'L1_xcond_router_W': _L1_xcond_in['router_W'], 'L1_xcond_router_b': _L1_xcond_in['router_b'], 'L1_xcond_e_w1': _L1_xcond_in['e_w1'], 'L1_xcond_e_b1': _L1_xcond_in['e_b1'], 'L1_xcond_e_w2': _L1_xcond_in['e_w2'], 'L1_xcond_e_b2': _L1_xcond_in['e_b2'], 'L1_xcond_gate_w1': _L1_xcond_in['gate_w1'], 'L1_xcond_gate_b1': _L1_xcond_in['gate_b1'], 'L1_xcond_gate_w2': _L1_xcond_in['gate_w2'], 'L1_xcond_gate_b2': _L1_xcond_in['gate_b2'], 'L1_xcond_out_w': _L1_xcond_in['out_w'], 'L1_xcond_out_b': _L1_xcond_in['out_b']}

def reference(x, cond_1024, ctx_1024, L0_xcond_w_ada, L0_xcond_b_ada, L0_xcond_w_qkv, L0_xcond_b_qkv, L0_xcond_w_so, L0_xcond_b_so, L0_xcond_w_q, L0_xcond_b_q, L0_xcond_w_kv, L0_xcond_b_kv, L0_xcond_w_co, L0_xcond_b_co, L0_xcond_w_m1, L0_xcond_b_m1, L0_xcond_w_m2, L0_xcond_b_m2, L1_xcond_ln_gamma, L1_xcond_ln_beta, L1_xcond_Wq, L1_xcond_Wk, L1_xcond_Wv, L1_xcond_router_W, L1_xcond_router_b, L1_xcond_e_w1, L1_xcond_e_b1, L1_xcond_e_w2, L1_xcond_e_b2, L1_xcond_gate_w1, L1_xcond_gate_b1, L1_xcond_gate_w2, L1_xcond_gate_b2, L1_xcond_out_w, L1_xcond_out_b):
    import jax
    import jax.numpy as jnp

    def _L0_xcond_ref(x, mod, context, w_ada, b_ada, w_qkv, b_qkv, w_so, b_so, w_q, b_q, w_kv, b_kv, w_co, b_co, w_m1, b_m1, w_m2, b_m2):
        import jax, jax.numpy as jnp
        import numpy as np
        C = 256
        H = 16
        D = C // H
        WIN = 128
        SHIFT = 64
        TOPK = 16
        HID = 1024
        EPS = 1e-06

        def _ln(x):
            x32 = x.astype(jnp.float32)
            m = x32.mean(-1, keepdims=True)
            v = jnp.mean((x32 - m) ** 2, axis=-1, keepdims=True)
            return ((x32 - m) * jax.lax.rsqrt(v + EPS)).astype(x.dtype)

        def _self_attn(h, w_qkv, b_qkv, w_so, b_so):
            B, L, _ = h.shape
            qkv = h @ w_qkv + b_qkv
            qkv = jnp.roll(qkv, -SHIFT, axis=1)
            nw = L // WIN
            qkv = qkv.reshape(B, nw, WIN, 3, H, D)
            q, k, v = (qkv[:, :, :, 0], qkv[:, :, :, 1], qkv[:, :, :, 2])
            scores = jnp.einsum('bnqhd,bnkhd->bnhqk', q, k) / jnp.sqrt(jnp.float32(D)).astype(h.dtype)
            attn = jax.nn.softmax(scores, axis=-1)
            o = jnp.einsum('bnhqk,bnkhd->bnqhd', attn, v).reshape(B, L, C)
            o = jnp.roll(o, SHIFT, axis=1)
            return o @ w_so + b_so

        def _topk_cross_attn(h, ctx, w_q, b_q, w_kv, b_kv, w_co, b_co):
            B, L, _ = h.shape
            Lc = ctx.shape[1]
            q = (h @ w_q + b_q).reshape(B, L, H, D)
            kv = (ctx @ w_kv + b_kv).reshape(B, Lc, 2, H, D)
            k, v = (kv[:, :, 0], kv[:, :, 1])
            scores = jnp.einsum('bqhd,bkhd->bhqk', q, k) / jnp.sqrt(jnp.float32(D)).astype(h.dtype)
            top_s, top_i = jax.lax.top_k(scores, TOPK)
            attn = jax.nn.softmax(top_s, axis=-1)
            v_bh = jnp.transpose(v, (0, 2, 1, 3))
            vg = jnp.take_along_axis(v_bh[:, :, None, :, :], top_i[..., None], axis=3)
            o = jnp.einsum('bhqk,bhqkd->bqhd', attn, vg).reshape(B, L, C)
            return o @ w_co + b_co

        def _swiglu(h, w_m1, b_m1, w_m2, b_m2):
            u = h @ w_m1 + b_m1
            a, b = (u[..., :HID], u[..., HID:])
            return jax.nn.silu(a) * b @ w_m2 + b_m2
        m = jax.nn.silu(mod) @ w_ada + b_ada
        sh_msa, sc_msa, g_msa, sh_mca, sc_mca, g_mca, sh_mlp, sc_mlp, g_mlp = [m[:, i * C:(i + 1) * C][:, None, :] for i in range(9)]
        h = _ln(x) * (1 + sc_msa) + sh_msa
        h = _self_attn(h, w_qkv, b_qkv, w_so, b_so)
        x = x + h * g_msa
        h = _ln(x) * (1 + sc_mca) + sh_mca
        h = _topk_cross_attn(h, context, w_q, b_q, w_kv, b_kv, w_co, b_co)
        x = x + h * g_mca
        h = _ln(x) * (1 + sc_mlp) + sh_mlp
        h = _swiglu(h, w_m1, b_m1, w_m2, b_m2)
        x = x + h * g_mlp
        return x

    def _L1_xcond_ref(mix_hidden_states, global_anchor, prototype_bank, ln_gamma, ln_beta, Wq, Wk, Wv, router_W, router_b, e_w1, e_b1, e_w2, e_b2, gate_w1, gate_b1, gate_w2, gate_b2, out_w, out_b):
        import jax, jax.numpy as jnp
        import numpy as np
        H = 256
        RH = 2 * H
        E = 3
        B, T, P = (8, 512, 64)
        LN_EPS = 1e-05

        def _layer_norm(x, gamma, beta):
            mu = jnp.mean(x, axis=-1, keepdims=True)
            var = jnp.mean(jnp.square(x - mu), axis=-1, keepdims=True)
            return (x - mu) * jax.lax.rsqrt(var + LN_EPS) * gamma + beta
        x = mix_hidden_states
        nx = _layer_norm(x, ln_gamma, ln_beta)
        q = nx @ Wq
        k = prototype_bank @ Wk
        v = prototype_bank @ Wv
        scores = jnp.einsum('bth,bph->btp', q, k) * H ** (-0.5)
        weights = jax.nn.softmax(scores, axis=-1)
        evidence = jnp.einsum('btp,bph->bth', weights, v)
        anchor = jnp.broadcast_to(global_anchor[:, None, :], nx.shape)
        combined = jnp.concatenate([nx, evidence, anchor], axis=-1)
        router_logits = combined @ router_W + router_b
        router_probs = jax.nn.softmax(router_logits, axis=-1)
        h = jax.nn.silu(jnp.einsum('btc,ecr->bter', combined, e_w1) + e_b1)
        expert_out = jnp.einsum('bter,erh->bteh', h, e_w2) + e_b2
        routed = jnp.sum(expert_out * router_probs[..., None], axis=-2)
        g = jax.nn.sigmoid(jax.nn.silu(combined @ gate_w1 + gate_b1) @ gate_w2 + gate_b2)
        refined_delta = g * (routed @ out_w + out_b)
        return x + refined_delta
    x = _L0_xcond_ref(x, cond_1024, ctx_1024, L0_xcond_w_ada, L0_xcond_b_ada, L0_xcond_w_qkv, L0_xcond_b_qkv, L0_xcond_w_so, L0_xcond_b_so, L0_xcond_w_q, L0_xcond_b_q, L0_xcond_w_kv, L0_xcond_b_kv, L0_xcond_w_co, L0_xcond_b_co, L0_xcond_w_m1, L0_xcond_b_m1, L0_xcond_w_m2, L0_xcond_b_m2)
    x = _L1_xcond_ref(x, cond_1024, ctx_1024, L1_xcond_ln_gamma, L1_xcond_ln_beta, L1_xcond_Wq, L1_xcond_Wk, L1_xcond_Wv, L1_xcond_router_W, L1_xcond_router_b, L1_xcond_e_w1, L1_xcond_e_b1, L1_xcond_e_w2, L1_xcond_e_b2, L1_xcond_gate_w1, L1_xcond_gate_b1, L1_xcond_gate_w2, L1_xcond_gate_b2, L1_xcond_out_w, L1_xcond_out_b)
    return x

_drawn_inputs = setup_inputs


def setup_inputs(seed=0):
    import zlib

    import numpy as np

    out = dict(_drawn_inputs(seed))
    spreads = {'L0_xcond_b_ada': (0.0, 0.396),
     'L0_xcond_b_qkv': (0.0, 0.8),
     'L0_xcond_b_so': (0.0, 0.374),
     'L0_xcond_b_q': (0.0, 0.8),
     'L0_xcond_b_kv': (0.0, 0.8),
     'L0_xcond_b_co': (0.0, 0.396),
     'L0_xcond_b_m1': (0.0, 0.8),
     'L0_xcond_b_m2': (0.0, 1.436),
     'L1_xcond_ln_gamma': (1.0, 0.6),
     'L1_xcond_ln_beta': (0.0, 2.0),
     'L1_xcond_router_b': (0.0, 2.0),
     'L1_xcond_e_b1': (0.0, 2.0),
     'L1_xcond_e_b2': (0.0, 0.8),
     'L1_xcond_gate_b1': (0.0, 2.0),
     'L1_xcond_gate_b2': (0.0, 2.0),
     'L1_xcond_out_b': (0.0, 0.8)}
    factors = {'L0_xcond_w_qkv': 8.0,
     'L0_xcond_w_so': 6.098,
     'L0_xcond_w_q': 7.352,
     'L0_xcond_w_kv': 3.901,
     'L0_xcond_w_co': 3.498,
     'L0_xcond_w_m1': 6.141,
     'L0_xcond_w_m2': 6.124,
     'L1_xcond_Wq': 8.0,
     'L1_xcond_Wk': 8.0,
     'L1_xcond_Wv': 4.574,
     'L1_xcond_router_W': 3.705,
     'L1_xcond_gate_w1': 6.683,
     'L1_xcond_gate_w2': 4.724}
    for name, (base, spread) in spreads.items():
        noise = np.random.default_rng([zlib.crc32(name.encode()), seed]).standard_normal(out[name].shape)
        drawn = base * np.exp(spread * noise) if base else spread * noise
        out[name] = jnp.asarray(drawn.astype(out[name].dtype))
    for name, factor in factors.items():
        out[name] = (out[name] * factor).astype(out[name].dtype)
    return out
```

```python
from contextlib import ExitStack

import concourse.bass as bass
from concourse import mybir

F32 = mybir.dt.float32
BF16 = mybir.dt.bfloat16
ALU = mybir.AluOpType
ACT = mybir.ActivationFunctionType
AX = mybir.AxisListType

P = 128
NB, L, C = 4, 1024, 256
CB = C // P
WIN, SHIFT = 128, 64
TILES = 2
UT = TILES * WIN
UNITS = L // UT
H, D = 16, 16
SLOTS, PAIR, PAR = 4, 2, 2
HPS = PAIR * PAR
LC = 77
DV = D + 1
HID = 1024
HJ = HID // P
E = 3
RH = 2 * C
RB = RH // P
W1N = E * RH + C
W1B = W1N // P
EPS0, EPS1 = 1e-6, 1e-5
KNOCKED = -3.0e38
KNOCKED_BELOW = -2.9e38

_slots = ["s0", "p0", "s1", "p1"]
_cross = ["c0", "c1", "y0", "y1"]
BANK_JOBS = [
    ["ln1"] + [f"{x}{0}" for x in _slots] + ["o1"] + [f"{x}{0}" for x in _cross] + ["o2"],
    ["q"] + [f"{x}{1}" for x in _slots] + ["so"] + [f"{x}{1}" for x in _cross] + ["co"],
    ["k"] + [f"{x}{2}" for x in _slots] + ["ln2"] + [f"{x}{2}" for x in _cross],
    ["v"] + [f"{x}{3}" for x in _slots] + ["q2"] + [f"{x}{3}" for x in _cross],
    ["pv0", "pv1", "xv0", "xv1"],
    ["ln3", "m1", "m3", "m5", "m7", "wt", "h01", "h11", "h21"],
    ["m0", "m2", "m4", "m6", "ln4", "h00", "h10", "h20", "hg"],
    ["mo", "ps", "rt", "e0", "e1", "e2", "g2"],
]
JOB = {name: (bank, i, len(jobs)) for bank, jobs in enumerate(BANK_JOBS) for i, name in enumerate(jobs)}

COLS = {}
_n = 0
for _name, _k in (("ada", 9 * CB), ("qkv", 3 * CB), ("q", CB), ("kv", 2 * CB), ("m1", 2 * HJ), ("gamma", CB),
                  ("beta", CB), ("e_b1", E * RB), ("gate_b1", CB), ("cond", NB * CB), ("e_b2", E * CB)):
    COLS[_name] = _n
    _n += _k
NCOL = _n

TANH_ORDER = [f"m{j}" for j in range(HJ)] + ["h00", "h01", "h10", "h11", "h20", "h21", "hg"]
TOPK_PER_UNIT = TILES * SLOTS * 4 * HPS

N_BIAS = 7
N_CONST = 9 + N_BIAS
STEP_SILU = 4
STEP_END = STEP_SILU + 4 * NB + 3 + E + 8 * (E + 1)
INIT_ADA_READ = 2 + 3 * NB
INIT_TURNS = INIT_ADA_READ + 2 + E + NB
INIT_E2_READ = INIT_TURNS + 4 + 2 * CB + 2
STEPS_A = 1 + 2 * (1 + 8)
STEPS_B = 5 + 8


def topk_base(t, s):
    return (t * SLOTS + s) * 4 * HPS


def tb_of(name):
    return JOB[name][0] - 5


def bass_pixart_experts(nc, x, cond, ctx_in, w_ada, b_ada, w_qkv, b_qkv, w_so, b_so, w_q, b_q, w_kv, b_kv,
                        w_co, b_co, w_m1, b_m1, w_m2, b_m2, gamma, beta, wq1, wk1, wv1, router_w, router_b,
                        e_w1, e_b1, e_w2, e_b2, gate_w1, gate_b1, gate_w2, gate_b2, out_w, out_b, out):
    x_rows = x.rearrange("b l c -> (b l) c")
    out_rows = out.rearrange("b l c -> (b l) c")
    ctx_rows = ctx_in.rearrange("b l c -> (b l) c")

    with ExitStack() as stack:
        def sb(name, shape, dt=F32):
            return stack.enter_context(nc.sbuf_tensor(name, shape, dt))

        def sem(name):
            return stack.enter_context(nc.semaphore(name))

        Wqkv = sb("Wqkv", [P, CB, 3 * C])
        Wso = sb("Wso", [P, CB, C])
        Wso_g = sb("Wso_g", [P, CB, C])
        Wq2 = sb("Wq2", [P, CB, C])
        Wkv = sb("Wkv", [P, CB, 2 * C])
        Wco = sb("Wco", [P, CB, C])
        Wco_g = sb("Wco_g", [P, CB, C])
        Wm1 = sb("Wm1", [P, CB, 2 * HID])
        Wm2_g = sb("Wm2_g", [P, HJ, C])
        W1nx = sb("W1nx", [P, CB, W1N])
        W1ev = sb("W1ev", [P, CB, W1N])
        Rw = sb("Rw", [P, 3 * CB, E])
        W2p = sb("W2p", [P, E * RB, C])
        Wg2 = sb("Wg2", [P, CB, C])
        MT = sb("MT", [P, CB, C])
        Wv1 = sb("Wv1", [P, CB, C])
        ident = sb("ident", [P, P])
        cols = sb("cols", [P, NCOL])
        b1half = sb("b1half", [P, HJ])
        Gall = sb("Gall", [P, NB * 3, C])
        mods = sb("mods", [P, NB, 12])
        betas = sb("betas", [P, NB, W1B])
        rbias_all = sb("rbias_all", [P, NB, E])
        maskE = sb("maskE", [P, 1])
        maskO = sb("maskO", [P, 1])
        neghalf = sb("neghalf", [P, TILES])
        ones3 = sb("ones3", [96, P], BF16)
        onesf = sb("onesf", [1, P])
        rows = sb("rows", [1, 4, C])
        bias3 = {n: sb(f"bias3_{n}", [96, TILES, C], BF16) for n in ("so", "co", "mo", "e0", "e1", "e2", "g2")}
        split = sb("split", [1, 2, C])
        split_b = sb("split_b", [1, C], BF16)

        modA = sb("modA", [P, 8])
        modB = sb("modB", [P, 4])
        ctx_sb = sb("ctx_sb", [LC, C])
        ctxT = sb("ctxT", [P, CB, LC])
        kc = [sb(f"kc{e}", [P, CB, LC]) for e in range(PAR)]
        vc = sb("vc", [LC, H, DV])
        vT1 = sb("vT1", [P, CB, LC])
        Gp = sb("Gp", [P, CB, LC])
        Vp = sb("Vp", [LC, W1N + E])
        betaF = sb("betaF", [P, W1B])
        betaH = sb("betaH", [P, W1B])
        rbias = sb("rbias", [P, E])

        xin = sb("xin", [P, TILES, C])
        x1 = sb("x1", [P, TILES, C])
        x2 = sb("x2", [P, TILES, C])
        xnA = sb("xnA", [P, TILES, C])
        xnB = sb("xnB", [P, TILES, C])
        stat = [sb(f"stat{i}", [P, TILES, 6]) for i in range(4)]
        mv = [sb(f"mv{i}", [P, TILES, 2]) for i in range(4)]
        vare = [sb(f"vare{i}", [P, TILES]) for i in range(4)]
        rstd = [sb(f"rstd{i}", [P, TILES]) for i in range(4)]
        hA = sb("hA", [P, CB, UT])
        qT = sb("qT", [P, CB, UT])
        keys_or_knocked = sb("keys_or_knocked", [P, 3 * CB * UT])
        kT, *km = [keys_or_knocked[:, i * CB * UT:(i + 1) * CB * UT].rearrange("p (f t) -> p f t", f=CB) for i in range(3)]
        K = keys_or_knocked[:, 0:H * LC].rearrange("p (h c) -> p h c", h=H)
        va = sb("va", [P, TILES, H, DV])
        rmax = sb("rmax", [P, TILES, H])
        prob_or_scores = sb("prob_or_scores", [P, TILES * H * LC])
        prob = prob_or_scores[:, 0:H * P].rearrange("p (s i k) -> p s i k", s=SLOTS, i=HPS)
        S = prob_or_scores[:, :].rearrange("p (t h c) -> p t h c", t=TILES, h=H)
        probT = sb("probT", [P, SLOTS, HPS, P])
        rsum = sb("rsum", [P, TILES, H])
        on, oT, q2T = xnA, hA, qT
        Dx = sb("Dx", [P, TILES, H, LC])
        M1 = sb("M1", [P, TILES, H, 8])
        M2 = sb("M2", [P, H, 8])

        hB = sb("hB", [P, CB, UT])
        nxT = hB
        tb = [sb(f"tb{i}", [P, 2 * UT]) for i in range(2)]
        gT = sb("gT", [P, HJ, UT])
        hE = gT[:, :, :].rearrange("p (a k) t -> p a k t", a=2)
        pw = sb("pw", [P, TILES, LC])
        pm = sb("pm", [P, TILES])
        psu = sb("psu", [P, TILES])
        wT = sb("wT", [LC, UT])
        rl = sb("rl", [P, TILES, E])
        rm = sb("rm", [P, TILES])
        rs = sb("rs", [P, TILES])
        rp = sb("rp", [P, TILES, E])
        gs = xnB
        acc = sb("acc", [P, TILES, C])
        tg = tb[0]

        colrows = tb[1][0:NCOL, 0:P]
        big = [Dx[:, :, :, :].rearrange("p t h c -> p (t h c)"), prob_or_scores[:, :]]
        Wada = [r[:, 0:9 * C] for r in big]
        W1an = [r[:, 0:W1N] for r in big]
        wk_sb, wq_sb, outw = hA, qT, kT
        wkT, wqT = km[0], km[1]
        ew2 = gT
        e2Tv = prob_or_scores[:, 0:CB * RB * P].rearrange("p (a k) -> p a k", a=CB)
        modBc = xnB
        siluT = sb("siluT", [P, NB, CB])
        tanhT = sb("tanhT", [P, NB, CB])

        psum = [stack.enter_context(nc.psum_tensor(f"bank{i}", [P, 512], F32)) for i in range(8)]

        full = [sem(f"full{i}") for i in range(8)]
        drained = [sem(f"drained{i}") for i in range(8)]
        x_loaded, y_ready, y_stored = sem("x_loaded"), sem("y_ready"), sem("y_stored")
        stats = [sem(f"ln_stats{i}") for i in range(4)]
        rstds = [sem(f"ln_rstd{i}") for i in range(4)]
        normed = [sem(f"normed{i}") for i in range(4)]
        keys_masked, row_max, probs = sem("keys_masked"), sem("row_max"), sem("probs")
        sums_inverted = sem("sums_inverted")
        topk, shifted, cross_exp, picked = sem("topk"), sem("shifted"), sem("cross_exp"), sem("picked")
        tanh_done, plus_one, half_gated = sem("tanh_done"), sem("plus_one"), sem("half_gated")
        proto_max, proto_exp, proto_steps = sem("proto_max"), sem("proto_exp"), sem("proto_steps")
        route_steps, route_exp, route_done = sem("route_steps"), sem("route_exp"), sem("route_done")
        mixed, gate_tanh = sem("mixed"), sem("gate_tanh")
        w_loaded, wm2_loaded, big_loaded, ew2_loaded, ctx_loaded = sem("w_loaded"), sem("wm2_loaded"), sem("big_loaded"), sem("ew2_loaded"), sem("ctx_loaded")
        consts, dve_step, init_full, init_read, init_tanh = sem("consts"), sem("dve_step"), sem("init_full"), sem("init_read"), sem("init_tanh")
        fullA, readA, doneA, gatedA = sem("prepA_full"), sem("prepA_read"), sem("prepA_done"), sem("gatedA")
        fullB, readB, doneB, gatedB = sem("prepB_full"), sem("prepB_read"), sem("prepB_done"), sem("gatedB")
        stepA, stepB = sem("prepA_step"), sem("prepB_step")

        passed = sem("passed")
        rrow = sb("rrow", [1, E])
        ROW = {"so": rows[0:1, 0, :], "co": rows[0:1, 1, :], "m2": rows[0:1, 2, :], "tmp": rows[0:1, 3, :],
               "gs": x1[0:1, 0, :], "gc": x1[0:1, 1, :], "gm": x2[0:1, 0, :], "out": x2[0:1, 1, :], "e0": acc[0:1, 0, :],
               "e1": acc[0:1, 1, :], "e2": xnA[0:1, 0, :], "g2": xnA[0:1, 1, :]}

        def row(n):
            return ROW[n]

        def wait_full(eng, name, u):
            bank, i, n = JOB[name]
            eng.wait_ge(full[bank], u * n + (i + 1))

        def wait_drained(eng, name, u):
            bank, i, n = JOB[name]
            eng.wait_ge(drained[bank], u * n + (i + 2))

        def wait_free(eng, name, u):
            bank, i, n = JOB[name]
            eng.wait_ge(drained[bank], u * n + (i + 1))

        def alone(eng):
            eng.sem_inc(passed, 1)

        def bank_of(name):
            return psum[JOB[name][0]]

        HEADS = [(s, j, e) for s in range(SLOTS) for j in range(PAIR) for e in range(PAR)]

        def head(s, i):
            return 8 * (i // PAR) + 2 * s + i % PAR

        col_loads = [("ada", b_ada, 9 * CB), ("qkv", b_qkv, 3 * CB), ("q", b_q, CB), ("kv", b_kv, 2 * CB), ("m1", b_m1, 2 * HJ),
                     ("gamma", gamma, CB), ("beta", beta, CB), ("e_b1", e_b1.rearrange("e r -> (e r)"), E * RB),
                     ("gate_b1", gate_b1, CB), ("cond", cond.rearrange("b c -> (b c)"), NB * CB),
                     ("e_b2", e_b2.rearrange("e c -> (e c)"), E * CB)]

        def blocks(w):
            return w.rearrange("(k p) n -> p k n", p=P)

        def rank1(v):
            return v.rearrange("(a n) -> a n", a=1)

        ew1 = [e_w1[e].rearrange("(k p) n -> p k n", p=P) for e in range(E)]
        gw1 = blocks(gate_w1)

        def part_loads(dst, part):
            k = slice(part * CB, (part + 1) * CB)
            return [(dst[:, :, e * RH:(e + 1) * RH], ew1[e][:, k, :]) for e in range(E)] + \
                   [(dst[:, :, E * RH:W1N], gw1[:, k, :])]

        small_loads = [(colrows[COLS[n]:COLS[n] + k, :], v.rearrange("(k p) -> k p", p=P)) for n, v, k in col_loads]
        small_loads += [(row("gs"), rank1(b_ada[2 * C:3 * C])), (row("gc"), rank1(b_ada[5 * C:6 * C])),
                        (row("gm"), rank1(b_ada[8 * C:9 * C])), (row("so"), rank1(b_so)), (row("co"), rank1(b_co)),
                        (row("m2"), rank1(b_m2)), (row("g2"), rank1(gate_b2)), (row("out"), rank1(out_b)),
                        (rrow[:, :], rank1(router_b))]
        big_loads = [(Wada[k], w_ada[k * P:(k + 1) * P, :]) for k in range(CB)]
        weight_loads = [(Wqkv[:, :, :], blocks(w_qkv)), (Wso[:, :, :], blocks(w_so)), (Wq2[:, :, :], blocks(w_q)),
                        (Wkv[:, :, :], blocks(w_kv)), (Wco[:, :, :], blocks(w_co)),
                        (wk_sb[:, :, :], blocks(wk1)), (wq_sb[:, :, :], blocks(wq1)), (outw[:, :, :], blocks(out_w)),
                        (Wv1[:, :, :], blocks(wv1)), (Wg2[:, :, :], blocks(gate_w2)), (Rw[:, :, :], blocks(router_w)),
                        (Wm1[:, :, :], blocks(w_m1))] + part_loads(W1nx, 0) + part_loads(W1ev, 1)
        anchor_loads = [(W1an[k][:, e * RH:(e + 1) * RH], ew1[e][:, 2 * CB + k, :]) for k in range(CB) for e in range(E)] + \
                       [(W1an[k][:, E * RH:W1N], gw1[:, 2 * CB + k, :]) for k in range(CB)]
        N_SMALL, N_W, N_AN = len(small_loads), len(weight_loads), len(anchor_loads)
        e2_rows = e_w2.rearrange("e (k p) n -> p (e k) n", p=P)
        EW = [(0, 4), (4, 8), (8, 12)]

        block = stack.enter_context(nc.Block())

        @block.sync
        def _(sp):
            for s in (*drained, mixed):
                sp.sem_inc(s, 1)
            sp.sem_inc(y_stored, 16)
            for dst, src in small_loads:
                sp.dma_start(dst, src).then_inc(w_loaded, 16)
            for dst, src in big_loads:
                sp.dma_start(dst, src).then_inc(big_loaded, 16)
            for dst, src in weight_loads:
                sp.dma_start(dst, src).then_inc(w_loaded, 16)
            sp.dma_start(ew2[:, :, :], e2_rows[:, 0:8, :]).then_inc(ew2_loaded, 16)
            sp.wait_ge(init_read, INIT_ADA_READ)
            for dst, src in anchor_loads:
                sp.dma_start(dst, src).then_inc(big_loaded, 16)
            sp.wait_ge(init_read, INIT_E2_READ)
            sp.dma_start(ew2[:, 0:4, :], e2_rows[:, 8:12, :]).then_inc(ew2_loaded, 16)

            def spans(u):
                at = ((u >> 2) & 3) * L
                uu = u & 3
                first = at + uu * UT + SHIFT
                return first, first + WIN, at + ((uu + 1) & 3) * UT

            def load_x(u):
                r0, r1, r2 = spans(u)
                sp.dma_start(xin[:, 0, :], x_rows[bass.ds(r0, WIN), :]).then_inc(x_loaded, 16)
                sp.dma_start(xin[0:SHIFT, 1, :], x_rows[bass.ds(r1, SHIFT), :]).then_inc(x_loaded, 16)
                sp.dma_start(xin[SHIFT:WIN, 1, :], x_rows[bass.ds(r2, SHIFT), :]).then_inc(x_loaded, 16)

            def store_y(u):
                r0, r1, r2 = spans(u)
                sp.wait_ge(y_ready, u + 1)
                alone(sp)
                sp.dma_start(out_rows[bass.ds(r0, WIN), :], acc[:, 0, :]).then_inc(y_stored, 16)
                sp.dma_start(out_rows[bass.ds(r1, SHIFT), :], acc[0:SHIFT, 1, :]).then_inc(y_stored, 16)
                sp.dma_start(out_rows[bass.ds(r2, SHIFT), :], acc[SHIFT:WIN, 1, :]).then_inc(y_stored, 16)

            def load_wm2():
                sp.dma_start(Wm2_g[:, :, :], blocks(w_m2)).then_inc(wm2_loaded, 16)

            def load_ctx(b):
                sp.dma_start(ctx_sb[:, :], ctx_rows[bass.ds((b & 3) * LC, LC), :]).then_inc(ctx_loaded, 16)

            load_ctx(0)
            load_x(0)
            load_wm2()
            with sp.Fori(0, NB) as b:
                sp.wait_ge(fullA, b * 3 + 1)
                alone(sp)
                load_ctx(b + 1)
                with sp.Fori(0, UNITS - 1) as r:
                    u = b * UNITS + r
                    wait_drained(sp, "so", u)
                    alone(sp)
                    load_x(u + 1)
                    store_y(u)
                u = b * UNITS + (UNITS - 1)
                wait_drained(sp, "so", u)
                alone(sp)
                load_x(u + 1)
                wait_full(sp, "mo", u)
                alone(sp)
                load_wm2()
                store_y(u)
            sp.wait_ge(wm2_loaded, 16 * (NB + 1))
            sp.wait_ge(y_stored, 48 * NB * UNITS + 16)
            sp.wait_ge(x_loaded, 48 * (NB * UNITS + 1))
            sp.wait_ge(ctx_loaded, 16 * (NB + 1))

        @block.tensor
        def _(pe):
            pe_job = [0]

            def init_job(n=1):
                k = pe_job[0]
                pe_job[0] += 1
                if k >= 8:
                    pe.wait_ge(init_read, k - 7)
                return psum[k % 8]

            def prep_weights():
                pe.wait_ge(consts, N_CONST)
                pe.wait_ge(w_loaded, 16 * (N_SMALL + N_W))
                bk = init_job()
                pe.transpose(bk[:, 0:NCOL], colrows[:, :], ident[0:NCOL, 0:NCOL]).then_inc(init_full, 1)
                pe.wait_ge(init_read, 1)
                pe.wait_ge(dve_step, STEP_SILU)
                pe.wait_ge(big_loaded, 16 * CB)
                bk = init_job()
                for n, sec in enumerate((1, 0, 4, 3, 7, 6)):
                    for f in range(CB):
                        o = bk[:, (n * CB + f) * NB:(n * CB + f + 1) * NB]
                        for k in range(CB):
                            m = pe.matmul(o, Wada[k][:, sec * C + f * P:sec * C + (f + 1) * P], siluT[:, :, k],
                                          start=(k == 0), stop=(k == CB - 1))
                m.then_inc(init_full, 1)
                for b in range(NB):
                    pe.wait_ge(dve_step, STEP_SILU + 2 * (b + 1))
                    for g, (sec, r) in enumerate(((2, "gs"), (5, "gc"), (8, "gm"))):
                        bk = init_job()
                        for k in range(CB):
                            pe.matmul(bk[:, 0:C], modBc[:, k, 0:P], Wada[k][:, sec * C:(sec + 1) * C], start=(k == 0), stop=False)
                        pe.matmul(bk[:, 0:C], onesf[:, :], row(r), start=False, stop=True).then_inc(init_full, 1)
                for col, w in ((COLS["qkv"] + 2 * CB, Wso), (COLS["kv"] + CB, Wco)):
                    bk = init_job()
                    for k in range(CB):
                        m = pe.matmul(bk[0:1, 0:C], cols[:, col + k:col + k + 1], w[:, k, :], start=(k == 0), stop=(k == CB - 1))
                    m.then_inc(init_full, 1)
                for e in range(E):
                    bk = init_job()
                    for k in range(CB):
                        col = COLS["e_b2"] + e * CB + k
                        m = pe.matmul(bk[0:1, 0:C], cols[:, col:col + 1], outw[:, k, :], start=(k == 0), stop=(k == CB - 1))
                    m.then_inc(init_full, 1)
                for b in range(NB):
                    pe.wait_ge(dve_step, STEP_SILU + 2 * NB + 2 * (b + 1))
                    bk = init_job()
                    for k in range(CB):
                        pe.matmul(bk[:, 0:E], modBc[:, k, 0:P], Rw[:, 2 * CB + k, :], start=(k == 0), stop=False)
                    pe.matmul(bk[:, 0:E], onesf[:, :], rrow[:, :], start=False, stop=True).then_inc(init_full, 1)
                for w in (wk_sb, wq_sb):
                    bk = init_job()
                    for k in range(CB):
                        for h in range(CB):
                            m = pe.transpose(bk[:, h * C + k * P:h * C + (k + 1) * P], w[:, k, h * P:(h + 1) * P], ident[:, :])
                    m.then_inc(init_full, 1)
                pe.wait_ge(init_read, pe_job[0])
                bk = init_job()
                for c in range(CB):
                    for h in range(CB):
                        m = pe.matmul(bk[:, c * C:(c + 1) * C], wkT[:, h, c * P:(c + 1) * P], wqT[:, h, :], start=(h == 0), stop=(h == CB - 1))
                m.then_inc(init_full, 1)
                pe.wait_ge(big_loaded, 16 * (CB + N_AN))
                bk = init_job()
                condT = cols[:, COLS["cond"]:COLS["cond"] + NB * CB].rearrange("p (b k) -> p b k", k=CB)
                for n in range(W1B):
                    for k in range(CB):
                        m = pe.matmul(bk[:, n * NB:(n + 1) * NB], W1an[k][:, n * P:(n + 1) * P], condT[:, :, k],
                                      start=(k == 0), stop=(k == CB - 1))
                m.then_inc(init_full, 1)
                for e in range(E):
                    pe.wait_ge(ew2_loaded, 16 if e < 2 else 32)
                    src = e * RB if e < 2 else 0
                    for h in range(CB):
                        bk = init_job()
                        for k in range(RB):
                            m = pe.transpose(bk[:, k * P:(k + 1) * P], ew2[:, src + k, h * P:(h + 1) * P], ident[:, :])
                        m.then_inc(init_full, 1)
                    pe.wait_ge(init_read, pe_job[0])
                    for k2 in range(RB // 2):
                        bk = init_job()
                        for k in (2 * k2, 2 * k2 + 1):
                            for h in range(CB):
                                m = pe.matmul(bk[:, (k % 2) * C:(k % 2 + 1) * C], e2Tv[:, h, k * P:(k + 1) * P], outw[:, h, :],
                                              start=(h == 0), stop=(h == CB - 1))
                        m.then_inc(init_full, 1)
                pe.wait_ge(init_read, pe_job[0])
                pe.wait_ge(dve_step, STEP_END)

            def prep_a(b, units):
                pe.wait_ge(ctx_loaded, b * 16 + 16)
                if not isinstance(units, int):
                    for i in range(4):
                        pe.wait_ge(drained[i], units * len(BANK_JOBS[i]) + 1)
                for k in range(CB):
                    m = pe.transpose(psum[0][:, k * LC:(k + 1) * LC], ctx_sb[:, k * P:(k + 1) * P], ident[0:LC, 0:LC])
                m.then_inc(fullA, 1)
                pe.wait_ge(readA, b * 3 + 1)
                for f in range(CB):
                    for k in range(CB):
                        m = pe.matmul(psum[1][:, f * LC:(f + 1) * LC], Wkv[:, k, f * P:(f + 1) * P], ctxT[:, k, :],
                                      start=(k == 0), stop=(k == CB - 1))
                m.then_inc(fullA, 1)
                for k in range(CB):
                    m = pe.matmul(psum[2][0:LC, 0:C], ctxT[:, k, :], Wkv[:, k, C:2 * C], start=(k == 0), stop=(k == CB - 1))
                m.then_inc(fullA, 1)
                pe.wait_ge(readA, b * 3 + 3)
                pe.wait_ge(gatedA, b * 4 + 4)
                pe.wait_ge(doneA, b + 1)

            def prep_b(b):
                if not isinstance(b, int):
                    for i in (5, 6, 7):
                        pe.wait_ge(drained[i], b * (UNITS * len(BANK_JOBS[i])) + 1)
                for h in range(CB):
                    for k in range(CB):
                        m = pe.matmul(psum[5][:, h * LC:(h + 1) * LC], Wv1[:, k, h * P:(h + 1) * P], ctxT[:, k, :],
                                      start=(k == 0), stop=(k == CB - 1))
                m.then_inc(fullB, 1)
                for c in range(CB):
                    for k in range(CB):
                        m = pe.matmul(psum[6][:, c * LC:(c + 1) * LC], MT[:, k, c * P:(c + 1) * P], ctxT[:, k, :],
                                      start=(k == 0), stop=(k == CB - 1))
                m.then_inc(fullB, 1)
                pe.wait_ge(readB, b * 6 + 1)
                for n in range(4):
                    bk = psum[(7, 5, 6, 7)[n]]
                    if n:
                        pe.wait_ge(readB, b * 6 + n)
                    c0, c1 = n * 512, min((n + 1) * 512, W1N)
                    for h in range(CB):
                        m = pe.matmul(bk[0:LC, 0:c1 - c0], vT1[:, h, :], W1ev[:, h, c0:c1], start=(h == 0), stop=(h == CB - 1))
                    if n == 3:
                        for h in range(CB):
                            m = pe.matmul(bk[0:LC, c1 - c0:c1 - c0 + E], vT1[:, h, :], Rw[:, CB + h, :],
                                          start=(h == 0), stop=(h == CB - 1))
                    m.then_inc(fullB, 1)
                pe.wait_ge(readB, b * 6 + 6)
                pe.wait_ge(gatedB, b * HJ + HJ)
                pe.wait_ge(doneB, b + 1)
                alone(pe)

            def turn(name, src, u, sem_, per):
                wait_free(pe, name, u)
                pe.wait_ge(sem_, u * per + per)
                bk = bank_of(name)
                for f in range(CB):
                    for t in range(TILES):
                        m = pe.transpose(bk[:, f * UT + t * P:f * UT + (t + 1) * P], src[:, t, f * P:(f + 1) * P], ident[:, :])
                m.then_inc(full[JOB[name][0]], 1)

            def feature_major(name, w, c0, src, u):
                wait_free(pe, name, u)
                bk = bank_of(name)
                for f in range(CB):
                    for k in range(CB):
                        m = pe.matmul(bk[:, f * UT:(f + 1) * UT], w[:, k, c0 + f * P:c0 + (f + 1) * P], src[:, k, :],
                                      start=(k == 0), stop=(k == CB - 1))
                m.then_inc(full[JOB[name][0]], 1)

            def bias_first(name, which):
                pe.matmul(bank_of(name)[:, :], ones3[:, :], bias3[which][:, :, :].rearrange("p t c -> p (t c)"),
                          start=True, stop=False, skip_group_check=True)

            def token_major(name, src, w, nk, last=True):
                bk = bank_of(name)
                for k in range(nk):
                    for t in range(TILES):
                        m = pe.matmul(bk[:, t * C:(t + 1) * C], src[:, k, t * P:(t + 1) * P], w[:, k, :],
                                      start=False, stop=(k == nk - 1), skip_group_check=True)
                m.then_inc(full[JOB[name][0]], 1)

            def a_qkv(u):
                turn("ln1", xnA, u, normed[0], TILES)
                wait_drained(pe, "ln1", u)
                feature_major("q", Wqkv, 0, hA, u)
                feature_major("k", Wqkv, C, hA, u)
                wait_free(pe, "v", u)
                for t in range(TILES):
                    for k in range(CB):
                        m = pe.matmul(bank_of("v")[:, t * C:(t + 1) * C], hA[:, k, t * P:(t + 1) * P], Wqkv[:, k, 2 * C:3 * C],
                                      start=(k == 0), stop=(k == CB - 1))
                m.then_inc(full[JOB["v"][0]], 1)

            def a_scores(t, u):
                if t == 0:
                    wait_drained(pe, "q", u)
                    pe.wait_ge(keys_masked, u * 2 + 2)
                for s in range(SLOTS):
                    name = f"s{t}{s}"
                    wait_free(pe, name, u)
                    for i in range(HPS):
                        j, e = i // PAR, i % PAR
                        r = slice(32 * s, 32 * s + 32)
                        m = pe.matmul(psum[s][:, i * P:(i + 1) * P], qT[r, j, t * P:(t + 1) * P], km[e][r, j, t * P:(t + 1) * P],
                                      start=True, stop=True)
                    m.then_inc(full[s], 1)

            def a_turn_probs(t, u):
                for s in range(SLOTS):
                    name = f"p{t}{s}"
                    pe.wait_ge(probs, u * (TILES * SLOTS) + (t * SLOTS + s + 1))
                    wait_free(pe, name, u)
                    for i in range(HPS):
                        m = pe.transpose(psum[s][:, i * P:(i + 1) * P], prob[:, s, i, :], ident[:, :])
                    m.then_inc(full[s], 1)

            def a_values(t, u):
                name = f"pv{t}"
                wait_free(pe, name, u)
                if t == 0:
                    wait_drained(pe, "v", u)
                for s in range(SLOTS):
                    wait_drained(pe, f"p{t}{s}", u)
                    for i in range(HPS):
                        h = head(s, i)
                        m = pe.matmul(psum[4][:, h * DV:(h + 1) * DV], probT[:, s, i, :], va[:, t, h, :], start=True, stop=True)
                m.then_inc(full[4], 1)

            def a_project(turn_name, name, which, w, u, pv):
                wait_drained(pe, pv, u)
                wait_free(pe, turn_name, u)
                bk = bank_of(turn_name)
                for f in range(CB):
                    for t in range(TILES):
                        m = pe.transpose(bk[:, f * UT + t * P:f * UT + (t + 1) * P], on[:, t, f * P:(f + 1) * P], ident[:, :])
                m.then_inc(full[JOB[turn_name][0]], 1)
                wait_free(pe, name, u)
                bias_first(name, which)
                wait_drained(pe, turn_name, u)
                token_major(name, oT, w, CB)

            def a_query(u):
                turn("ln2", xnA, u, normed[1], TILES)
                wait_drained(pe, "ln2", u)
                feature_major("q2", Wq2, 0, hA, u)

            def a_cross_scores(t, u):
                if t == 0:
                    wait_drained(pe, "q2", u)
                for s in range(SLOTS):
                    wait_free(pe, f"c{t}{s}", u)
                    for i in range(HPS):
                        j, e = i // PAR, i % PAR
                        r = slice(32 * s, 32 * s + 32)
                        m = pe.matmul(psum[s][:, i * LC:(i + 1) * LC], q2T[r, j, t * P:(t + 1) * P], kc[e][r, j, :],
                                      start=True, stop=True)
                    m.then_inc(full[s], 1)

            def a_turn_picked(t, u):
                pe.wait_ge(picked, u * TILES + (t + 1))
                for s in range(SLOTS):
                    wait_free(pe, f"y{t}{s}", u)
                    for i in range(HPS):
                        m = pe.transpose(psum[s][0:LC, i * P:(i + 1) * P], Dx[:, t, s * HPS + i, :], ident[:, :])
                    m.then_inc(full[s], 1)

            def a_cross_values(t, u):
                wait_free(pe, f"xv{t}", u)
                for s in range(SLOTS):
                    wait_drained(pe, f"y{t}{s}", u)
                    for i in range(HPS):
                        h = head(s, i)
                        m = pe.matmul(psum[4][:, h * DV:(h + 1) * DV], probT[0:LC, s, i, :], vc[:, h, :], start=True, stop=True)
                m.then_inc(full[4], 1)

            def b_hidden(j, u):
                name = f"m{j}"
                if j == 0:
                    wait_drained(pe, "ln3", u)
                wait_free(pe, name, u)
                for half in range(2):
                    for k in range(CB):
                        c = half * HID + j * P
                        m = pe.matmul(bank_of(name)[:, half * UT:(half + 1) * UT], Wm1[:, k, c:c + P], hB[:, k, :],
                                      start=(k == 0), stop=(k == CB - 1))
                m.then_inc(full[JOB[name][0]], 1)

            def b_down(j, u):
                if j == 0:
                    wait_free(pe, "mo", u)
                    bias_first("mo", "mo")
                wait_drained(pe, f"m{j}", u)
                for t in range(TILES):
                    m = pe.matmul(psum[7][:, t * C:(t + 1) * C], gT[:, j, t * P:(t + 1) * P], Wm2_g[:, j, :],
                                  start=False, stop=(j == HJ - 1), skip_group_check=True)
                if j == HJ - 1:
                    m.then_inc(full[7], 1)

            def b_proto_scores(u):
                turn("ln4", xnB, u, normed[3], TILES)
                wait_drained(pe, "ln4", u)
                wait_free(pe, "ps", u)
                for t in range(TILES):
                    for k in range(CB):
                        m = pe.matmul(psum[7][:, t * LC:(t + 1) * LC], nxT[:, k, t * P:(t + 1) * P], Gp[:, k, :],
                                      start=(k == 0), stop=(k == CB - 1))
                m.then_inc(full[7], 1)

            def b_turn_weights(u):
                pe.wait_ge(proto_steps, u * 3 + 3)
                wait_free(pe, "wt", u)
                for t in range(TILES):
                    m = pe.transpose(bank_of("wt")[0:LC, t * P:(t + 1) * P], pw[:, t, :], ident[:, :])
                m.then_inc(full[JOB["wt"][0]], 1)

            def b_router(u):
                wait_drained(pe, "wt", u)
                wait_free(pe, "rt", u)
                for t in range(TILES):
                    o = psum[7][:, t * E:(t + 1) * E]
                    for k in range(CB):
                        pe.matmul(o, nxT[:, k, t * P:(t + 1) * P], Rw[:, k, :], start=(k == 0), stop=False)
                    m = pe.matmul(o, wT[:, t * P:(t + 1) * P], Vp[:, W1N:W1N + E], start=False, stop=True)
                m.then_inc(full[7], 1)

            def b_first(name, c0, u):
                wait_free(pe, name, u)
                for n in range(2):
                    o = bank_of(name)[:, n * UT:(n + 1) * UT]
                    c = slice(c0 + n * P, c0 + (n + 1) * P)
                    for k in range(CB):
                        pe.matmul(o, W1nx[:, k, c], nxT[:, k, :], start=(k == 0), stop=False)
                    m = pe.matmul(o, Vp[:, c], wT[:, :], start=False, stop=True)
                m.then_inc(full[JOB[name][0]], 1)

            def b_second(e, u):
                name = f"e{e}"
                wait_free(pe, name, u)
                bias_first(name, name)
                wait_drained(pe, f"h{e}1", u)
                wait_drained(pe, f"h{e}0", u)
                token_major(name, hE[:, e % 2], W2p[:, e * RB:(e + 1) * RB, :], RB)

            def b_gate(u):
                wait_free(pe, "g2", u)
                bias_first("g2", "g2")
                wait_drained(pe, "hg", u)
                token_major("g2", gs, Wg2, CB)

            def stage_a(u):
                a_qkv(u)
                a_scores(0, u)
                a_turn_probs(0, u)
                a_scores(1, u)
                a_values(0, u)
                a_turn_probs(1, u)
                a_values(1, u)
                a_project("o1", "so", "so", Wso_g, u, "pv1")
                a_query(u)
                a_cross_scores(0, u)
                a_cross_scores(1, u)
                a_turn_picked(0, u)
                a_cross_values(0, u)
                a_turn_picked(1, u)
                a_cross_values(1, u)
                a_project("o2", "co", "co", Wco_g, u, "xv1")

            def both(ua, ub):
                a_qkv(ua)
                turn("ln3", xnB, ub, normed[2], TILES)
                a_scores(0, ua)
                b_hidden(0, ub)
                b_hidden(1, ub)
                b_hidden(2, ub)
                b_down(0, ub)
                a_turn_probs(0, ua)
                b_hidden(3, ub)
                a_scores(1, ua)
                b_down(1, ub)
                b_hidden(4, ub)
                a_values(0, ua)
                b_down(2, ub)
                b_hidden(5, ub)
                b_down(3, ub)
                b_hidden(6, ub)
                a_turn_probs(1, ua)
                b_down(4, ub)
                b_hidden(7, ub)
                b_down(5, ub)
                a_values(1, ua)
                b_down(6, ub)
                b_down(7, ub)
                a_project("o1", "so", "so", Wso_g, ua, "pv1")
                b_proto_scores(ub)
                a_query(ua)
                b_turn_weights(ub)
                a_cross_scores(0, ua)
                b_router(ub)
                b_first("h00", 0, ub)
                a_cross_scores(1, ua)
                b_first("h01", 2 * P, ub)
                b_first("h10", RH, ub)
                b_second(0, ub)
                b_first("h11", RH + 2 * P, ub)
                a_turn_picked(0, ua)
                b_first("h20", 2 * RH, ub)
                b_second(1, ub)
                a_cross_values(0, ua)
                b_first("h21", 2 * RH + 2 * P, ub)
                b_first("hg", 3 * RH, ub)
                a_turn_picked(1, ua)
                b_second(2, ub)
                a_cross_values(1, ua)
                b_gate(ub)
                a_project("o2", "co", "co", Wco_g, ua, "xv1")

            prep_weights()
            prep_a(0, 0)
            stage_a(0)
            with pe.Fori(0, NB) as b:
                prep_b(b)
                with pe.Fori(0, UNITS - 1) as r:
                    u = b * UNITS + r
                    both(u + 1, u)
                prep_a(b + 1, b * UNITS + UNITS)
                both(b * UNITS + UNITS, b * UNITS + (UNITS - 1))

        @block.scalar
        def _(act):
            def copy_job(dst, name, u, view=None):
                wait_full(act, name, u)
                act.activation(dst, bank_of(name)[:, :] if view is None else view, ACT.Copy).then_inc(drained[JOB[name][0]], 1)

            def modulate(dst, name, u, scale, shift):
                wait_full(act, name, u)
                for f in range(CB):
                    i = act.activation(dst[:, f, :], bank_of(name)[:, f * UT:(f + 1) * UT], ACT.Identity,
                                       bias=shift(f), scale=scale(f))
                i.then_inc(drained[JOB[name][0]], 1)

            def add_bias(dst, name, u, c0):
                wait_full(act, name, u)
                for f in range(CB):
                    i = act.activation(dst[:, f, :], bank_of(name)[:, f * UT:(f + 1) * UT], ACT.Identity,
                                       bias=cols[:, c0 + f:c0 + f + 1])
                i.then_inc(drained[JOB[name][0]], 1)

            def a_modulate(name, u, first):
                modulate(hA, name, u, lambda f: modA[:, first + f:first + f + 1], lambda f: modA[:, first + CB + f:first + CB + f + 1])

            def a_qk(u):
                a_modulate("ln1", u, 0)
                add_bias(qT, "q", u, COLS["qkv"])
                add_bias(kT, "k", u, COLS["qkv"] + CB)

            def a_exp(t, u):
                for s in range(SLOTS):
                    wait_drained(act, f"s{t}{s}", u)
                    act.activation(prob[:, s], prob[:, s], ACT.Exp, scale=float(D) ** -0.5).then_inc(probs, 1)

            def a_copy_turned(t, u, kind, np_=P):
                for s in range(SLOTS):
                    name = f"{kind}{t}{s}"
                    wait_full(act, name, u)
                    act.activation(probT[0:np_, s], psum[s][0:np_, :].rearrange("p (i q) -> p i q", i=HPS), ACT.Copy)\
                       .then_inc(drained[s], 1)

            def a_copy_outputs(name, u):
                copy_job(oT[:, :, :].rearrange("p f t -> p (f t)"), name, u)

            def a_copy_scores(t, u):
                if t == 0:
                    act.wait_ge(topk, u * TOPK_PER_UNIT)
                for s in range(SLOTS):
                    wait_full(act, f"c{t}{s}", u)
                    act.activation(S[:, t, s * HPS:(s + 1) * HPS, :], psum[s][:, 0:HPS * LC].rearrange("p (i c) -> p i c", i=HPS),
                                   ACT.Copy).then_inc(drained[s], 1)

            def a_cross_exp(t, u):
                act.wait_ge(shifted, u * (TILES * SLOTS) + (t + 1) * SLOTS)
                act.activation(Dx[:, t], Dx[:, t], ACT.Exp, scale=float(D) ** -0.5).then_inc(cross_exp, 1)

            def b_tanh_mlp(j, u):
                name = f"m{j}"
                if j == 0:
                    act.wait_ge(mixed, u + 1)
                wait_full(act, name, u)
                act.activation(tb[tb_of(name)][:, 0:UT], bank_of(name)[:, 0:UT], ACT.Tanh, bias=b1half[:, j:j + 1], scale=0.5)\
                   .then_inc(tanh_done, 1)

            def b_tanh_first(name, n0, u):
                wait_full(act, name, u)
                for n in range(2):
                    i = act.activation(tb[tb_of(name)][:, n * UT:(n + 1) * UT], bank_of(name)[:, n * UT:(n + 1) * UT], ACT.Tanh,
                                       bias=betaH[:, n0 + n:n0 + n + 1], scale=0.5)
                i.then_inc(tanh_done, 1)

            def b_modulate(u):
                modulate(hB, "ln3", u, lambda f: modB[:, f:f + 1], lambda f: modB[:, CB + f:CB + f + 1])

            def b_affine(u):
                g, c = COLS["gamma"], COLS["beta"]
                modulate(nxT, "ln4", u, lambda f: cols[:, g + f:g + f + 1], lambda f: cols[:, c + f:c + f + 1])

            def b_proto_exp(u):
                wait_drained(act, "ps", u)
                act.activation(pw[:, :, :], pw[:, :, :], ACT.Exp, scale=float(C) ** -0.5).then_inc(proto_exp, 1)

            def b_copy_weights(u):
                wait_full(act, "wt", u)
                act.activation(wT[:, :], bank_of("wt")[0:LC, 0:UT], ACT.Copy).then_inc(drained[JOB["wt"][0]], 1)

            def b_route_exp(u):
                act.wait_ge(route_steps, u * 5 + 2)
                act.activation(rl[:, :, :], rl[:, :, :], ACT.Exp).then_inc(route_exp, 1)

            def b_gate_tanh(u):
                wait_full(act, "g2", u)
                act.activation(tg[:, :], psum[7][:, :], ACT.Tanh, scale=0.5).then_inc(drained[7], 1)

            def stage_a(u):
                a_qk(u)
                a_exp(0, u)
                a_copy_turned(0, u, "p")
                a_exp(1, u)
                a_copy_turned(1, u, "p")
                a_copy_outputs("o1", u)
                a_modulate("ln2", u, 2 * CB)
                add_bias(q2T, "q2", u, COLS["q"])
                a_copy_scores(0, u)
                a_copy_scores(1, u)
                a_cross_exp(0, u)
                a_copy_turned(0, u, "y", LC)
                a_cross_exp(1, u)
                a_copy_turned(1, u, "y", LC)
                a_copy_outputs("o2", u)

            def both(ua, ub):
                a_qk(ua)
                b_modulate(ub)
                a_exp(0, ua)
                b_tanh_mlp(0, ub)
                b_tanh_mlp(1, ub)
                b_tanh_mlp(2, ub)
                a_copy_turned(0, ua, "p")
                b_tanh_mlp(3, ub)
                a_exp(1, ua)
                b_tanh_mlp(4, ub)
                b_tanh_mlp(5, ub)
                b_tanh_mlp(6, ub)
                a_copy_turned(1, ua, "p")
                b_tanh_mlp(7, ub)
                a_copy_outputs("o1", ua)
                b_affine(ub)
                a_modulate("ln2", ua, 2 * CB)
                b_proto_exp(ub)
                add_bias(q2T, "q2", ua, COLS["q"])
                b_copy_weights(ub)
                a_copy_scores(0, ua)
                b_route_exp(ub)
                b_tanh_first("h00", 0, ub)
                a_copy_scores(1, ua)
                b_tanh_first("h01", 2, ub)
                b_tanh_first("h10", 4, ub)
                b_tanh_first("h11", 6, ub)
                a_cross_exp(0, ua)
                a_copy_turned(0, ua, "y", LC)
                b_tanh_first("h20", 8, ub)
                b_tanh_first("h21", 10, ub)
                b_tanh_first("hg", 12, ub)
                a_cross_exp(1, ua)
                a_copy_turned(1, ua, "y", LC)
                b_gate_tanh(ub)
                a_copy_outputs("o2", ua)

            act.wait_ge(init_read, 1)
            act.activation(tanhT[:, :, :], cols[:, COLS["cond"]:COLS["cond"] + NB * CB].rearrange("p (b k) -> p b k", k=CB),
                           ACT.Tanh, scale=0.5).then_inc(init_tanh, 1)
            act.wait_ge(dve_step, STEP_END)
            act.wait_ge(doneA, 1)
            stage_a(0)
            with act.Fori(0, NB) as b:
                act.wait_ge(doneB, b + 1)
                with act.Fori(0, UNITS - 1) as r:
                    u = b * UNITS + r
                    both(u + 1, u)
                act.wait_ge(doneA, b + 2)
                both(b * UNITS + UNITS, b * UNITS + (UNITS - 1))

        @block.gpsimd
        def _(pool):
            def rstd_of(i, eps, u):
                pool.wait_ge(stats[i], u * 4 + 4)
                alone(pool)
                pool.tensor_scalar(vare[i][:, :], mv[i][:, :, 1], eps, None, ALU.add).then_inc(rstds[i], 1)
                pool.wait_ge(rstds[i], u * 2 + 1)
                pool.tensor_tensor(rstd[i][:, :], vare[i][:, :], neghalf[:, :], ALU.pow).then_inc(rstds[i], 1)

            def a_mask_keys(u):
                wait_drained(pool, "k", u)
                alone(pool)
                for e, m in enumerate((maskE, maskO)):
                    pool.tensor_scalar(km[e][:, :, :], kT[:, :, :], m[:, 0:1], None, ALU.mult).then_inc(keys_masked, 1)

            def a_shift(t, s, u):
                pool.wait_ge(topk, u * TOPK_PER_UNIT + (topk_base(t, s) + HPS))
                g = slice(s * HPS, (s + 1) * HPS)
                pool.tensor_tensor(Dx[:, t, g, :], S[:, t, g, :], M1[:, t, g, 0:1].to_broadcast([P, HPS, LC]), ALU.subtract)\
                    .then_inc(shifted, 1)

            def b_plus_one(name, u):
                n = TANH_ORDER.index(name)
                pool.wait_ge(tanh_done, u * len(TANH_ORDER) + (n + 1))
                alone(pool)
                t = tb[tb_of(name)][:, 0:UT] if name[0] == "m" else tb[tb_of(name)][:, :]
                pool.tensor_scalar(t, t, 1.0, None, ALU.add).then_inc(plus_one, 1)

            def gate_a(b):
                for n, (dst, w) in enumerate(((Wso_g, Wso), (Wco_g, Wco))):
                    for k in range(CB):
                        pool.tensor_tensor(dst[:, k, :], w[:, k, :], Gall[:, bass.ds((b & 3) * 3 + n, 1), :]
                                           .rearrange("p a c -> p (a c)"), ALU.mult).then_inc(gatedA, 1)

            def gate_b(b):
                pool.wait_ge(wm2_loaded, b * 16 + 16)
                for k in range(HJ):
                    pool.tensor_tensor(Wm2_g[:, k, :], Wm2_g[:, k, :], Gall[:, bass.ds((b & 3) * 3 + 2, 1), :]
                                       .rearrange("p a c -> p (a c)"), ALU.mult).then_inc(gatedB, 1)

            def stage_a(u):
                rstd_of(0, EPS0, u)
                a_mask_keys(u)
                rstd_of(1, EPS0, u)
                for t in range(TILES):
                    for s in range(SLOTS):
                        a_shift(t, s, u)

            def both(ua, ub):
                rstd_of(0, EPS0, ua)
                rstd_of(2, EPS0, ub)
                a_mask_keys(ua)
                for j in range(HJ):
                    b_plus_one(f"m{j}", ub)
                rstd_of(3, EPS1, ub)
                rstd_of(1, EPS0, ua)
                for s in range(SLOTS):
                    a_shift(0, s, ua)
                    if s == 1:
                        b_plus_one("h00", ub)
                    if s == 2:
                        b_plus_one("h01", ub)
                b_plus_one("h10", ub)
                a_shift(1, 0, ua)
                b_plus_one("h11", ub)
                a_shift(1, 1, ua)
                b_plus_one("h20", ub)
                a_shift(1, 2, ua)
                b_plus_one("h21", ub)
                a_shift(1, 3, ua)
                b_plus_one("hg", ub)

            pool.memset(ident[:, :], 0.0).then_inc(consts, 1)
            pool.memset(maskE[:, :], 0.0).then_inc(consts, 1)
            pool.memset(maskO[:, :], 0.0).then_inc(consts, 1)
            pool.memset(neghalf[:, :], -0.5).then_inc(consts, 1)
            pool.memset(onesf[:, :], 1.0).then_inc(consts, 1)
            pool.memset(ones3[:, :], 1.0).then_inc(consts, 1)
            pool.memset(va[:, :, :, :], 1.0).then_inc(consts, 1)
            pool.memset(vc[:, :, :], 1.0).then_inc(consts, 1)
            for n in bias3:
                pool.memset(bias3[n][:, :, :], 0.0).then_inc(consts, 1)
            pool.wait_ge(consts, 8 + len(bias3))
            pool.affine_select(out=ident[:, :], in_=ident[:, :], compare_op=ALU.not_equal, fill=1.0, base=0,
                               pattern=[[-1, P]], channel_multiplier=1).then_inc(consts, 1)
            pool.wait_ge(consts, 9 + len(bias3))
            pool.wait_ge(dve_step, STEP_END)
            gate_a(0)
            stage_a(0)
            with pool.Fori(0, NB) as b:
                gate_b(b)
                with pool.Fori(0, UNITS - 1) as r:
                    u = b * UNITS + r
                    both(u + 1, u)
                bank, i, n = JOB["co"]
                pool.wait_ge(full[bank], b * (UNITS * n) + UNITS * n)
                gate_a(b + 1)
                both(b * UNITS + UNITS, b * UNITS + (UNITS - 1))

        @block.vector
        def _(dve):
            step = [0]

            def chain(i, s=None):
                step[0] += 1
                i.then_inc(dve_step, 1)
                dve.wait_ge(dve_step, step[0])

            init = [0]

            def read_job(*ops):
                k = init[0]
                init[0] += 1
                dve.wait_ge(init_full, k + 1)
                for o in ops[:-1]:
                    o(psum[k % 8])
                ops[-1](psum[k % 8]).then_inc(init_read, 1)

            def three_parts(src, dst, sem_, base):
                n = [0]

                def go(i):
                    n[0] += 1
                    i.then_inc(sem_, 1)
                    dve.wait_ge(sem_, base + n[0])

                def spread(part):
                    return split_b[0:1, :].rearrange("p (a c) -> p a c", a=1).to_broadcast([1, TILES, C])

                cur = src
                for p in range(3):
                    go(dve.tensor_copy(split_b[0:1, :], cur))
                    go(dve.tensor_copy(dst[32 * p:32 * p + 1, :, :], spread(p)))
                    if p < 2:
                        nxt = split[0:1, p, :]
                        go(dve.tensor_tensor(nxt, cur, split_b[0:1, :], ALU.subtract))
                        cur = nxt
                return n[0]

            def prep_weights():
                dve.wait_ge(consts, 9 + len(bias3))
                for m, o in ((maskE, 0), (maskO, D)):
                    cv = ident[:, :].rearrange("p (s d) -> p s d", d=32)[:, :, o:o + D]
                    i = dve.tensor_reduce(m[:, :], cv, AX.XY, ALU.add)
                    chain(i)
                read_job(lambda bk: dve.tensor_copy(cols[:, :], bk[:, 0:NCOL]))
                dve.wait_ge(init_tanh, 1)
                dve.wait_ge(init_read, 1)
                condT = cols[:, COLS["cond"]:COLS["cond"] + NB * CB].rearrange("p (b k) -> p b k", k=CB)
                chain(dve.scalar_tensor_tensor(siluT[:, :, :], tanhT[:, :, :], 1.0, condT, ALU.add, ALU.mult))
                chain(dve.tensor_scalar(siluT[:, :, :], siluT[:, :, :], 0.5, None, ALU.mult))
                assert step[0] == STEP_SILU
                ada = cols[:, COLS["ada"]:COLS["ada"] + 9 * CB]

                def read_mods(bk):
                    v = bk[:, 0:12 * NB].rearrange("p (n b) -> p b n", b=NB)
                    for n, (sec, one) in enumerate(((1, 1.0), (0, 0.0), (4, 1.0), (3, 0.0), (7, 1.0), (6, 0.0))):
                        for f in range(CB):
                            i = dve.tensor_scalar(mods[:, :, n * CB + f], v[:, :, n * CB + f],
                                                  ada[:, sec * CB + f:sec * CB + f + 1], one, ALU.add, ALU.add)
                    return i

                read_job(read_mods)

                def spread_cols(src, b):
                    if b > 0:
                        dve.wait_ge(init_read, init[0])
                    for k in range(CB):
                        chain(dve.tensor_copy(modBc[:, k, 0:P], src[:, b, k:k + 1].to_broadcast([P, P])))

                for b in range(NB):
                    spread_cols(siluT, b)
                    for g in range(3):
                        read_job(lambda bk, b=b, g=g: dve.tensor_scalar(Gall[:, b * 3 + g, :], bk[:, 0:C], 0.5 if g == 2 else 1.0, None, ALU.mult))
                assert init[0] == INIT_ADA_READ
                for n in ("so", "co"):
                    read_job(lambda bk, n=n: dve.tensor_tensor(row(n), row(n), bk[0:1, 0:C], ALU.add))
                for e in range(E):
                    read_job(lambda bk, e=e: dve.tensor_tensor(row(f"e{e}"), bk[0:1, 0:C], row("out"), ALU.add))
                for b in range(NB):
                    spread_cols(condT, b)
                    read_job(lambda bk, b=b: dve.tensor_copy(rbias_all[:, b, :], bk[:, 0:E]))
                assert init[0] == INIT_TURNS
                for w in (wkT, wqT):
                    read_job(lambda bk, w=w: dve.tensor_copy(w[:, :, :].rearrange("p h c -> p (h c)"), bk[:, :]))
                read_job(lambda bk: dve.tensor_copy(MT[:, :, :].rearrange("p h c -> p (h c)"), bk[:, :]))
                def read_betas(bk):
                    v = bk[:, 0:W1B * NB].rearrange("p (n b) -> p b n", b=NB)
                    b1 = cols[:, COLS["e_b1"]:COLS["e_b1"] + W1B]
                    for b in range(NB):
                        i = dve.tensor_tensor(betas[:, b, :], v[:, b, :], b1, ALU.add)
                    return i

                read_job(read_betas)
                for e in range(E):
                    for h in range(CB):
                        read_job(lambda bk, h=h: dve.tensor_copy(e2Tv[:, h, :], bk[:, :]))
                    if e == 1:
                        assert init[0] == INIT_E2_READ
                    for k2 in range(RB // 2):
                        read_job(lambda bk, e=e, k2=k2: dve.tensor_scalar(
                            W2p[:, e * RB + 2 * k2:e * RB + 2 * k2 + 2, :].rearrange("p k c -> p (k c)"), bk[:, :], 0.25, None, ALU.mult))

                dve.wait_ge(init_read, init[0])
                chain(dve.tensor_scalar(Wg2[:, :, :], Wg2[:, :, :], 0.5, None, ALU.mult))
                chain(dve.tensor_scalar(row("m2"), row("m2"), 2.0, None, ALU.mult))
                chain(dve.tensor_scalar(b1half[:, :], cols[:, COLS["m1"]:COLS["m1"] + HJ], 0.5, None, ALU.mult))
                for e in range(E):
                    chain(dve.tensor_scalar(row(f"e{e}"), row(f"e{e}"), 0.5, None, ALU.mult))
                for n, r in (("e0", "e0"), ("e1", "e1"), ("e2", "e2"), ("g2", "g2")):
                    step[0] += three_parts(row(r), bias3[n], dve_step, step[0])
                assert step[0] == STEP_END, step[0]

            def prep_a(b):
                bb = b & 3
                n = [0]

                def go(i):
                    n[0] += 1
                    i.then_inc(stepA, 1)
                    dve.wait_ge(stepA, b * STEPS_A + n[0])

                go(dve.tensor_copy(modA[:, :], mods[:, bass.ds(bb, 1), 0:8].rearrange("p a n -> p (a n)")))
                for name, g in (("so", 0), ("co", 1)):
                    go(dve.tensor_tensor(row("tmp"), row(name), Gall[0:1, bass.ds(bb * 3 + g, 1), :].rearrange("p a c -> p (a c)"), ALU.mult))
                    n[0] += three_parts(row("tmp"), bias3[name], stepA, b * STEPS_A + n[0])
                assert n[0] == STEPS_A, n[0]
                dve.wait_ge(fullA, b * 3 + 1)
                dve.tensor_copy(ctxT[:, :, :].rearrange("p k c -> p (k c)"), psum[0][:, 0:CB * LC]).then_inc(readA, 1)
                dve.wait_ge(fullA, b * 3 + 2)
                for f in range(CB):
                    for e, m in enumerate((maskE, maskO)):
                        c = COLS["kv"] + f
                        i = dve.tensor_scalar(kc[e][:, f, :], psum[1][:, f * LC:(f + 1) * LC], cols[:, c:c + 1], m[:, 0:1],
                                              ALU.add, ALU.mult)
                i.then_inc(readA, 1)
                dve.wait_ge(fullA, b * 3 + 3)
                dve.tensor_copy(vc[:, :, 0:D], psum[2][0:LC, 0:C].rearrange("p (h d) -> p h d", h=H)).then_inc(readA, 1)
                dve.tensor_copy(M2[:, 0, 0:1], modA[:, 0:1]).then_inc(doneA, 1)

            def prep_b(b):
                n = [0]

                def go(i):
                    n[0] += 1
                    i.then_inc(stepB, 1)
                    dve.wait_ge(stepB, b * STEPS_B + n[0])

                go(dve.tensor_copy(modB[:, :], mods[:, bass.ds(b, 1), 8:12].rearrange("p a n -> p (a n)")))
                go(dve.tensor_copy(betaF[:, :], betas[:, bass.ds(b, 1), :].rearrange("p a n -> p (a n)")))
                go(dve.tensor_scalar(betaH[:, :], betaF[:, :], 0.5, None, ALU.mult))
                go(dve.tensor_copy(rbias[:, :], rbias_all[:, bass.ds(b, 1), :].rearrange("p a n -> p (a n)")))
                go(dve.tensor_tensor(row("tmp"), row("m2"), Gall[0:1, bass.ds(b * 3 + 2, 1), :].rearrange("p a c -> p (a c)"), ALU.mult))
                n[0] += three_parts(row("tmp"), bias3["mo"], stepB, b * STEPS_B + n[0])
                assert n[0] == STEPS_B, n[0]
                dve.wait_ge(fullB, b * 6 + 1)
                dve.tensor_copy(vT1[:, :, :].rearrange("p k c -> p (k c)"), psum[5][:, 0:CB * LC]).then_inc(readB, 1)
                dve.wait_ge(fullB, b * 6 + 2)
                dve.tensor_copy(Gp[:, :, :].rearrange("p k c -> p (k c)"), psum[6][:, 0:CB * LC]).then_inc(readB, 1)
                for k in range(4):
                    dve.wait_ge(fullB, b * 6 + 3 + k)
                    c0, c1 = k * 512, min((k + 1) * 512, W1N + E)
                    dve.tensor_copy(Vp[:, c0:c1], psum[(7, 5, 6, 7)[k]][0:LC, 0:c1 - c0]).then_inc(readB, 1)
                dve.tensor_copy(M2[:, 1, 0:1], modB[:, 0:1]).then_inc(doneB, 1)

            def ln_stats(i, src, u):
                for t in range(TILES):
                    dve.bn_stats(stat[i][:, t, :], src[:, t, :]).then_inc(stats[i], 1)
                dve.wait_ge(stats[i], u * 4 + 2)
                alone(dve)
                for t in range(TILES):
                    dve.bn_aggr(mv[i][:, t, :], stat[i][:, t, :]).then_inc(stats[i], 1)

            def ln_apply(i, src, dst, u):
                dve.wait_ge(rstds[i], u * 2 + 2)
                dve.wait_ge(stats[i], u * 4 + 4)
                for t in range(TILES):
                    dve.tensor_scalar(dst[:, t, :], src[:, t, :], mv[i][:, t, 0:1], rstd[i][:, t:t + 1], ALU.subtract, ALU.mult)\
                       .then_inc(normed[i], 1)

            def a_copy_values(u):
                wait_full(dve, "v", u)
                dve.tensor_copy(va[:, :, :, 0:D], bank_of("v")[:, :].rearrange("p (t h d) -> p t h d", t=TILES, h=H))\
                   .then_inc(drained[JOB["v"][0]], 1)

            def a_softmax(t, u):
                def bankv(s):
                    return psum[s][:, :].rearrange("p (i k) -> p i k", i=HPS)

                def sub(s):
                    dve.wait_ge(row_max, u * (TILES * SLOTS) + (t * SLOTS + s + 1))
                    dve.tensor_tensor(prob[:, s], bankv(s), rmax[:, t, s * HPS:(s + 1) * HPS].rearrange("p (i a) -> p i a", a=1)
                                      .to_broadcast([P, HPS, P]), ALU.subtract).then_inc(drained[s], 1)

                for s in range(SLOTS):
                    wait_full(dve, f"s{t}{s}", u)
                    dve.tensor_reduce(rmax[:, t, s * HPS:(s + 1) * HPS], bankv(s), AX.X, ALU.max).then_inc(row_max, 1)
                    if s:
                        sub(s - 1)
                sub(SLOTS - 1)

            def a_normalise(n, name, t, u):
                wait_full(dve, name, u)
                v = psum[4][:, 0:H * DV].rearrange("p (h d) -> p h d", h=H)
                dve.reciprocal(rsum[:, t, :], v[:, :, D]).then_inc(sums_inverted, 1)
                dve.wait_ge(sums_inverted, u * 4 + n + 1)
                dve.tensor_tensor(on[:, t, :].rearrange("p (h d) -> p h d", h=H), v[:, :, 0:D],
                                  rsum[:, t, :].rearrange("p (h a) -> p h a", a=1).to_broadcast([P, H, D]), ALU.mult)\
                   .then_inc(drained[4], 1)

            def a_residual(dst, src, name, u):
                wait_full(dve, name, u)
                dve.tensor_tensor(dst[:, :, :].rearrange("p t c -> p (t c)"), src[:, :, :].rearrange("p t c -> p (t c)"),
                                  bank_of(name)[:, :], ALU.add).then_inc(drained[JOB[name][0]], 1)

            def a_topk(t, s, u):
                wait_drained(dve, f"c{t}{s}", u)
                base = u * TOPK_PER_UNIT + topk_base(t, s)
                alone(dve)

                def phase(n, one):
                    for i in range(HPS):
                        if n and i % 2 == 0:
                            dve.wait_ge(topk, base + ((n - 1) * HPS + i + 2))
                            alone(dve)
                        one(s * HPS + i).then_inc(topk, 1)

                phase(0, lambda h: dve.max(M1[:, t, h, :], S[:, t, h, :]))
                phase(1, lambda h: dve.match_replace(K[:, h, :], M1[:, t, h, :], S[:, t, h, :], KNOCKED))
                phase(2, lambda h: dve.max(M2[:, h, :], K[:, h, :]))
                phase(3, lambda h: dve.match_replace(K[:, h, :], M2[:, h, :], K[:, h, :], KNOCKED))

            def a_pick(t, u):
                dve.wait_ge(cross_exp, u * TILES + (t + 1))
                dve.wait_ge(topk, u * TOPK_PER_UNIT + topk_base(t, SLOTS - 1) + 4 * HPS)
                dve.scalar_tensor_tensor(Dx[:, t].rearrange("p h c -> p (h c)"), K[:, :, :].rearrange("p h c -> p (h c)"), KNOCKED_BELOW,
                                         Dx[:, t].rearrange("p h c -> p (h c)"), ALU.is_lt, ALU.mult).then_inc(picked, 1)

            def b_swiglu(j, u):
                name = f"m{j}"
                w = tb_of(name)
                dve.wait_ge(plus_one, u * len(TANH_ORDER) + (TANH_ORDER.index(name) + 1))
                dve.scalar_tensor_tensor(tb[w][:, 0:UT], bank_of(name)[:, 0:UT], cols[:, COLS["m1"] + j:COLS["m1"] + j + 1],
                                         tb[w][:, 0:UT], ALU.add, ALU.mult).then_inc(half_gated, 1)
                dve.wait_ge(half_gated, u * HJ + (j + 1))
                c = COLS["m1"] + HJ + j
                dve.scalar_tensor_tensor(gT[:, j, :], bank_of(name)[:, UT:2 * UT], cols[:, c:c + 1], tb[w][:, 0:UT], ALU.add, ALU.mult)\
                   .then_inc(drained[JOB[name][0]], 1)

            def b_silu(name, dst, d0, n0, u):
                dve.wait_ge(plus_one, u * len(TANH_ORDER) + (TANH_ORDER.index(name) + 1))
                for n in range(2):
                    i = dve.scalar_tensor_tensor(dst[:, d0 + n, :], bank_of(name)[:, n * UT:(n + 1) * UT], betaF[:, n0 + n:n0 + n + 1],
                                                 tb[tb_of(name)][:, n * UT:(n + 1) * UT], ALU.add, ALU.mult)
                i.then_inc(drained[JOB[name][0]], 1)

            def b_proto_shift(u):
                wait_full(dve, "ps", u)
                v = psum[7][:, 0:TILES * LC].rearrange("p (t c) -> p t c", t=TILES)
                dve.tensor_reduce(pm[:, :], v, AX.X, ALU.max).then_inc(proto_max, 1)
                dve.wait_ge(proto_max, u + 1)
                dve.tensor_tensor(pw[:, :, :], v, pm[:, :].rearrange("p (t a) -> p t a", a=1).to_broadcast([P, TILES, LC]),
                                  ALU.subtract).then_inc(drained[7], 1)

            def b_proto_norm(u):
                dve.wait_ge(proto_exp, u + 1)
                dve.tensor_reduce(psu[:, :], pw[:, :, :], AX.X, ALU.add).then_inc(proto_steps, 1)
                dve.wait_ge(proto_steps, u * 3 + 1)
                dve.reciprocal(psu[:, :], psu[:, :]).then_inc(proto_steps, 1)
                dve.wait_ge(proto_steps, u * 3 + 2)
                dve.tensor_tensor(pw[:, :, :], pw[:, :, :], psu[:, :].rearrange("p (t a) -> p t a", a=1).to_broadcast([P, TILES, LC]),
                                  ALU.mult).then_inc(proto_steps, 1)

            def b_route_shift(u):
                wait_full(dve, "rt", u)
                v = psum[7][:, 0:TILES * E].rearrange("p (t c) -> p t c", t=TILES)
                dve.tensor_tensor(rl[:, :, :], v, rbias[:, :].rearrange("p (a e) -> p a e", a=1).to_broadcast([P, TILES, E]), ALU.add)\
                   .then_inc(drained[7], 1)
                wait_drained(dve, "rt", u)
                dve.tensor_reduce(rm[:, :], rl[:, :, :], AX.X, ALU.max).then_inc(route_steps, 1)
                dve.wait_ge(route_steps, u * 5 + 1)
                dve.tensor_tensor(rl[:, :, :], rl[:, :, :], rm[:, :].rearrange("p (t a) -> p t a", a=1).to_broadcast([P, TILES, E]),
                                  ALU.subtract).then_inc(route_steps, 1)

            def b_route_norm(u):
                dve.wait_ge(route_exp, u + 1)
                dve.tensor_reduce(rs[:, :], rl[:, :, :], AX.X, ALU.add).then_inc(route_steps, 1)
                dve.wait_ge(route_steps, u * 5 + 3)
                dve.reciprocal(rs[:, :], rs[:, :]).then_inc(route_steps, 1)
                dve.wait_ge(route_steps, u * 5 + 4)
                dve.tensor_tensor(rp[:, :, :], rl[:, :, :], rs[:, :].rearrange("p (t a) -> p t a", a=1).to_broadcast([P, TILES, E]),
                                  ALU.mult).then_inc(route_steps, 1)

            def b_mix(e, u):
                wait_full(dve, f"e{e}", u)
                if e == 0:
                    dve.wait_ge(route_steps, u * 5 + 5)
                    dve.wait_ge(y_stored, u * 48 + 16)
                else:
                    wait_drained(dve, f"e{e - 1}", u)
                for t in range(TILES):
                    o, v = acc[:, t, :], psum[7][:, t * C:(t + 1) * C]
                    if e == 0:
                        i = dve.tensor_scalar(o, v, rp[:, t, 0:1], None, ALU.mult)
                    else:
                        i = dve.scalar_tensor_tensor(o, v, rp[:, t, e:e + 1], o, ALU.mult, ALU.add)
                i.then_inc(drained[7], 1)

            def b_finish(u):
                wait_drained(dve, "g2", u)
                flat = lambda a: a[:, :, :].rearrange("p t c -> p (t c)")
                dve.scalar_tensor_tensor(flat(acc), tg[:, :], 1.0, flat(acc), ALU.add, ALU.mult).then_inc(mixed, 1)
                dve.wait_ge(mixed, u + 2)
                dve.tensor_tensor(flat(acc), flat(x2), flat(acc), ALU.add).then_inc(y_ready, 1)

            def a_load(u):
                dve.wait_ge(x_loaded, u * 48 + 48)

            def stage_a(u):
                a_load(u)
                ln_stats(0, xin, u)
                ln_apply(0, xin, xnA, u)
                a_copy_values(u)
                a_softmax(0, u)
                a_softmax(1, u)
                a_normalise(0, "pv0", 0, u)
                a_normalise(1, "pv1", 1, u)
                a_residual(x1, xin, "so", u)
                wait_drained(dve, "so", u)
                ln_stats(1, x1, u)
                ln_apply(1, x1, xnA, u)
                for t in range(TILES):
                    for s in range(SLOTS):
                        a_topk(t, s, u)
                    a_pick(t, u)
                a_normalise(2, "xv0", 0, u)
                a_normalise(3, "xv1", 1, u)
                a_residual(x2, x1, "co", u)
                wait_drained(dve, "co", u)

            def both(ua, ub):
                a_load(ua)
                ln_stats(0, xin, ua)
                ln_stats(2, x2, ub)
                ln_apply(0, xin, xnA, ua)
                ln_apply(2, x2, xnB, ub)
                a_copy_values(ua)
                a_softmax(0, ua)
                b_swiglu(0, ub)
                b_swiglu(1, ub)
                b_swiglu(2, ub)
                b_swiglu(3, ub)
                a_softmax(1, ua)
                b_swiglu(4, ub)
                a_normalise(0, "pv0", 0, ua)
                b_swiglu(5, ub)
                b_swiglu(6, ub)
                b_swiglu(7, ub)
                a_normalise(1, "pv1", 1, ua)
                a_residual(x2, x2, "mo", ub)
                wait_drained(dve, "mo", ub)
                ln_stats(3, x2, ub)
                a_residual(x1, xin, "so", ua)
                ln_apply(3, x2, xnB, ub)
                wait_drained(dve, "so", ua)
                ln_stats(1, x1, ua)
                ln_apply(1, x1, xnA, ua)
                b_proto_shift(ub)
                b_proto_norm(ub)
                a_topk(0, 0, ua)
                b_route_shift(ub)
                a_topk(0, 1, ua)
                b_route_norm(ub)
                b_silu("h00", hE[:, 0], 0, 0, ub)
                a_topk(0, 2, ua)
                b_silu("h01", hE[:, 0], 2, 2, ub)
                a_topk(0, 3, ua)
                b_silu("h10", hE[:, 1], 0, 4, ub)
                b_mix(0, ub)
                a_pick(0, ua)
                a_topk(1, 0, ua)
                b_silu("h11", hE[:, 1], 2, 6, ub)
                a_topk(1, 1, ua)
                b_silu("h20", hE[:, 0], 0, 8, ub)
                b_mix(1, ub)
                a_topk(1, 2, ua)
                a_normalise(2, "xv0", 0, ua)
                b_silu("h21", hE[:, 0], 2, 10, ub)
                a_topk(1, 3, ua)
                b_silu("hg", gs, 0, 12, ub)
                a_pick(1, ua)
                b_mix(2, ub)
                a_normalise(3, "xv1", 1, ua)
                b_finish(ub)
                dve.wait_ge(y_ready, ub + 1)
                a_residual(x2, x1, "co", ua)
                wait_drained(dve, "co", ua)

            prep_weights()
            prep_a(0)
            stage_a(0)
            with dve.Fori(0, NB) as b:
                prep_b(b)
                with dve.Fori(0, UNITS - 1) as r:
                    u = b * UNITS + r
                    both(u + 1, u)
                prep_a(b + 1)
                both(b * UNITS + UNITS, b * UNITS + (UNITS - 1))



_INS = ["x", "cond_1024", "ctx_1024"] + \
       ["L0_xcond_" + n for n in ("w_ada", "b_ada", "w_qkv", "b_qkv", "w_so", "b_so", "w_q", "b_q", "w_kv", "b_kv", "w_co", "b_co",
                                  "w_m1", "b_m1", "w_m2", "b_m2")] + \
       ["L1_xcond_" + n for n in ("ln_gamma", "ln_beta", "Wq", "Wk", "Wv", "router_W", "router_b", "e_w1", "e_b1", "e_w2", "e_b2",
                                  "gate_w1", "gate_b1", "gate_w2", "gate_b2", "out_w", "out_b")]
_OUT = (NB, L, C)


def kernel(**inputs):
    import numpy as _np
    import concourse.bacc as _bacc
    from concourse import mybir as _mybir
    from concourse.bass_utils import run_bass_kernel_spmd as _run

    nc = _bacc.Bacc("TRN2", target_bir_lowering=False, num_devices=1)
    arrays, args = {}, []
    for name in _INS:
        a = _np.ascontiguousarray(inputs[name])
        arrays[f"in_{name}_dram"] = a
        args.append(nc.dram_tensor(f"in_{name}_dram", a.shape, _mybir.dt.from_np(a.dtype), kind="ExternalInput").ap())
    args.append(nc.dram_tensor("out_dram", _OUT, _mybir.dt.float32, kind="ExternalOutput").ap())
    bass_pixart_experts(nc, *args)
    r = _run(nc, [arrays], core_ids=[0])
    return r.results[0]["out_dram"]
```

```python
from contextlib import ExitStack

import concourse.bass as bass
from concourse import mybir

F32 = mybir.dt.float32
BF16 = mybir.dt.bfloat16
ALU = mybir.AluOpType
ACT = mybir.ActivationFunctionType
AX = mybir.AxisListType

P = 128
NB, L, C = 4, 1024, 256
CB = C // P
WIN, SHIFT = 128, 64
TILES = 2
UT = TILES * WIN
UNITS = L // UT
H, D = 16, 16
SLOTS, PAIR, PAR = 4, 2, 2
HPS = PAIR * PAR
LC = 77
DV = D + 1
HID = 1024
HJ = HID // P
E = 3
RH = 2 * C
RB = RH // P
W1N = E * RH + C
W1B = W1N // P
EPS0, EPS1 = 1e-6, 1e-5
KNOCKED = -3.0e38
KNOCKED_BELOW = -2.9e38

_slots = ["s0", "p0", "s1", "p1"]
_cross = ["c0", "c1", "y0", "y1"]
BANK_JOBS = [
    ["q"] + [f"{x}{0}" for x in _slots] + ["o1"] + [f"{x}{0}" for x in _cross] + ["o2"],
    [f"{x}{1}" for x in _slots] + ["so"] + [f"{x}{1}" for x in _cross] + ["co"],
    ["k"] + [f"{x}{2}" for x in _slots] + ["ln2"] + [f"{x}{2}" for x in _cross],
    ["ln1", "v"] + [f"{x}{3}" for x in _slots] + ["q2"] + [f"{x}{3}" for x in _cross],
    ["pv0", "pv1", "xv0", "xv1"],
    ["ln3", "m1", "m3", "m5", "m7", "h01", "h11", "h21"],
    ["m0", "m2", "m4", "m6", "ln4", "h00", "h10", "h20", "hg"],
    ["mo", "ps", "wt", "rt", "e0", "e1", "e2", "g2"],
]
JOB = {name: (bank, i, len(jobs)) for bank, jobs in enumerate(BANK_JOBS) for i, name in enumerate(jobs)}

COLS = {}
_n = 0
for _name, _k in (("ada", 9 * CB), ("qkv", 3 * CB), ("q", CB), ("kv", 2 * CB), ("m1", 2 * HJ), ("gamma", CB),
                  ("beta", CB), ("e_b1", E * RB), ("gate_b1", CB), ("cond", NB * CB), ("e_b2", E * CB)):
    COLS[_name] = _n
    _n += _k
NCOL = _n

FIRST_ORDER = ["h00", "h01", "h10", "h11", "h20", "h21", "hg"]
TANH_ORDER = [f"m{j}" for j in range(HJ)] + FIRST_ORDER
TOPK_PER_UNIT = TILES * SLOTS * 4 * HPS

N_BIAS = 7
N_CONST = 9 + N_BIAS
STEP_SILU = 4
STEP_END = STEP_SILU + 4 * NB + 3 + PAR + E + 8 * (E + 1)
INIT_ADA_READ = 2 + 3 * NB
INIT_TURNS = INIT_ADA_READ + 2 + E + NB
INIT_E2_READ = INIT_TURNS + 4 + 2 * CB + 2
STEPS_A = 1 + 2 * (1 + 8)
STEPS_B = 5 + 8


def topk_base(t, s):
    return (t * SLOTS + s) * 4 * HPS


def tb_of(name):
    return JOB[name][0] - 5


def bass_pixart_experts(nc, x, cond, ctx_in, w_ada, b_ada, w_qkv, b_qkv, w_so, b_so, w_q, b_q, w_kv, b_kv,
                        w_co, b_co, w_m1, b_m1, w_m2, b_m2, gamma, beta, wq1, wk1, wv1, router_w, router_b,
                        e_w1, e_b1, e_w2, e_b2, gate_w1, gate_b1, gate_w2, gate_b2, out_w, out_b, out):
    x_rows = x.rearrange("b l c -> (b l) c")
    out_rows = out.rearrange("b l c -> (b l) c")
    ctx_rows = ctx_in.rearrange("b l c -> (b l) c")

    with ExitStack() as stack:
        def sb(name, shape, dt=F32):
            return stack.enter_context(nc.sbuf_tensor(name, shape, dt))

        def sem(name):
            return stack.enter_context(nc.semaphore(name))

        Wqkv = sb("Wqkv", [P, CB, 3 * C])
        Wso = sb("Wso", [P, CB, C])
        Wso_g = sb("Wso_g", [P, CB, C])
        Wq2 = sb("Wq2", [P, CB, C])
        Wkv = sb("Wkv", [P, CB, 2 * C])
        Wco = sb("Wco", [P, CB, C])
        Wco_g = sb("Wco_g", [P, CB, C])
        Wm1 = sb("Wm1", [P, CB, 2 * HID])
        Wm2_g = sb("Wm2_g", [P, HJ, C])
        W1nx = sb("W1nx", [P, CB, W1N])
        W1ev = sb("W1ev", [P, CB, W1N])
        Rw = sb("Rw", [P, 3 * CB, E])
        W2p = sb("W2p", [P, E * RB, C])
        Wg2 = sb("Wg2", [P, CB, C])
        MT = sb("MT", [P, CB, C])
        Wv1 = sb("Wv1", [P, CB, C])
        ident = sb("ident", [P, P])
        cols = sb("cols", [P, NCOL])
        b1half = sb("b1half", [P, HJ])
        Gall = sb("Gall", [P, NB * 3, C])
        mods = sb("mods", [P, NB, 12])
        betas = sb("betas", [P, NB, W1B])
        rbias_all = sb("rbias_all", [P, NB, E])
        maskE = sb("maskE", [P, 1])
        maskO = sb("maskO", [P, 1])
        kbias = sb("kbias", [P, PAR, CB])
        neghalf = sb("neghalf", [P, TILES])
        ones3 = sb("ones3", [96, P], BF16)
        onesf = sb("onesf", [1, P])
        rows = sb("rows", [1, 4, C])
        bias3 = {n: sb(f"bias3_{n}", [96, TILES, C], BF16) for n in ("so", "co", "mo", "e0", "e1", "e2", "g2")}
        split = sb("split", [1, 2, C])
        split_b = sb("split_b", [1, C], BF16)

        modA = sb("modA", [P, 8])
        modB = sb("modB", [P, 4])
        ctx_sb = sb("ctx_sb", [LC, C])
        ctxT = sb("ctxT", [P, CB, LC])
        kc = [sb(f"kc{e}", [P, CB, LC]) for e in range(PAR)]
        vc = sb("vc", [LC, H, DV])
        vT1 = sb("vT1", [P, CB, LC])
        Gp = sb("Gp", [P, CB, LC])
        Vp = sb("Vp", [LC, W1N + E])
        betaF = sb("betaF", [P, W1B])
        betaH = sb("betaH", [P, W1B])
        rbias = sb("rbias", [P, E])

        xin = sb("xin", [P, TILES, C])
        x1 = sb("x1", [P, TILES, C])
        x2 = sb("x2", [P, TILES, C])
        xnA = sb("xnA", [P, TILES, C])
        xnB = sb("xnB", [P, TILES, C])
        stat = [sb(f"stat{i}", [P, TILES, 6]) for i in range(4)]
        mv = [sb(f"mv{i}", [P, TILES, 2]) for i in range(4)]
        vare = [sb(f"vare{i}", [P, TILES]) for i in range(4)]
        rstd = [sb(f"rstd{i}", [P, TILES]) for i in range(4)]
        hA = sb("hA", [P, CB, UT])
        qT = sb("qT", [P, CB, UT])
        keys_or_knocked = sb("keys_or_knocked", [P, H * LC])
        km = [keys_or_knocked[:, i * CB * UT:(i + 1) * CB * UT].rearrange("p (f t) -> p f t", f=CB) for i in range(PAR)]
        K = keys_or_knocked[:, 0:H * LC].rearrange("p (h c) -> p h c", h=H)
        va = sb("va", [P, TILES, H, DV])
        rmax = sb("rmax", [P, TILES, H])
        prob_or_scores = sb("prob_or_scores", [P, TILES * H * LC])
        prob = prob_or_scores[:, 0:H * P].rearrange("p (s i k) -> p s i k", s=SLOTS, i=HPS)
        S = prob_or_scores[:, :].rearrange("p (t h c) -> p t h c", t=TILES, h=H)
        probT = sb("probT", [P, SLOTS, HPS, P])
        rsum = sb("rsum", [P, TILES, H])
        on, oT, q2T = xnA, hA, qT
        on2 = prob_or_scores[:, 0:TILES * C].rearrange("p (t c) -> p t c", t=TILES)
        oT2 = km[0]
        Dx = sb("Dx", [P, TILES, H, LC])
        M1 = sb("M1", [P, TILES, H, 8])
        M2 = sb("M2", [P, H, 8])

        hB = sb("hB", [P, CB, UT])
        nxT = hB
        tb = [sb(f"tb{i}", [P, 2 * UT]) for i in range(2)]
        gT = sb("gT", [P, HJ, UT])
        hE = gT[:, :, :].rearrange("p (a k) t -> p a k t", a=2)
        pw = sb("pw", [P, TILES, LC])
        pm = sb("pm", [P, TILES])
        psu = sb("psu", [P, TILES])
        wT = sb("wT", [LC, UT])
        rl = sb("rl", [P, TILES, E])
        rm = sb("rm", [P, TILES])
        rs = sb("rs", [P, TILES])
        rp = sb("rp", [P, TILES, E])
        gs = xnB
        acc = sb("acc", [P, TILES, C])
        tg = tb[0]

        colrows = tb[1][0:NCOL, 0:P]
        big = [Dx[:, :, :, :].rearrange("p t h c -> p (t h c)"), prob_or_scores[:, :]]
        Wada = [r[:, 0:9 * C] for r in big]
        W1an = [r[:, 0:W1N] for r in big]
        wk_sb, wq_sb, outw = hA, qT, probT[:, 0].rearrange("p (k a) c -> p k (a c)", k=CB)
        wkT, wqT = km[0], km[1]
        ew2 = gT
        e2Tv = prob_or_scores[:, 0:CB * RB * P].rearrange("p (a k) -> p a k", a=CB)
        modBc = xnB
        siluT = sb("siluT", [P, NB, CB])
        tanhT = sb("tanhT", [P, NB, CB])

        psum = [stack.enter_context(nc.psum_tensor(f"bank{i}", [P, 512], F32)) for i in range(8)]

        full = [sem(f"full{i}") for i in range(8)]
        drained = [sem(f"drained{i}") for i in range(8)]
        x_loaded, y_ready, y_stored = sem("x_loaded"), sem("y_ready"), sem("y_stored")
        stats = [sem(f"ln_stats{i}") for i in range(4)]
        rstds = [sem(f"ln_rstd{i}") for i in range(4)]
        normed = [sem(f"normed{i}") for i in range(4)]
        row_max, probs = sem("row_max"), sem("probs")
        sums_inverted = sem("sums_inverted")
        topk, shifted, cross_exp, picked = sem("topk"), sem("shifted"), sem("cross_exp"), sem("picked")
        tanh_done, half_gated, gated = sem("tanh_done"), sem("half_gated"), sem("gated")
        proto_max, proto_exp, proto_steps = sem("proto_max"), sem("proto_exp"), sem("proto_steps")
        route_steps, route_exp, route_done = sem("route_steps"), sem("route_exp"), sem("route_done")
        mixed, gate_tanh = sem("mixed"), sem("gate_tanh")
        w_loaded, wm2_loaded, big_loaded, ew2_loaded, ctx_loaded = sem("w_loaded"), sem("wm2_loaded"), sem("big_loaded"), sem("ew2_loaded"), sem("ctx_loaded")
        consts, dve_step, init_full, init_read, init_tanh = sem("consts"), sem("dve_step"), sem("init_full"), sem("init_read"), sem("init_tanh")
        fullA, readA, doneA, gatedA = sem("prepA_full"), sem("prepA_read"), sem("prepA_done"), sem("gatedA")
        fullB, readB, doneB, gatedB = sem("prepB_full"), sem("prepB_read"), sem("prepB_done"), sem("gatedB")
        stepA, stepB = sem("prepA_step"), sem("prepB_step")

        passed = sem("passed")
        rrow = sb("rrow", [1, E])
        ROW = {"so": rows[0:1, 0, :], "co": rows[0:1, 1, :], "m2": rows[0:1, 2, :], "tmp": rows[0:1, 3, :],
               "gs": x1[0:1, 0, :], "gc": x1[0:1, 1, :], "gm": x2[0:1, 0, :], "out": x2[0:1, 1, :], "e0": acc[0:1, 0, :],
               "e1": acc[0:1, 1, :], "e2": xnA[0:1, 0, :], "g2": xnA[0:1, 1, :]}

        def row(n):
            return ROW[n]

        def wait_full(eng, name, u):
            bank, i, n = JOB[name]
            eng.wait_ge(full[bank], u * n + (i + 1))

        def wait_drained(eng, name, u):
            bank, i, n = JOB[name]
            eng.wait_ge(drained[bank], u * n + (i + 2))

        def wait_free(eng, name, u):
            bank, i, n = JOB[name]
            eng.wait_ge(drained[bank], u * n + (i + 1))

        def alone(eng):
            eng.sem_inc(passed, 1)

        def bank_of(name):
            return psum[JOB[name][0]]

        HEADS = [(s, j, e) for s in range(SLOTS) for j in range(PAIR) for e in range(PAR)]

        def head(s, i):
            return 8 * (i // PAR) + 2 * s + i % PAR

        col_loads = [("ada", b_ada, 9 * CB), ("qkv", b_qkv, 3 * CB), ("q", b_q, CB), ("kv", b_kv, 2 * CB), ("m1", b_m1, 2 * HJ),
                     ("gamma", gamma, CB), ("beta", beta, CB), ("e_b1", e_b1.rearrange("e r -> (e r)"), E * RB),
                     ("gate_b1", gate_b1, CB), ("cond", cond.rearrange("b c -> (b c)"), NB * CB),
                     ("e_b2", e_b2.rearrange("e c -> (e c)"), E * CB)]

        def blocks(w):
            return w.rearrange("(k p) n -> p k n", p=P)

        def rank1(v):
            return v.rearrange("(a n) -> a n", a=1)

        ew1 = [e_w1[e].rearrange("(k p) n -> p k n", p=P) for e in range(E)]
        gw1 = blocks(gate_w1)

        def part_loads(dst, part):
            k = slice(part * CB, (part + 1) * CB)
            return [(dst[:, :, e * RH:(e + 1) * RH], ew1[e][:, k, :]) for e in range(E)] + \
                   [(dst[:, :, E * RH:W1N], gw1[:, k, :])]

        small_loads = [(colrows[COLS[n]:COLS[n] + k, :], v.rearrange("(k p) -> k p", p=P)) for n, v, k in col_loads]
        small_loads += [(row("gs"), rank1(b_ada[2 * C:3 * C])), (row("gc"), rank1(b_ada[5 * C:6 * C])),
                        (row("gm"), rank1(b_ada[8 * C:9 * C])), (row("so"), rank1(b_so)), (row("co"), rank1(b_co)),
                        (row("m2"), rank1(b_m2)), (row("g2"), rank1(gate_b2)), (row("out"), rank1(out_b)),
                        (rrow[:, :], rank1(router_b))]
        big_loads = [(Wada[k], w_ada[k * P:(k + 1) * P, :]) for k in range(CB)]
        weight_loads = [(Wqkv[:, :, :], blocks(w_qkv)), (Wso[:, :, :], blocks(w_so)), (Wq2[:, :, :], blocks(w_q)),
                        (Wkv[:, :, :], blocks(w_kv)), (Wco[:, :, :], blocks(w_co)),
                        (wk_sb[:, :, :], blocks(wk1)), (wq_sb[:, :, :], blocks(wq1)), (outw[:, :, :], blocks(out_w)),
                        (Wv1[:, :, :], blocks(wv1)), (Wg2[:, :, :], blocks(gate_w2)), (Rw[:, :, :], blocks(router_w)),
                        (Wm1[:, :, :], blocks(w_m1))] + part_loads(W1nx, 0) + part_loads(W1ev, 1)
        anchor_loads = [(W1an[k][:, e * RH:(e + 1) * RH], ew1[e][:, 2 * CB + k, :]) for k in range(CB) for e in range(E)] + \
                       [(W1an[k][:, E * RH:W1N], gw1[:, 2 * CB + k, :]) for k in range(CB)]
        N_SMALL, N_W, N_AN = len(small_loads), len(weight_loads), len(anchor_loads)
        e2_rows = e_w2.rearrange("e (k p) n -> p (e k) n", p=P)
        EW = [(0, 4), (4, 8), (8, 12)]

        block = stack.enter_context(nc.Block())

        @block.sync
        def _(sp):
            for s in (*drained, mixed):
                sp.sem_inc(s, 1)
            sp.sem_inc(y_stored, 16)
            for dst, src in small_loads:
                sp.dma_start(dst, src).then_inc(w_loaded, 16)
            for dst, src in big_loads:
                sp.dma_start(dst, src).then_inc(big_loaded, 16)
            for dst, src in weight_loads:
                sp.dma_start(dst, src).then_inc(w_loaded, 16)
            sp.dma_start(ew2[:, :, :], e2_rows[:, 0:8, :]).then_inc(ew2_loaded, 16)
            sp.wait_ge(init_read, INIT_ADA_READ)
            for dst, src in anchor_loads:
                sp.dma_start(dst, src).then_inc(big_loaded, 16)
            sp.wait_ge(init_read, INIT_E2_READ)
            sp.dma_start(ew2[:, 0:4, :], e2_rows[:, 8:12, :]).then_inc(ew2_loaded, 16)

            def spans(u):
                at = ((u >> 2) & 3) * L
                uu = u & 3
                first = at + uu * UT + SHIFT
                return first, first + WIN, at + ((uu + 1) & 3) * UT

            def load_x(u):
                r0, r1, r2 = spans(u)
                sp.dma_start(xin[:, 0, :], x_rows[bass.ds(r0, WIN), :]).then_inc(x_loaded, 16)
                sp.dma_start(xin[0:SHIFT, 1, :], x_rows[bass.ds(r1, SHIFT), :]).then_inc(x_loaded, 16)
                sp.dma_start(xin[SHIFT:WIN, 1, :], x_rows[bass.ds(r2, SHIFT), :]).then_inc(x_loaded, 16)

            def store_y(u):
                r0, r1, r2 = spans(u)
                sp.wait_ge(y_ready, u + 1)
                alone(sp)
                sp.dma_start(out_rows[bass.ds(r0, WIN), :], acc[:, 0, :]).then_inc(y_stored, 16)
                sp.dma_start(out_rows[bass.ds(r1, SHIFT), :], acc[0:SHIFT, 1, :]).then_inc(y_stored, 16)
                sp.dma_start(out_rows[bass.ds(r2, SHIFT), :], acc[SHIFT:WIN, 1, :]).then_inc(y_stored, 16)

            def load_wm2():
                sp.dma_start(Wm2_g[:, :, :], blocks(w_m2)).then_inc(wm2_loaded, 16)

            def load_ctx(b):
                sp.dma_start(ctx_sb[:, :], ctx_rows[bass.ds((b & 3) * LC, LC), :]).then_inc(ctx_loaded, 16)

            load_ctx(0)
            load_x(0)
            load_wm2()
            wait_drained(sp, "so", 0)
            load_x(1)
            with sp.Fori(0, NB) as b:
                sp.wait_ge(fullA, b * 3 + 1)
                alone(sp)
                load_ctx(b + 1)
                with sp.Fori(0, UNITS - 1) as r:
                    u = b * UNITS + r
                    wait_drained(sp, "so", u + 1)
                    alone(sp)
                    load_x(u + 2)
                    store_y(u)
                u = b * UNITS + (UNITS - 1)
                wait_full(sp, "mo", u)
                alone(sp)
                load_wm2()
                wait_drained(sp, "so", u + 1)
                alone(sp)
                load_x(u + 2)
                store_y(u)
            sp.wait_ge(wm2_loaded, 16 * (NB + 1))
            sp.wait_ge(y_stored, 48 * NB * UNITS + 16)
            sp.wait_ge(x_loaded, 48 * (NB * UNITS + 2))
            sp.wait_ge(ctx_loaded, 16 * (NB + 1))

        @block.tensor
        def _(pe):
            pe_job = [0]

            def init_job(n=1):
                k = pe_job[0]
                pe_job[0] += 1
                if k >= 8:
                    pe.wait_ge(init_read, k - 7)
                return psum[k % 8]

            def prep_weights():
                pe.wait_ge(consts, N_CONST)
                pe.wait_ge(w_loaded, 16 * (N_SMALL + N_W))
                bk = init_job()
                pe.transpose(bk[:, 0:NCOL], colrows[:, :], ident[0:NCOL, 0:NCOL]).then_inc(init_full, 1)
                pe.wait_ge(init_read, 1)
                pe.wait_ge(dve_step, STEP_SILU)
                pe.wait_ge(big_loaded, 16 * CB)
                bk = init_job()
                for n, sec in enumerate((1, 0, 4, 3, 7, 6)):
                    for f in range(CB):
                        o = bk[:, (n * CB + f) * NB:(n * CB + f + 1) * NB]
                        for k in range(CB):
                            m = pe.matmul(o, Wada[k][:, sec * C + f * P:sec * C + (f + 1) * P], siluT[:, :, k],
                                          start=(k == 0), stop=(k == CB - 1))
                m.then_inc(init_full, 1)
                for b in range(NB):
                    pe.wait_ge(dve_step, STEP_SILU + 2 * (b + 1))
                    for g, (sec, r) in enumerate(((2, "gs"), (5, "gc"), (8, "gm"))):
                        bk = init_job()
                        for k in range(CB):
                            pe.matmul(bk[:, 0:C], modBc[:, k, 0:P], Wada[k][:, sec * C:(sec + 1) * C], start=(k == 0), stop=False)
                        pe.matmul(bk[:, 0:C], onesf[:, :], row(r), start=False, stop=True).then_inc(init_full, 1)
                for col, w in ((COLS["qkv"] + 2 * CB, Wso), (COLS["kv"] + CB, Wco)):
                    bk = init_job()
                    for k in range(CB):
                        m = pe.matmul(bk[0:1, 0:C], cols[:, col + k:col + k + 1], w[:, k, :], start=(k == 0), stop=(k == CB - 1))
                    m.then_inc(init_full, 1)
                for e in range(E):
                    bk = init_job()
                    for k in range(CB):
                        col = COLS["e_b2"] + e * CB + k
                        m = pe.matmul(bk[0:1, 0:C], cols[:, col:col + 1], outw[:, k, :], start=(k == 0), stop=(k == CB - 1))
                    m.then_inc(init_full, 1)
                for b in range(NB):
                    pe.wait_ge(dve_step, STEP_SILU + 2 * NB + 2 * (b + 1))
                    bk = init_job()
                    for k in range(CB):
                        pe.matmul(bk[:, 0:E], modBc[:, k, 0:P], Rw[:, 2 * CB + k, :], start=(k == 0), stop=False)
                    pe.matmul(bk[:, 0:E], onesf[:, :], rrow[:, :], start=False, stop=True).then_inc(init_full, 1)
                for w in (wk_sb, wq_sb):
                    bk = init_job()
                    for k in range(CB):
                        for h in range(CB):
                            m = pe.transpose(bk[:, h * C + k * P:h * C + (k + 1) * P], w[:, k, h * P:(h + 1) * P], ident[:, :])
                    m.then_inc(init_full, 1)
                pe.wait_ge(init_read, pe_job[0])
                bk = init_job()
                for c in range(CB):
                    for h in range(CB):
                        m = pe.matmul(bk[:, c * C:(c + 1) * C], wkT[:, h, c * P:(c + 1) * P], wqT[:, h, :], start=(h == 0), stop=(h == CB - 1))
                m.then_inc(init_full, 1)
                pe.wait_ge(big_loaded, 16 * (CB + N_AN))
                bk = init_job()
                condT = cols[:, COLS["cond"]:COLS["cond"] + NB * CB].rearrange("p (b k) -> p b k", k=CB)
                for n in range(W1B):
                    for k in range(CB):
                        m = pe.matmul(bk[:, n * NB:(n + 1) * NB], W1an[k][:, n * P:(n + 1) * P], condT[:, :, k],
                                      start=(k == 0), stop=(k == CB - 1))
                m.then_inc(init_full, 1)
                for e in range(E):
                    pe.wait_ge(ew2_loaded, 16 if e < 2 else 32)
                    src = e * RB if e < 2 else 0
                    for h in range(CB):
                        bk = init_job()
                        for k in range(RB):
                            m = pe.transpose(bk[:, k * P:(k + 1) * P], ew2[:, src + k, h * P:(h + 1) * P], ident[:, :])
                        m.then_inc(init_full, 1)
                    pe.wait_ge(init_read, pe_job[0])
                    for k2 in range(RB // 2):
                        bk = init_job()
                        for k in (2 * k2, 2 * k2 + 1):
                            for h in range(CB):
                                m = pe.matmul(bk[:, (k % 2) * C:(k % 2 + 1) * C], e2Tv[:, h, k * P:(k + 1) * P], outw[:, h, :],
                                              start=(h == 0), stop=(h == CB - 1))
                        m.then_inc(init_full, 1)
                pe.wait_ge(init_read, pe_job[0])
                pe.wait_ge(dve_step, STEP_END)

            def prep_a(b, units):
                pe.wait_ge(ctx_loaded, b * 16 + 16)
                if not isinstance(units, int):
                    for i in range(4):
                        pe.wait_ge(drained[i], units * len(BANK_JOBS[i]) + 1)
                for k in range(CB):
                    m = pe.transpose(psum[0][:, k * LC:(k + 1) * LC], ctx_sb[:, k * P:(k + 1) * P], ident[0:LC, 0:LC])
                m.then_inc(fullA, 1)
                pe.wait_ge(readA, b * 3 + 1)
                for f in range(CB):
                    for k in range(CB):
                        m = pe.matmul(psum[1][:, f * LC:(f + 1) * LC], Wkv[:, k, f * P:(f + 1) * P], ctxT[:, k, :],
                                      start=(k == 0), stop=(k == CB - 1))
                m.then_inc(fullA, 1)
                for k in range(CB):
                    m = pe.matmul(psum[2][0:LC, 0:C], ctxT[:, k, :], Wkv[:, k, C:2 * C], start=(k == 0), stop=(k == CB - 1))
                m.then_inc(fullA, 1)
                pe.wait_ge(readA, b * 3 + 3)
                pe.wait_ge(gatedA, b * 4 + 4)
                pe.wait_ge(doneA, b + 1)

            def prep_b(b):
                if not isinstance(b, int):
                    for i in (5, 6, 7):
                        pe.wait_ge(drained[i], b * (UNITS * len(BANK_JOBS[i])) + 1)
                for h in range(CB):
                    for k in range(CB):
                        m = pe.matmul(psum[5][:, h * LC:(h + 1) * LC], Wv1[:, k, h * P:(h + 1) * P], ctxT[:, k, :],
                                      start=(k == 0), stop=(k == CB - 1))
                m.then_inc(fullB, 1)
                for c in range(CB):
                    for k in range(CB):
                        m = pe.matmul(psum[6][:, c * LC:(c + 1) * LC], MT[:, k, c * P:(c + 1) * P], ctxT[:, k, :],
                                      start=(k == 0), stop=(k == CB - 1))
                m.then_inc(fullB, 1)
                pe.wait_ge(readB, b * 6 + 1)
                for n in range(4):
                    bk = psum[(7, 5, 6, 7)[n]]
                    if n:
                        pe.wait_ge(readB, b * 6 + n)
                    c0, c1 = n * 512, min((n + 1) * 512, W1N)
                    for h in range(CB):
                        m = pe.matmul(bk[0:LC, 0:c1 - c0], vT1[:, h, :], W1ev[:, h, c0:c1], start=(h == 0), stop=(h == CB - 1))
                    if n == 3:
                        for h in range(CB):
                            m = pe.matmul(bk[0:LC, c1 - c0:c1 - c0 + E], vT1[:, h, :], Rw[:, CB + h, :],
                                          start=(h == 0), stop=(h == CB - 1))
                    m.then_inc(fullB, 1)
                pe.wait_ge(readB, b * 6 + 6)
                pe.wait_ge(gatedB, b * HJ + HJ)
                pe.wait_ge(doneB, b + 1)
                alone(pe)

            def turn(name, src, u, sem_, per):
                wait_free(pe, name, u)
                pe.wait_ge(sem_, u * per + per)
                bk = bank_of(name)
                for f in range(CB):
                    for t in range(TILES):
                        m = pe.transpose(bk[:, f * UT + t * P:f * UT + (t + 1) * P], src[:, t, f * P:(f + 1) * P], ident[:, :])
                m.then_inc(full[JOB[name][0]], 1)

            def feature_major(name, w, c0, src, u):
                wait_free(pe, name, u)
                bk = bank_of(name)
                for f in range(CB):
                    for k in range(CB):
                        m = pe.matmul(bk[:, f * UT:(f + 1) * UT], w[:, k, c0 + f * P:c0 + (f + 1) * P], src[:, k, :],
                                      start=(k == 0), stop=(k == CB - 1))
                m.then_inc(full[JOB[name][0]], 1)

            def bias_first(name, which):
                pe.matmul(bank_of(name)[:, :], ones3[:, :], bias3[which][:, :, :].rearrange("p t c -> p (t c)"),
                          start=True, stop=False, skip_group_check=True)

            def token_major(name, src, w, nk, last=True):
                bk = bank_of(name)
                for k in range(nk):
                    for t in range(TILES):
                        m = pe.matmul(bk[:, t * C:(t + 1) * C], src[:, k, t * P:(t + 1) * P], w[:, k, :],
                                      start=False, stop=(k == nk - 1), skip_group_check=True)
                m.then_inc(full[JOB[name][0]], 1)

            def a_turn_input(u):
                turn("ln1", xnA, u, normed[0], TILES)

            def a_q(u):
                wait_drained(pe, "ln1", u)
                feature_major("q", Wqkv, 0, hA, u)

            def a_k(u):
                feature_major("k", Wqkv, C, hA, u)

            def a_v(u):
                wait_free(pe, "v", u)
                for t in range(TILES):
                    for k in range(CB):
                        m = pe.matmul(bank_of("v")[:, t * C:(t + 1) * C], hA[:, k, t * P:(t + 1) * P], Wqkv[:, k, 2 * C:3 * C],
                                      start=(k == 0), stop=(k == CB - 1))
                m.then_inc(full[JOB["v"][0]], 1)

            def a_scores(t, s, u):
                if t == 0 and s == 0:
                    wait_drained(pe, "q", u)
                    wait_drained(pe, "k", u)
                wait_free(pe, f"s{t}{s}", u)
                for i in range(HPS):
                    j, e = i // PAR, i % PAR
                    r = slice(32 * s, 32 * s + 32)
                    m = pe.matmul(psum[s][:, i * P:(i + 1) * P], qT[r, j, t * P:(t + 1) * P], km[e][r, j, t * P:(t + 1) * P],
                                  start=True, stop=True)
                m.then_inc(full[s], 1)

            def a_turn_probs(t, s, u):
                pe.wait_ge(probs, u * (TILES * SLOTS) + (t * SLOTS + s + 1))
                wait_free(pe, f"p{t}{s}", u)
                for i in range(HPS):
                    m = pe.transpose(psum[s][:, i * P:(i + 1) * P], prob[:, s, i, :], ident[:, :])
                m.then_inc(full[s], 1)

            def a_values(t, s, u):
                if s == 0:
                    wait_free(pe, f"pv{t}", u)
                    if t == 0:
                        wait_drained(pe, "v", u)
                wait_drained(pe, f"p{t}{s}", u)
                for i in range(HPS):
                    h = head(s, i)
                    m = pe.matmul(psum[4][:, h * DV:(h + 1) * DV], probT[:, s, i, :], va[:, t, h, :], start=True, stop=True)
                if s == SLOTS - 1:
                    m.then_inc(full[4], 1)

            def a_turn_outputs(name, src, pv, u):
                wait_drained(pe, pv, u)
                wait_free(pe, name, u)
                bk = bank_of(name)
                for f in range(CB):
                    for t in range(TILES):
                        m = pe.transpose(bk[:, f * UT + t * P:f * UT + (t + 1) * P], src[:, t, f * P:(f + 1) * P], ident[:, :])
                m.then_inc(full[JOB[name][0]], 1)

            def a_project(turn_name, src, name, w, u):
                wait_free(pe, name, u)
                bias_first(name, name)
                wait_drained(pe, turn_name, u)
                token_major(name, src, w, CB)

            def a_turn_query(u):
                turn("ln2", xnA, u, normed[1], TILES)

            def a_query(u):
                wait_drained(pe, "ln2", u)
                feature_major("q2", Wq2, 0, hA, u)

            def a_cross_scores(t, s, u):
                if t == 0 and s == 0:
                    wait_drained(pe, "q2", u)
                wait_free(pe, f"c{t}{s}", u)
                for i in range(HPS):
                    j, e = i // PAR, i % PAR
                    r = slice(32 * s, 32 * s + 32)
                    m = pe.matmul(psum[s][:, i * LC:(i + 1) * LC], q2T[r, j, t * P:(t + 1) * P], kc[e][r, j, :],
                                  start=True, stop=True)
                m.then_inc(full[s], 1)

            def a_turn_picked(t, s, u):
                if s % 2 == 0:
                    pe.wait_ge(picked, u * (TILES * 2) + (2 * t + s // 2 + 1))
                wait_free(pe, f"y{t}{s}", u)
                for i in range(HPS):
                    m = pe.transpose(psum[s][0:LC, i * P:(i + 1) * P], Dx[:, t, s * HPS + i, :], ident[:, :])
                m.then_inc(full[s], 1)

            def a_cross_values(t, s, u):
                if s == 0:
                    wait_free(pe, f"xv{t}", u)
                wait_drained(pe, f"y{t}{s}", u)
                for i in range(HPS):
                    h = head(s, i)
                    m = pe.matmul(psum[4][:, h * DV:(h + 1) * DV], probT[0:LC, s, i, :], vc[:, h, :], start=True, stop=True)
                if s == SLOTS - 1:
                    m.then_inc(full[4], 1)

            def b_hidden(j, u):
                name = f"m{j}"
                if j == 0:
                    wait_drained(pe, "ln3", u)
                wait_free(pe, name, u)
                for half in range(2):
                    for k in range(CB):
                        c = half * HID + j * P
                        m = pe.matmul(bank_of(name)[:, half * UT:(half + 1) * UT], Wm1[:, k, c:c + P], hB[:, k, :],
                                      start=(k == 0), stop=(k == CB - 1))
                m.then_inc(full[JOB[name][0]], 1)

            def b_down(j, u):
                if j == 0:
                    wait_free(pe, "mo", u)
                    bias_first("mo", "mo")
                wait_drained(pe, f"m{j}", u)
                for t in range(TILES):
                    m = pe.matmul(psum[7][:, t * C:(t + 1) * C], gT[:, j, t * P:(t + 1) * P], Wm2_g[:, j, :],
                                  start=False, stop=(j == HJ - 1), skip_group_check=True)
                if j == HJ - 1:
                    m.then_inc(full[7], 1)

            def b_turn_normed(u):
                turn("ln4", xnB, u, normed[3], TILES)

            def b_proto_scores(u):
                wait_drained(pe, "ln4", u)
                wait_free(pe, "ps", u)
                for t in range(TILES):
                    for k in range(CB):
                        m = pe.matmul(psum[7][:, t * LC:(t + 1) * LC], nxT[:, k, t * P:(t + 1) * P], Gp[:, k, :],
                                      start=(k == 0), stop=(k == CB - 1))
                m.then_inc(full[7], 1)

            def b_turn_weights(u):
                pe.wait_ge(proto_steps, u * 3 + 3)
                wait_free(pe, "wt", u)
                for t in range(TILES):
                    m = pe.transpose(bank_of("wt")[0:LC, t * P:(t + 1) * P], pw[:, t, :], ident[:, :])
                m.then_inc(full[JOB["wt"][0]], 1)

            def b_router(u):
                wait_drained(pe, "wt", u)
                wait_free(pe, "rt", u)
                for t in range(TILES):
                    o = psum[7][:, t * E:(t + 1) * E]
                    for k in range(CB):
                        pe.matmul(o, nxT[:, k, t * P:(t + 1) * P], Rw[:, k, :], start=(k == 0), stop=False)
                    m = pe.matmul(o, wT[:, t * P:(t + 1) * P], Vp[:, W1N:W1N + E], start=False, stop=True)
                m.then_inc(full[7], 1)

            def b_first_nx(name, c0, u):
                wait_free(pe, name, u)
                for n in range(2):
                    for k in range(CB):
                        pe.matmul(bank_of(name)[:, n * UT:(n + 1) * UT], W1nx[:, k, c0 + n * P:c0 + (n + 1) * P], nxT[:, k, :],
                                  start=(n == 0 and k == 0), stop=False, skip_group_check=True)

            def b_first_evidence(name, c0, u):
                for n in range(2):
                    m = pe.matmul(bank_of(name)[:, n * UT:(n + 1) * UT], Vp[:, c0 + n * P:c0 + (n + 1) * P], wT[:, :],
                                  start=False, stop=True, skip_group_check=True)
                m.then_inc(full[JOB[name][0]], 1)

            def b_first(name, c0, u):
                b_first_nx(name, c0, u)
                b_first_evidence(name, c0, u)

            def b_second(e, part, u):
                name = f"e{e}"
                if part == 0:
                    wait_free(pe, name, u)
                    bias_first(name, name)
                pe.wait_ge(gated, u * len(FIRST_ORDER) + (2 * e + part + 1))
                for k in (2 * part, 2 * part + 1):
                    for t in range(TILES):
                        m = pe.matmul(psum[7][:, t * C:(t + 1) * C], hE[:, e % 2, k, t * P:(t + 1) * P], W2p[:, e * RB + k, :],
                                      start=False, stop=(k == RB - 1), skip_group_check=True)
                if part == 1:
                    m.then_inc(full[7], 1)

            def b_gate(u):
                wait_free(pe, "g2", u)
                bias_first("g2", "g2")
                pe.wait_ge(gated, u * len(FIRST_ORDER) + len(FIRST_ORDER))
                token_major("g2", gs, Wg2, CB)

            def stage_a(u):
                a_turn_input(u)
                a_q(u)
                a_k(u)
                a_v(u)
                for s in range(SLOTS):
                    a_scores(0, s, u)
                for s in range(SLOTS):
                    a_turn_probs(0, s, u)
                    a_scores(1, s, u)
                for s in range(SLOTS):
                    a_values(0, s, u)
                for s in range(SLOTS):
                    a_turn_probs(1, s, u)
                for s in range(SLOTS):
                    a_values(1, s, u)
                a_turn_outputs("o1", on, "pv1", u)
                a_project("o1", oT, "so", Wso_g, u)
                a_turn_query(u)
                a_query(u)
                for t in range(TILES):
                    for s in range(SLOTS):
                        a_cross_scores(t, s, u)
                for t in range(TILES):
                    for s in range(SLOTS):
                        a_turn_picked(t, s, u)
                    for s in range(SLOTS):
                        a_cross_values(t, s, u)
                a_turn_outputs("o2", on2, "xv1", u)
                a_turn_input(u + 1)
                a_project("o2", oT2, "co", Wco_g, u)

            def both(ua, ub):
                a_q(ua)
                a_k(ua)
                a_v(ua)
                for s in range(SLOTS):
                    a_scores(0, s, ua)
                turn("ln3", xnB, ub, normed[2], TILES)
                a_turn_probs(0, 0, ua)
                b_hidden(0, ub)
                a_turn_probs(0, 1, ua)
                b_hidden(1, ub)
                a_turn_probs(0, 2, ua)
                a_turn_probs(0, 3, ua)
                a_scores(1, 0, ua)
                b_hidden(2, ub)
                a_scores(1, 1, ua)
                b_down(0, ub)
                a_scores(1, 2, ua)
                a_scores(1, 3, ua)
                b_down(1, ub)
                b_hidden(3, ub)
                a_values(0, 0, ua)
                a_values(0, 1, ua)
                b_hidden(4, ub)
                a_values(0, 2, ua)
                a_values(0, 3, ua)
                b_down(2, ub)
                a_turn_probs(1, 0, ua)
                a_turn_probs(1, 1, ua)
                b_hidden(5, ub)
                a_turn_probs(1, 2, ua)
                a_turn_probs(1, 3, ua)
                a_values(1, 0, ua)
                a_values(1, 1, ua)
                a_values(1, 2, ua)
                a_values(1, 3, ua)
                b_down(3, ub)
                a_turn_outputs("o1", on, "pv1", ua)
                b_down(4, ub)
                a_project("o1", oT, "so", Wso_g, ua)
                b_hidden(6, ub)
                b_down(5, ub)
                b_hidden(7, ub)
                a_turn_query(ua)
                b_down(6, ub)
                a_query(ua)
                b_down(7, ub)
                for s in range(SLOTS):
                    a_cross_scores(0, s, ua)
                a_cross_scores(1, 0, ua)
                b_turn_normed(ub)
                a_cross_scores(1, 1, ua)
                b_proto_scores(ub)
                b_first_nx("h00", 0, ub)
                a_cross_scores(1, 2, ua)
                b_turn_weights(ub)
                b_first_nx("h01", 2 * P, ub)
                a_cross_scores(1, 3, ua)
                b_router(ub)
                b_first_evidence("h00", 0, ub)
                b_first_evidence("h01", 2 * P, ub)
                b_first("h10", RH, ub)
                b_second(0, 0, ub)
                b_second(0, 1, ub)
                b_first("h11", RH + 2 * P, ub)
                for s in range(SLOTS):
                    a_turn_picked(0, s, ua)
                b_first("h20", 2 * RH, ub)
                a_cross_values(0, 0, ua)
                a_cross_values(0, 1, ua)
                b_second(1, 0, ub)
                a_cross_values(0, 2, ua)
                a_cross_values(0, 3, ua)
                b_second(1, 1, ub)
                b_first("h21", 2 * RH + 2 * P, ub)
                b_first("hg", 3 * RH, ub)
                for s in range(SLOTS):
                    a_turn_picked(1, s, ua)
                b_second(2, 0, ub)
                a_cross_values(1, 0, ua)
                a_cross_values(1, 1, ua)
                b_second(2, 1, ub)
                a_cross_values(1, 2, ua)
                a_cross_values(1, 3, ua)
                a_turn_input(ua + 1)
                a_turn_outputs("o2", on2, "xv1", ua)
                b_gate(ub)
                a_project("o2", oT2, "co", Wco_g, ua)

            prep_weights()
            prep_a(0, 0)
            stage_a(0)
            with pe.Fori(0, NB) as b:
                prep_b(b)
                with pe.Fori(0, UNITS - 1) as r:
                    u = b * UNITS + r
                    both(u + 1, u)
                prep_a(b + 1, b * UNITS + UNITS)
                both(b * UNITS + UNITS, b * UNITS + (UNITS - 1))

        @block.scalar
        def _(act):
            def copy_job(dst, name, u, view=None):
                wait_full(act, name, u)
                act.activation(dst, bank_of(name)[:, :] if view is None else view, ACT.Copy).then_inc(drained[JOB[name][0]], 1)

            def modulate(dst, name, u, scale, shift):
                wait_full(act, name, u)
                for f in range(CB):
                    i = act.activation(dst[:, f, :], bank_of(name)[:, f * UT:(f + 1) * UT], ACT.Identity,
                                       bias=shift(f), scale=scale(f))
                i.then_inc(drained[JOB[name][0]], 1)

            def add_bias(dst, name, u, c0):
                wait_full(act, name, u)
                for f in range(CB):
                    i = act.activation(dst[:, f, :], bank_of(name)[:, f * UT:(f + 1) * UT], ACT.Identity,
                                       bias=cols[:, c0 + f:c0 + f + 1])
                i.then_inc(drained[JOB[name][0]], 1)

            def a_modulate(name, u, first):
                modulate(hA, name, u, lambda f: modA[:, first + f:first + f + 1], lambda f: modA[:, first + CB + f:first + CB + f + 1])

            def a_keys(u):
                wait_full(act, "k", u)
                for e, m in enumerate((maskE, maskO)):
                    for f in range(CB):
                        i = act.activation(km[e][:, f, :], bank_of("k")[:, f * UT:(f + 1) * UT], ACT.Identity,
                                           bias=kbias[:, e, f:f + 1], scale=m[:, 0:1])
                i.then_inc(drained[JOB["k"][0]], 1)

            def a_exp(t, s, u):
                wait_drained(act, f"s{t}{s}", u)
                act.activation(prob[:, s], prob[:, s], ACT.Exp, scale=float(D) ** -0.5).then_inc(probs, 1)

            def a_copy_turned(t, s, u, kind, np_=P):
                name = f"{kind}{t}{s}"
                wait_full(act, name, u)
                act.activation(probT[0:np_, s], psum[s][0:np_, :].rearrange("p (i q) -> p i q", i=HPS), ACT.Copy)\
                   .then_inc(drained[s], 1)

            def a_copy_outputs(name, dst, u):
                copy_job(dst[:, :, :].rearrange("p f t -> p (f t)"), name, u)

            def a_copy_scores(t, s, u):
                wait_full(act, f"c{t}{s}", u)
                act.activation(S[:, t, s * HPS:(s + 1) * HPS, :], psum[s][:, 0:HPS * LC].rearrange("p (i c) -> p i c", i=HPS),
                               ACT.Copy).then_inc(drained[s], 1)

            def a_cross_exp(t, half, u):
                act.wait_ge(shifted, u * (TILES * SLOTS) + (2 * (2 * t + half) + 2))
                g = slice(half * (H // 2), (half + 1) * (H // 2))
                act.activation(Dx[:, t, g], Dx[:, t, g], ACT.Exp, scale=float(D) ** -0.5).then_inc(cross_exp, 1)

            def b_tanh_mlp(j, u):
                name = f"m{j}"
                if j == 0:
                    act.wait_ge(mixed, u + 1)
                wait_full(act, name, u)
                act.activation(tb[tb_of(name)][:, 0:UT], bank_of(name)[:, 0:UT], ACT.Tanh, bias=b1half[:, j:j + 1], scale=0.5)
                c = COLS["m1"] + j
                act.activation(gT[:, j, :], bank_of(name)[:, 0:UT], ACT.Identity, bias=cols[:, c:c + 1]).then_inc(tanh_done, 1)

            def b_tanh_first(name, dst, d0, n0, u):
                i = FIRST_ORDER.index(name)
                if i >= 2:
                    act.wait_ge(gated, u * len(FIRST_ORDER) + (i - 1))
                wait_full(act, name, u)
                for n in range(2):
                    act.activation(tb[tb_of(name)][:, n * UT:(n + 1) * UT], bank_of(name)[:, n * UT:(n + 1) * UT], ACT.Tanh,
                                   bias=betaH[:, n0 + n:n0 + n + 1], scale=0.5)
                for n in range(2):
                    o = dst[:, d0 + n, :]
                    if n == 0:
                        act.activation(o, bank_of(name)[:, 0:UT], ACT.Identity, bias=betaF[:, n0:n0 + 1]).then_inc(tanh_done, 1)
                    else:
                        act.activation(o, bank_of(name)[:, UT:2 * UT], ACT.Identity, bias=betaF[:, n0 + 1:n0 + 2])\
                           .then_inc(drained[JOB[name][0]], 1)

            def b_modulate(u):
                modulate(hB, "ln3", u, lambda f: modB[:, f:f + 1], lambda f: modB[:, CB + f:CB + f + 1])

            def b_affine(u):
                g, c = COLS["gamma"], COLS["beta"]
                modulate(nxT, "ln4", u, lambda f: cols[:, g + f:g + f + 1], lambda f: cols[:, c + f:c + f + 1])

            def b_proto_exp(u):
                wait_drained(act, "ps", u)
                act.activation(pw[:, :, :], pw[:, :, :], ACT.Exp, scale=float(C) ** -0.5).then_inc(proto_exp, 1)

            def b_copy_weights(u):
                wait_full(act, "wt", u)
                act.activation(wT[:, :], bank_of("wt")[0:LC, 0:UT], ACT.Copy).then_inc(drained[JOB["wt"][0]], 1)

            def b_route_exp(u):
                act.wait_ge(route_steps, u * 5 + 2)
                act.activation(rl[:, :, :], rl[:, :, :], ACT.Exp).then_inc(route_exp, 1)

            def b_gate_tanh(u):
                wait_full(act, "g2", u)
                act.activation(tg[:, :], psum[7][:, :], ACT.Tanh, scale=0.5).then_inc(drained[7], 1)

            def stage_a(u):
                a_modulate("ln1", u, 0)
                a_keys(u)
                for s in range(SLOTS):
                    a_exp(0, s, u)
                for s in range(SLOTS):
                    a_copy_turned(0, s, u, "p")
                for s in range(SLOTS):
                    a_exp(1, s, u)
                for s in range(SLOTS):
                    a_copy_turned(1, s, u, "p")
                a_copy_outputs("o1", oT, u)
                a_modulate("ln2", u, 2 * CB)
                add_bias(q2T, "q2", u, COLS["q"])
                for t in range(TILES):
                    for s in range(SLOTS):
                        a_copy_scores(t, s, u)
                for t in range(TILES):
                    a_cross_exp(t, 0, u)
                    a_cross_exp(t, 1, u)
                    for s in range(SLOTS):
                        a_copy_turned(t, s, u, "y", LC)
                a_copy_outputs("o2", oT2, u)

            def both(ua, ub):
                a_modulate("ln1", ua, 0)
                a_keys(ua)
                a_exp(0, 0, ua)
                b_modulate(ub)
                a_exp(0, 1, ua)
                a_copy_turned(0, 0, ua, "p")
                a_exp(0, 2, ua)
                b_tanh_mlp(0, ub)
                a_exp(0, 3, ua)
                a_copy_turned(0, 1, ua, "p")
                b_tanh_mlp(1, ub)
                a_copy_turned(0, 2, ua, "p")
                a_copy_turned(0, 3, ua, "p")
                b_tanh_mlp(2, ub)
                for s in range(SLOTS):
                    a_exp(1, s, ua)
                b_tanh_mlp(3, ub)
                b_tanh_mlp(4, ub)
                a_copy_turned(1, 0, ua, "p")
                a_copy_turned(1, 1, ua, "p")
                b_tanh_mlp(5, ub)
                a_copy_turned(1, 2, ua, "p")
                a_copy_turned(1, 3, ua, "p")
                a_copy_outputs("o1", oT, ua)
                b_tanh_mlp(6, ub)
                b_tanh_mlp(7, ub)
                a_modulate("ln2", ua, 2 * CB)
                add_bias(q2T, "q2", ua, COLS["q"])
                for s in range(SLOTS):
                    a_copy_scores(0, s, ua)
                a_copy_scores(1, 0, ua)
                b_affine(ub)
                a_copy_scores(1, 1, ua)
                b_proto_exp(ub)
                a_copy_scores(1, 2, ua)
                b_copy_weights(ub)
                a_copy_scores(1, 3, ua)
                b_route_exp(ub)
                b_tanh_first("h00", hE[:, 0], 0, 0, ub)
                a_cross_exp(0, 0, ua)
                b_tanh_first("h01", hE[:, 0], 2, 2, ub)
                a_cross_exp(0, 1, ua)
                b_tanh_first("h10", hE[:, 1], 0, 4, ub)
                b_tanh_first("h11", hE[:, 1], 2, 6, ub)
                for s in range(SLOTS):
                    a_copy_turned(0, s, ua, "y", LC)
                b_tanh_first("h20", hE[:, 0], 0, 8, ub)
                a_cross_exp(1, 0, ua)
                b_tanh_first("h21", hE[:, 0], 2, 10, ub)
                a_cross_exp(1, 1, ua)
                b_tanh_first("hg", gs, 0, 12, ub)
                for s in range(SLOTS):
                    a_copy_turned(1, s, ua, "y", LC)
                a_copy_outputs("o2", oT2, ua)
                b_gate_tanh(ub)

            act.wait_ge(init_read, 1)
            act.activation(tanhT[:, :, :], cols[:, COLS["cond"]:COLS["cond"] + NB * CB].rearrange("p (b k) -> p b k", k=CB),
                           ACT.Tanh, scale=0.5).then_inc(init_tanh, 1)
            act.wait_ge(dve_step, STEP_END)
            act.wait_ge(doneA, 1)
            stage_a(0)
            with act.Fori(0, NB) as b:
                act.wait_ge(doneB, b + 1)
                with act.Fori(0, UNITS - 1) as r:
                    u = b * UNITS + r
                    both(u + 1, u)
                act.wait_ge(doneA, b + 2)
                both(b * UNITS + UNITS, b * UNITS + (UNITS - 1))

        @block.gpsimd
        def _(pool):
            def rstd_of(i, eps, u):
                pool.wait_ge(stats[i], u * 4 + 4)
                alone(pool)
                pool.tensor_scalar(vare[i][:, :], mv[i][:, :, 1], eps, None, ALU.add).then_inc(rstds[i], 1)
                pool.wait_ge(rstds[i], u * 2 + 1)
                pool.tensor_tensor(rstd[i][:, :], vare[i][:, :], neghalf[:, :], ALU.pow).then_inc(rstds[i], 1)

            def a_shift(t, s, u):
                pool.wait_ge(topk, u * TOPK_PER_UNIT + (topk_base(t, s) + HPS))
                g = slice(s * HPS, (s + 1) * HPS)
                pool.tensor_tensor(Dx[:, t, g, :], S[:, t, g, :], M1[:, t, g, 0:1].to_broadcast([P, HPS, LC]), ALU.subtract)\
                    .then_inc(shifted, 1)

            def gate_a(b):
                for n, (dst, w) in enumerate(((Wso_g, Wso), (Wco_g, Wco))):
                    for k in range(CB):
                        pool.tensor_tensor(dst[:, k, :], w[:, k, :], Gall[:, bass.ds((b & 3) * 3 + n, 1), :]
                                           .rearrange("p a c -> p (a c)"), ALU.mult).then_inc(gatedA, 1)

            def gate_b(b):
                pool.wait_ge(wm2_loaded, b * 16 + 16)
                for k in range(HJ):
                    pool.tensor_tensor(Wm2_g[:, k, :], Wm2_g[:, k, :], Gall[:, bass.ds((b & 3) * 3 + 2, 1), :]
                                       .rearrange("p a c -> p (a c)"), ALU.mult).then_inc(gatedB, 1)

            def cross(u):
                for t in range(TILES):
                    for s in range(SLOTS):
                        a_shift(t, s, u)
                        if (t, s) == (1, 1):
                            rstd_of(0, EPS0, u + 1)

            def stage_a(u):
                rstd_of(0, EPS0, u)
                rstd_of(1, EPS0, u)
                cross(u)

            def both(ua, ub):
                rstd_of(2, EPS0, ub)
                rstd_of(1, EPS0, ua)
                rstd_of(3, EPS1, ub)
                cross(ua)

            pool.memset(ident[:, :], 0.0).then_inc(consts, 1)
            pool.memset(maskE[:, :], 0.0).then_inc(consts, 1)
            pool.memset(maskO[:, :], 0.0).then_inc(consts, 1)
            pool.memset(neghalf[:, :], -0.5).then_inc(consts, 1)
            pool.memset(onesf[:, :], 1.0).then_inc(consts, 1)
            pool.memset(ones3[:, :], 1.0).then_inc(consts, 1)
            pool.memset(va[:, :, :, :], 1.0).then_inc(consts, 1)
            pool.memset(vc[:, :, :], 1.0).then_inc(consts, 1)
            for n in bias3:
                pool.memset(bias3[n][:, :, :], 0.0).then_inc(consts, 1)
            pool.wait_ge(consts, 8 + len(bias3))
            pool.affine_select(out=ident[:, :], in_=ident[:, :], compare_op=ALU.not_equal, fill=1.0, base=0,
                               pattern=[[-1, P]], channel_multiplier=1).then_inc(consts, 1)
            pool.wait_ge(consts, 9 + len(bias3))
            pool.wait_ge(dve_step, STEP_END)
            gate_a(0)
            stage_a(0)
            with pool.Fori(0, NB) as b:
                gate_b(b)
                with pool.Fori(0, UNITS - 1) as r:
                    u = b * UNITS + r
                    both(u + 1, u)
                bank, i, n = JOB["co"]
                pool.wait_ge(full[bank], b * (UNITS * n) + UNITS * n)
                gate_a(b + 1)
                both(b * UNITS + UNITS, b * UNITS + (UNITS - 1))

        @block.vector
        def _(dve):
            step = [0]

            def chain(i, s=None):
                step[0] += 1
                i.then_inc(dve_step, 1)
                dve.wait_ge(dve_step, step[0])

            init = [0]

            def read_job(*ops):
                k = init[0]
                init[0] += 1
                dve.wait_ge(init_full, k + 1)
                for o in ops[:-1]:
                    o(psum[k % 8])
                ops[-1](psum[k % 8]).then_inc(init_read, 1)

            def three_parts(src, dst, sem_, base):
                n = [0]

                def go(i):
                    n[0] += 1
                    i.then_inc(sem_, 1)
                    dve.wait_ge(sem_, base + n[0])

                def spread(part):
                    return split_b[0:1, :].rearrange("p (a c) -> p a c", a=1).to_broadcast([1, TILES, C])

                cur = src
                for p in range(3):
                    go(dve.tensor_copy(split_b[0:1, :], cur))
                    go(dve.tensor_copy(dst[32 * p:32 * p + 1, :, :], spread(p)))
                    if p < 2:
                        nxt = split[0:1, p, :]
                        go(dve.tensor_tensor(nxt, cur, split_b[0:1, :], ALU.subtract))
                        cur = nxt
                return n[0]

            def prep_weights():
                dve.wait_ge(consts, 9 + len(bias3))
                for m, o in ((maskE, 0), (maskO, D)):
                    cv = ident[:, :].rearrange("p (s d) -> p s d", d=32)[:, :, o:o + D]
                    i = dve.tensor_reduce(m[:, :], cv, AX.XY, ALU.add)
                    chain(i)
                read_job(lambda bk: dve.tensor_copy(cols[:, :], bk[:, 0:NCOL]))
                dve.wait_ge(init_tanh, 1)
                dve.wait_ge(init_read, 1)
                condT = cols[:, COLS["cond"]:COLS["cond"] + NB * CB].rearrange("p (b k) -> p b k", k=CB)
                chain(dve.scalar_tensor_tensor(siluT[:, :, :], tanhT[:, :, :], 1.0, condT, ALU.add, ALU.mult))
                chain(dve.tensor_scalar(siluT[:, :, :], siluT[:, :, :], 0.5, None, ALU.mult))
                assert step[0] == STEP_SILU
                ada = cols[:, COLS["ada"]:COLS["ada"] + 9 * CB]

                def read_mods(bk):
                    v = bk[:, 0:12 * NB].rearrange("p (n b) -> p b n", b=NB)
                    for n, (sec, one) in enumerate(((1, 1.0), (0, 0.0), (4, 1.0), (3, 0.0), (7, 1.0), (6, 0.0))):
                        for f in range(CB):
                            i = dve.tensor_scalar(mods[:, :, n * CB + f], v[:, :, n * CB + f],
                                                  ada[:, sec * CB + f:sec * CB + f + 1], one, ALU.add, ALU.add)
                    return i

                read_job(read_mods)

                def spread_cols(src, b):
                    if b > 0:
                        dve.wait_ge(init_read, init[0])
                    for k in range(CB):
                        chain(dve.tensor_copy(modBc[:, k, 0:P], src[:, b, k:k + 1].to_broadcast([P, P])))

                for b in range(NB):
                    spread_cols(siluT, b)
                    for g in range(3):
                        read_job(lambda bk, b=b, g=g: dve.tensor_scalar(Gall[:, b * 3 + g, :], bk[:, 0:C], 0.5 if g == 2 else 1.0, None, ALU.mult))
                assert init[0] == INIT_ADA_READ
                for n in ("so", "co"):
                    read_job(lambda bk, n=n: dve.tensor_tensor(row(n), row(n), bk[0:1, 0:C], ALU.add))
                for e in range(E):
                    read_job(lambda bk, e=e: dve.tensor_tensor(row(f"e{e}"), bk[0:1, 0:C], row("out"), ALU.add))
                for b in range(NB):
                    spread_cols(condT, b)
                    read_job(lambda bk, b=b: dve.tensor_copy(rbias_all[:, b, :], bk[:, 0:E]))
                assert init[0] == INIT_TURNS
                for w in (wkT, wqT):
                    read_job(lambda bk, w=w: dve.tensor_copy(w[:, :, :].rearrange("p h c -> p (h c)"), bk[:, :]))
                read_job(lambda bk: dve.tensor_copy(MT[:, :, :].rearrange("p h c -> p (h c)"), bk[:, :]))
                def read_betas(bk):
                    v = bk[:, 0:W1B * NB].rearrange("p (n b) -> p b n", b=NB)
                    b1 = cols[:, COLS["e_b1"]:COLS["e_b1"] + W1B]
                    for b in range(NB):
                        i = dve.tensor_tensor(betas[:, b, :], v[:, b, :], b1, ALU.add)
                    return i

                read_job(read_betas)
                for e in range(E):
                    for h in range(CB):
                        read_job(lambda bk, h=h: dve.tensor_copy(e2Tv[:, h, :], bk[:, :]))
                    if e == 1:
                        assert init[0] == INIT_E2_READ
                    for k2 in range(RB // 2):
                        read_job(lambda bk, e=e, k2=k2: dve.tensor_scalar(
                            W2p[:, e * RB + 2 * k2:e * RB + 2 * k2 + 2, :].rearrange("p k c -> p (k c)"), bk[:, :], 0.25, None, ALU.mult))

                dve.wait_ge(init_read, init[0])
                chain(dve.tensor_scalar(Wg2[:, :, :], Wg2[:, :, :], 0.5, None, ALU.mult))
                for e, m in enumerate((maskE, maskO)):
                    chain(dve.tensor_scalar(kbias[:, e, :], cols[:, COLS["qkv"] + CB:COLS["qkv"] + 2 * CB], m[:, 0:1], None, ALU.mult))
                chain(dve.tensor_scalar(row("m2"), row("m2"), 2.0, None, ALU.mult))
                chain(dve.tensor_scalar(b1half[:, :], cols[:, COLS["m1"]:COLS["m1"] + HJ], 0.5, None, ALU.mult))
                for e in range(E):
                    chain(dve.tensor_scalar(row(f"e{e}"), row(f"e{e}"), 0.5, None, ALU.mult))
                for n, r in (("e0", "e0"), ("e1", "e1"), ("e2", "e2"), ("g2", "g2")):
                    step[0] += three_parts(row(r), bias3[n], dve_step, step[0])
                assert step[0] == STEP_END, step[0]

            def prep_a(b):
                bb = b & 3
                n = [0]

                def go(i):
                    n[0] += 1
                    i.then_inc(stepA, 1)
                    dve.wait_ge(stepA, b * STEPS_A + n[0])

                go(dve.tensor_copy(modA[:, :], mods[:, bass.ds(bb, 1), 0:8].rearrange("p a n -> p (a n)")))
                for name, g in (("so", 0), ("co", 1)):
                    go(dve.tensor_tensor(row("tmp"), row(name), Gall[0:1, bass.ds(bb * 3 + g, 1), :].rearrange("p a c -> p (a c)"), ALU.mult))
                    n[0] += three_parts(row("tmp"), bias3[name], stepA, b * STEPS_A + n[0])
                assert n[0] == STEPS_A, n[0]
                dve.wait_ge(fullA, b * 3 + 1)
                dve.tensor_copy(ctxT[:, :, :].rearrange("p k c -> p (k c)"), psum[0][:, 0:CB * LC]).then_inc(readA, 1)
                dve.wait_ge(fullA, b * 3 + 2)
                for f in range(CB):
                    for e, m in enumerate((maskE, maskO)):
                        c = COLS["kv"] + f
                        i = dve.tensor_scalar(kc[e][:, f, :], psum[1][:, f * LC:(f + 1) * LC], cols[:, c:c + 1], m[:, 0:1],
                                              ALU.add, ALU.mult)
                i.then_inc(readA, 1)
                dve.wait_ge(fullA, b * 3 + 3)
                dve.tensor_copy(vc[:, :, 0:D], psum[2][0:LC, 0:C].rearrange("p (h d) -> p h d", h=H)).then_inc(readA, 1)
                dve.tensor_copy(M2[:, 0, 0:1], modA[:, 0:1]).then_inc(doneA, 1)

            def prep_b(b):
                n = [0]

                def go(i):
                    n[0] += 1
                    i.then_inc(stepB, 1)
                    dve.wait_ge(stepB, b * STEPS_B + n[0])

                go(dve.tensor_copy(modB[:, :], mods[:, bass.ds(b, 1), 8:12].rearrange("p a n -> p (a n)")))
                go(dve.tensor_copy(betaF[:, :], betas[:, bass.ds(b, 1), :].rearrange("p a n -> p (a n)")))
                go(dve.tensor_scalar(betaH[:, :], betaF[:, :], 0.5, None, ALU.mult))
                go(dve.tensor_copy(rbias[:, :], rbias_all[:, bass.ds(b, 1), :].rearrange("p a n -> p (a n)")))
                go(dve.tensor_tensor(row("tmp"), row("m2"), Gall[0:1, bass.ds(b * 3 + 2, 1), :].rearrange("p a c -> p (a c)"), ALU.mult))
                n[0] += three_parts(row("tmp"), bias3["mo"], stepB, b * STEPS_B + n[0])
                assert n[0] == STEPS_B, n[0]
                dve.wait_ge(fullB, b * 6 + 1)
                dve.tensor_copy(vT1[:, :, :].rearrange("p k c -> p (k c)"), psum[5][:, 0:CB * LC]).then_inc(readB, 1)
                dve.wait_ge(fullB, b * 6 + 2)
                dve.tensor_copy(Gp[:, :, :].rearrange("p k c -> p (k c)"), psum[6][:, 0:CB * LC]).then_inc(readB, 1)
                for k in range(4):
                    dve.wait_ge(fullB, b * 6 + 3 + k)
                    c0, c1 = k * 512, min((k + 1) * 512, W1N + E)
                    dve.tensor_copy(Vp[:, c0:c1], psum[(7, 5, 6, 7)[k]][0:LC, 0:c1 - c0]).then_inc(readB, 1)
                dve.tensor_copy(M2[:, 1, 0:1], modB[:, 0:1]).then_inc(doneB, 1)

            def ln_stats(i, src, u):
                for t in range(TILES):
                    dve.bn_stats(stat[i][:, t, :], src[:, t, :]).then_inc(stats[i], 1)
                dve.wait_ge(stats[i], u * 4 + 2)
                alone(dve)
                for t in range(TILES):
                    dve.bn_aggr(mv[i][:, t, :], stat[i][:, t, :]).then_inc(stats[i], 1)

            def ln_apply(i, src, dst, u):
                dve.wait_ge(rstds[i], u * 2 + 2)
                dve.wait_ge(stats[i], u * 4 + 4)
                for t in range(TILES):
                    dve.tensor_scalar(dst[:, t, :], src[:, t, :], mv[i][:, t, 0:1], rstd[i][:, t:t + 1], ALU.subtract, ALU.mult)\
                       .then_inc(normed[i], 1)

            def a_copy_values(u):
                wait_full(dve, "v", u)
                dve.tensor_copy(va[:, :, :, 0:D], bank_of("v")[:, :].rearrange("p (t h d) -> p t h d", t=TILES, h=H))\
                   .then_inc(drained[JOB["v"][0]], 1)

            def a_bias_queries(u):
                wait_full(dve, "q", u)
                for f in range(CB):
                    c = COLS["qkv"] + f
                    i = dve.tensor_scalar(qT[:, f, :], bank_of("q")[:, f * UT:(f + 1) * UT], cols[:, c:c + 1], None, ALU.add)
                i.then_inc(drained[JOB["q"][0]], 1)

            def slot_scores(s):
                return psum[s][:, :].rearrange("p (i k) -> p i k", i=HPS)

            def a_max(t, s, u):
                wait_full(dve, f"s{t}{s}", u)
                dve.tensor_reduce(rmax[:, t, s * HPS:(s + 1) * HPS], slot_scores(s), AX.X, ALU.max).then_inc(row_max, 1)

            def a_subtract(t, s, u):
                dve.wait_ge(row_max, u * (TILES * SLOTS) + (t * SLOTS + s + 1))
                dve.tensor_tensor(prob[:, s], slot_scores(s), rmax[:, t, s * HPS:(s + 1) * HPS].rearrange("p (i a) -> p i a", a=1)
                                  .to_broadcast([P, HPS, P]), ALU.subtract).then_inc(drained[s], 1)

            def a_softmax(t, slots, u):
                for n, s in enumerate(slots):
                    a_max(t, s, u)
                    if n:
                        a_subtract(t, slots[n - 1], u)
                a_subtract(t, slots[-1], u)

            def a_normalise(n, name, dst, t, u):
                wait_full(dve, name, u)
                v = psum[4][:, 0:H * DV].rearrange("p (h d) -> p h d", h=H)
                dve.reciprocal(rsum[:, t, :], v[:, :, D]).then_inc(sums_inverted, 1)
                dve.wait_ge(sums_inverted, u * 4 + n + 1)
                dve.tensor_tensor(dst[:, t, :].rearrange("p (h d) -> p h d", h=H), v[:, :, 0:D],
                                  rsum[:, t, :].rearrange("p (h a) -> p h a", a=1).to_broadcast([P, H, D]), ALU.mult)\
                   .then_inc(drained[4], 1)

            def a_residual(dst, src, name, u):
                wait_full(dve, name, u)
                dve.tensor_tensor(dst[:, :, :].rearrange("p t c -> p (t c)"), src[:, :, :].rearrange("p t c -> p (t c)"),
                                  bank_of(name)[:, :], ALU.add).then_inc(drained[JOB[name][0]], 1)

            def a_topk(t, s, u, steps=(0, 1, 2, 3)):
                if 0 in steps:
                    wait_drained(dve, f"c{t}{s}", u)
                base = u * TOPK_PER_UNIT + topk_base(t, s)
                if 0 in steps:
                    alone(dve)

                def phase(n, one):
                    if n not in steps:
                        return
                    for i in range(HPS):
                        if n and i % 2 == 0:
                            dve.wait_ge(topk, base + ((n - 1) * HPS + i + 2))
                            alone(dve)
                        one(s * HPS + i).then_inc(topk, 1)

                phase(0, lambda h: dve.max(M1[:, t, h, :], S[:, t, h, :]))
                phase(1, lambda h: dve.match_replace(K[:, h, :], M1[:, t, h, :], S[:, t, h, :], KNOCKED))
                phase(2, lambda h: dve.max(M2[:, h, :], K[:, h, :]))
                phase(3, lambda h: dve.match_replace(K[:, h, :], M2[:, h, :], K[:, h, :], KNOCKED))

            def a_pick(t, half, u):
                dve.wait_ge(cross_exp, u * (TILES * 2) + (2 * t + half + 1))
                dve.wait_ge(topk, u * TOPK_PER_UNIT + topk_base(t, 2 * half + 1) + 4 * HPS)
                g = slice(half * (H // 2), (half + 1) * (H // 2))
                dve.scalar_tensor_tensor(Dx[:, t, g].rearrange("p h c -> p (h c)"), K[:, g, :].rearrange("p h c -> p (h c)"), KNOCKED_BELOW,
                                         Dx[:, t, g].rearrange("p h c -> p (h c)"), ALU.is_lt, ALU.mult).then_inc(picked, 1)

            def b_swiglu(j, u):
                name = f"m{j}"
                w = tb_of(name)
                dve.wait_ge(tanh_done, u * len(TANH_ORDER) + (TANH_ORDER.index(name) + 1))
                dve.scalar_tensor_tensor(gT[:, j, :], tb[w][:, 0:UT], 1.0, gT[:, j, :], ALU.add, ALU.mult).then_inc(half_gated, 1)
                dve.wait_ge(half_gated, u * HJ + (j + 1))
                c = COLS["m1"] + HJ + j
                dve.scalar_tensor_tensor(gT[:, j, :], bank_of(name)[:, UT:2 * UT], cols[:, c:c + 1], gT[:, j, :], ALU.add, ALU.mult)\
                   .then_inc(drained[JOB[name][0]], 1)

            def b_silu(name, dst, d0, u):
                wait_drained(dve, name, u)
                o = dst[:, d0:d0 + 2, :].rearrange("p k t -> p (k t)")
                dve.scalar_tensor_tensor(o, tb[tb_of(name)][:, :], 1.0, o, ALU.add, ALU.mult).then_inc(gated, 1)

            def b_proto_shift(u):
                wait_full(dve, "ps", u)
                v = psum[7][:, 0:TILES * LC].rearrange("p (t c) -> p t c", t=TILES)
                dve.tensor_reduce(pm[:, :], v, AX.X, ALU.max).then_inc(proto_max, 1)
                dve.wait_ge(proto_max, u + 1)
                dve.tensor_tensor(pw[:, :, :], v, pm[:, :].rearrange("p (t a) -> p t a", a=1).to_broadcast([P, TILES, LC]),
                                  ALU.subtract).then_inc(drained[7], 1)

            def b_proto_norm(u):
                dve.wait_ge(proto_exp, u + 1)
                dve.tensor_reduce(psu[:, :], pw[:, :, :], AX.X, ALU.add).then_inc(proto_steps, 1)
                dve.wait_ge(proto_steps, u * 3 + 1)
                dve.reciprocal(psu[:, :], psu[:, :]).then_inc(proto_steps, 1)
                dve.wait_ge(proto_steps, u * 3 + 2)
                dve.tensor_tensor(pw[:, :, :], pw[:, :, :], psu[:, :].rearrange("p (t a) -> p t a", a=1).to_broadcast([P, TILES, LC]),
                                  ALU.mult).then_inc(proto_steps, 1)

            def b_route_shift(u):
                wait_full(dve, "rt", u)
                v = psum[7][:, 0:TILES * E].rearrange("p (t c) -> p t c", t=TILES)
                dve.tensor_tensor(rl[:, :, :], v, rbias[:, :].rearrange("p (a e) -> p a e", a=1).to_broadcast([P, TILES, E]), ALU.add)\
                   .then_inc(drained[7], 1)
                wait_drained(dve, "rt", u)
                dve.tensor_reduce(rm[:, :], rl[:, :, :], AX.X, ALU.max).then_inc(route_steps, 1)
                dve.wait_ge(route_steps, u * 5 + 1)
                dve.tensor_tensor(rl[:, :, :], rl[:, :, :], rm[:, :].rearrange("p (t a) -> p t a", a=1).to_broadcast([P, TILES, E]),
                                  ALU.subtract).then_inc(route_steps, 1)

            def b_route_norm(u):
                dve.wait_ge(route_exp, u + 1)
                dve.tensor_reduce(rs[:, :], rl[:, :, :], AX.X, ALU.add).then_inc(route_steps, 1)
                dve.wait_ge(route_steps, u * 5 + 3)
                dve.reciprocal(rs[:, :], rs[:, :]).then_inc(route_steps, 1)
                dve.wait_ge(route_steps, u * 5 + 4)
                dve.tensor_tensor(rp[:, :, :], rl[:, :, :], rs[:, :].rearrange("p (t a) -> p t a", a=1).to_broadcast([P, TILES, E]),
                                  ALU.mult).then_inc(route_steps, 1)

            def b_mix(e, u):
                wait_full(dve, f"e{e}", u)
                if e == 0:
                    dve.wait_ge(route_steps, u * 5 + 5)
                    dve.wait_ge(y_stored, u * 48 + 16)
                else:
                    wait_drained(dve, f"e{e - 1}", u)
                for t in range(TILES):
                    o, v = acc[:, t, :], psum[7][:, t * C:(t + 1) * C]
                    if e == 0:
                        i = dve.tensor_scalar(o, v, rp[:, t, 0:1], None, ALU.mult)
                    else:
                        i = dve.scalar_tensor_tensor(o, v, rp[:, t, e:e + 1], o, ALU.mult, ALU.add)
                i.then_inc(drained[7], 1)

            def b_finish(u):
                wait_drained(dve, "g2", u)
                flat = lambda a: a[:, :, :].rearrange("p t c -> p (t c)")
                dve.scalar_tensor_tensor(flat(acc), tg[:, :], 1.0, flat(acc), ALU.add, ALU.mult).then_inc(mixed, 1)
                dve.wait_ge(mixed, u + 2)
                dve.tensor_tensor(flat(acc), flat(x2), flat(acc), ALU.add).then_inc(y_ready, 1)

            def a_load(u):
                dve.wait_ge(x_loaded, u * 48 + 48)

            def a_norm_input(u):
                a_load(u)
                ln_stats(0, xin, u)

            def stage_a(u):
                a_norm_input(u)
                ln_apply(0, xin, xnA, u)
                a_bias_queries(u)
                a_copy_values(u)
                a_softmax(0, range(SLOTS), u)
                a_softmax(1, range(SLOTS), u)
                a_normalise(0, "pv0", on, 0, u)
                a_normalise(1, "pv1", on, 1, u)
                a_residual(x1, xin, "so", u)
                wait_drained(dve, "so", u)
                ln_stats(1, x1, u)
                ln_apply(1, x1, xnA, u)
                for s in range(SLOTS):
                    a_topk(0, s, u)
                a_pick(0, 0, u)
                a_topk(1, 0, u)
                a_topk(1, 1, u)
                a_pick(0, 1, u)
                a_norm_input(u + 1)
                a_topk(1, 2, u)
                wait_full(dve, "ln2", u)
                ln_apply(0, xin, xnA, u + 1)
                a_topk(1, 3, u)
                a_pick(1, 0, u)
                a_pick(1, 1, u)
                a_normalise(2, "xv0", on2, 0, u)
                a_normalise(3, "xv1", on2, 1, u)
                a_residual(x2, x1, "co", u)
                wait_drained(dve, "co", u)

            def both(ua, ub):
                ln_stats(2, x2, ub)
                a_bias_queries(ua)
                ln_apply(2, x2, xnB, ub)
                a_copy_values(ua)
                a_softmax(0, range(SLOTS), ua)
                b_swiglu(0, ub)
                b_swiglu(1, ub)
                a_softmax(1, (0, 1), ua)
                b_swiglu(2, ub)
                a_softmax(1, (2, 3), ua)
                b_swiglu(3, ub)
                b_swiglu(4, ub)
                a_normalise(0, "pv0", on, 0, ua)
                b_swiglu(5, ub)
                a_normalise(1, "pv1", on, 1, ua)
                a_residual(x1, xin, "so", ua)
                wait_drained(dve, "so", ua)
                ln_stats(1, x1, ua)
                b_swiglu(6, ub)
                ln_apply(1, x1, xnA, ua)
                b_swiglu(7, ub)
                a_residual(x2, x2, "mo", ub)
                wait_drained(dve, "mo", ub)
                ln_stats(3, x2, ub)
                a_topk(0, 0, ua, (0, 1))
                ln_apply(3, x2, xnB, ub)
                a_topk(0, 0, ua, (2, 3))
                a_topk(0, 1, ua, (0, 1))
                b_proto_shift(ub)
                a_topk(0, 1, ua, (2, 3))
                b_proto_norm(ub)
                a_topk(0, 2, ua)
                b_route_shift(ub)
                a_topk(0, 3, ua, (0, 1))
                b_route_norm(ub)
                a_topk(0, 3, ua, (2, 3))
                b_silu("h00", hE[:, 0], 0, ub)
                a_pick(0, 0, ua)
                b_silu("h01", hE[:, 0], 2, ub)
                a_pick(0, 1, ua)
                a_topk(1, 0, ua)
                a_topk(1, 1, ua)
                b_silu("h10", hE[:, 1], 0, ub)
                b_mix(0, ub)
                a_norm_input(ua + 1)
                b_silu("h11", hE[:, 1], 2, ub)
                a_topk(1, 2, ua)
                wait_full(dve, "ln2", ua)
                ln_apply(0, xin, xnA, ua + 1)
                a_topk(1, 3, ua)
                b_silu("h20", hE[:, 0], 0, ub)
                a_pick(1, 0, ua)
                a_pick(1, 1, ua)
                a_normalise(2, "xv0", on2, 0, ua)
                b_mix(1, ub)
                b_silu("h21", hE[:, 0], 2, ub)
                b_silu("hg", gs, 0, ub)
                b_mix(2, ub)
                a_normalise(3, "xv1", on2, 1, ua)
                b_finish(ub)
                dve.wait_ge(y_ready, ub + 1)
                a_residual(x2, x1, "co", ua)
                wait_drained(dve, "co", ua)

            prep_weights()
            prep_a(0)
            stage_a(0)
            with dve.Fori(0, NB) as b:
                prep_b(b)
                with dve.Fori(0, UNITS - 1) as r:
                    u = b * UNITS + r
                    both(u + 1, u)
                prep_a(b + 1)
                both(b * UNITS + UNITS, b * UNITS + (UNITS - 1))



_INS = ["x", "cond_1024", "ctx_1024"] + \
       ["L0_xcond_" + n for n in ("w_ada", "b_ada", "w_qkv", "b_qkv", "w_so", "b_so", "w_q", "b_q", "w_kv", "b_kv", "w_co", "b_co",
                                  "w_m1", "b_m1", "w_m2", "b_m2")] + \
       ["L1_xcond_" + n for n in ("ln_gamma", "ln_beta", "Wq", "Wk", "Wv", "router_W", "router_b", "e_w1", "e_b1", "e_w2", "e_b2",
                                  "gate_w1", "gate_b1", "gate_w2", "gate_b2", "out_w", "out_b")]
_OUT = (NB, L, C)


def kernel(**inputs):
    import numpy as _np
    import concourse.bacc as _bacc
    from concourse import mybir as _mybir
    from concourse.bass_utils import run_bass_kernel_spmd as _run

    nc = _bacc.Bacc("TRN2", target_bir_lowering=False, num_devices=1)
    arrays, args = {}, []
    for name in _INS:
        a = _np.ascontiguousarray(inputs[name])
        arrays[f"in_{name}_dram"] = a
        args.append(nc.dram_tensor(f"in_{name}_dram", a.shape, _mybir.dt.from_np(a.dtype), kind="ExternalInput").ap())
    args.append(nc.dram_tensor("out_dram", _OUT, _mybir.dt.float32, kind="ExternalOutput").ap())
    bass_pixart_experts(nc, *args)
    r = _run(nc, [arrays], core_ids=[0])
    return r.results[0]["out_dram"]
```

```python
from contextlib import ExitStack

import concourse.bass as bass
from concourse import mybir

F32 = mybir.dt.float32
BF16 = mybir.dt.bfloat16
ALU = mybir.AluOpType
ACT = mybir.ActivationFunctionType
AX = mybir.AxisListType

P = 128
NB, L, C = 4, 1024, 256
CB = C // P
WIN, SHIFT = 128, 64
TILES = 2
UT = TILES * WIN
UNITS = L // UT
H, D = 16, 16
SLOTS, PAIR, PAR = 4, 2, 2
HPS = PAIR * PAR
LC = 77
DV = D + 1
HID = 1024
HJ = HID // P
E = 3
RH = 2 * C
RB = RH // P
W1N = E * RH + C
W1B = W1N // P
EPS0, EPS1 = 1e-6, 1e-5
KNOCKED = -3.0e38
KNOCKED_BELOW = -2.9e38

_slots = ["s0", "p0", "s1", "p1"]
_cross = ["c0", "c1", "y0", "y1"]
BANK_JOBS = [
    ["q"] + [f"{x}{0}" for x in _slots] + ["o1"] + [f"{x}{0}" for x in _cross] + ["o2"],
    [f"{x}{1}" for x in _slots] + ["so"] + [f"{x}{1}" for x in _cross] + ["co"],
    ["k"] + [f"{x}{2}" for x in _slots] + ["ln2"] + [f"{x}{2}" for x in _cross],
    ["ln1"] + [f"{x}{3}" for x in _slots] + ["q2"] + [f"{x}{3}" for x in _cross],
    ["v", "pv0", "pv1", "h10", "xv0", "xv1"],
    ["ln3", "m1", "m3", "m5", "m7", "h01", "h11", "h21"],
    ["m0", "m2", "m4", "m6", "ln4", "h00", "h20", "hg"],
    ["mo", "ps", "wt", "rt", "e0", "e1", "e2", "g2"],
]
JOB = {name: (bank, i + (len(jobs) if name == "h10" else 0), len(jobs))
       for bank, jobs in enumerate(BANK_JOBS) for i, name in enumerate(jobs)}

COLS = {}
_n = 0
for _name, _k in (("ada", 9 * CB), ("qkv", 3 * CB), ("q", CB), ("kv", 2 * CB), ("m1", 2 * HJ), ("gamma", CB),
                  ("beta", CB), ("e_b1", E * RB), ("gate_b1", CB), ("cond", NB * CB), ("e_b2", E * CB)):
    COLS[_name] = _n
    _n += _k
NCOL = _n

FIRST_ORDER = ["h00", "h01", "h10", "h11", "h20", "h21", "hg"]
TANH_ORDER = [f"m{j}" for j in range(HJ)] + FIRST_ORDER
TOPK_PER_UNIT = TILES * SLOTS * 4 * HPS

BIAS = ["so", "co", "mo", "e0", "e1", "e2", "g2"]
STEPS_A, STEPS_B = 2, 5


def topk_base(t, s):
    return (t * SLOTS + s) * 4 * HPS


def tb_of(name):
    return 1 - TANH_ORDER.index(name) % 2


def bass_pixart_experts(nc, x, cond, ctx_in, w_ada, b_ada, w_qkv, b_qkv, w_so, b_so, w_q, b_q, w_kv, b_kv,
                        w_co, b_co, w_m1, b_m1, w_m2, b_m2, gamma, beta, wq1, wk1, wv1, router_w, router_b,
                        e_w1, e_b1, e_w2, e_b2, gate_w1, gate_b1, gate_w2, gate_b2, out_w, out_b, out):
    x_rows = x.rearrange("b l c -> (b l) c")
    out_rows = out.rearrange("b l c -> (b l) c")
    ctx_rows = ctx_in.rearrange("b l c -> (b l) c")

    with ExitStack() as stack:
        def sb(name, shape, dt=F32):
            return stack.enter_context(nc.sbuf_tensor(name, shape, dt))

        def sem(name):
            return stack.enter_context(nc.semaphore(name))

        Wqkv = sb("Wqkv", [P, CB, 3 * C])
        Wso = sb("Wso", [P, CB, C])
        Wso_g = sb("Wso_g", [P, CB, C])
        Wq2 = sb("Wq2", [P, CB, C])
        Wkv = sb("Wkv", [P, CB, 2 * C])
        Wco = sb("Wco", [P, CB, C])
        Wco_g = sb("Wco_g", [P, CB, C])
        Wm1 = sb("Wm1", [P, CB, 2 * HID])
        Wm2_g = sb("Wm2_g", [P, HJ, C])
        W1nx = sb("W1nx", [P, CB, W1N])
        W1ev = sb("W1ev", [P, CB, W1N])
        Rw = sb("Rw", [P, 3 * CB, E])
        W2p = sb("W2p", [P, E * RB, C])
        Wg2 = sb("Wg2", [P, CB, C])
        MT = sb("MT", [P, CB, C])
        Wv1 = sb("Wv1", [P, CB, C])
        ident = sb("ident", [P, P])
        cols = sb("cols", [P, NCOL])
        b1half = sb("b1half", [P, HJ])
        Gall = sb("Gall", [P, NB * 3, C])
        mods = sb("mods", [P, NB, 12])
        betas = sb("betas", [P, NB, W1B])
        rbias_all = sb("rbias_all", [P, NB, E])
        maskE = sb("maskE", [P, 1])
        maskO = sb("maskO", [P, 1])
        kbias = sb("kbias", [P, PAR, CB])
        neghalf = sb("neghalf", [P, TILES])
        ones3 = sb("ones3", [96, P], BF16)
        bias3 = sb("bias3", [96, len(BIAS), C], BF16)
        choose = sb("choose", [96, NB, P], BF16)
        chooseA = sb("chooseA", [96, P], BF16)
        chooseB = sb("chooseB", [96, P], BF16)

        modS = sb("modS", [P, 4])
        modC = sb("modC", [P, 4])
        modB = sb("modB", [P, 4])
        ctx_sb = sb("ctx_sb", [LC, C])
        ctxT = sb("ctxT", [P, CB, LC])
        kc = sb("kc", [P, PAR, CB, LC])
        vc = sb("vc", [LC, H, DV])
        vT1 = sb("vT1", [P, CB, LC])
        GpR = sb("GpR", [P, CB, LC + E])
        Vp = sb("Vp", [LC, W1N + E])
        betaF = sb("betaF", [P, W1B])
        betaH = sb("betaH", [P, W1B])
        rbias = sb("rbias", [P, E])

        xin = sb("xin", [P, TILES, C])
        x1 = sb("x1", [P, TILES, C])
        x2 = sb("x2", [P, TILES, C])
        xnA = sb("xnA", [P, TILES, C])
        xnB = sb("xnB", [P, TILES, C])
        stat = [sb(f"stat{i}", [P, TILES, 6]) for i in range(4)]
        mv = [sb(f"mv{i}", [P, TILES, 2]) for i in range(4)]
        vare = [sb(f"vare{i}", [P, TILES]) for i in range(4)]
        rstd = [sb(f"rstd{i}", [P, TILES]) for i in range(4)]
        hA = sb("hA", [P, CB, UT])
        qT = sb("qT", [P, CB, UT])
        keys_or_knocked = sb("keys_or_knocked", [P, H * LC])
        km = keys_or_knocked[:, 0:PAR * CB * UT].rearrange("p (e f t) -> p e f t", e=PAR, f=CB)
        K = keys_or_knocked[:, 0:H * LC].rearrange("p (h c) -> p h c", h=H)
        va = sb("va", [P, TILES, H, DV])
        rmax = sb("rmax", [P, TILES, H])
        prob_or_scores = sb("prob_or_scores", [P, TILES * H * LC])
        prob = prob_or_scores[:, 0:H * P].rearrange("p (s i k) -> p s i k", s=SLOTS, i=HPS)
        S = prob_or_scores[:, :].rearrange("p (t h c) -> p t h c", t=TILES, h=H)
        probT = sb("probT", [P, SLOTS, HPS, P])
        rsum = sb("rsum", [P, TILES, H])
        on, oT, q2T = xnA, hA, qT
        on2 = prob_or_scores[:, 0:TILES * C].rearrange("p (t c) -> p t c", t=TILES)
        oT2 = km[:, 0]
        Dx = sb("Dx", [P, TILES, H, LC])
        M1 = sb("M1", [P, TILES, H, 8])
        M2 = sb("M2", [P, H, 8])

        hB = sb("hB", [P, CB, UT])
        nxT = hB
        tb = [sb(f"tb{i}", [P, 2 * UT]) for i in range(2)]
        gT = sb("gT", [P, HJ, UT])
        hE = gT[:, :, :].rearrange("p (a k) t -> p a k t", a=2)
        pw = sb("pw", [P, TILES, LC])
        pm = sb("pm", [P, TILES])
        psu = sb("psu", [P, TILES])
        wT = sb("wT", [LC, UT])
        rl = sb("rl", [P, TILES, E])
        rn = sb("rn", [P, TILES, E])
        rm = sb("rm", [P, TILES])
        rs = sb("rs", [P, TILES])
        rp = sb("rp", [P, TILES, E])
        gs = xnB
        acc = sb("acc", [P, TILES, C])
        tg = tb[0]

        colrows = tb[1][0:NCOL, 0:P]
        Wada = [r[:, 0:9 * C] for r in (Dx[:, :, :, :].rearrange("p t h c -> p (t h c)"), prob_or_scores[:, :])]
        wk_sb, wq_sb, outw, wkT = [Wm2_g[:, 2 * i:2 * i + 2, :] for i in range(4)]
        wqT = hB
        ew2 = gT
        e2T = [b[:, :, :].rearrange("p t c -> p (t c)") for b in (xnB, acc)]
        W1an = W1ev
        ada = sb("ada", [NB, 9, C])
        rows = Vp[0:NB, 0:len(BIAS) * C].rearrange("b (n c) -> b n c", n=len(BIAS))
        out_row = sb("out_row", [1, C])
        split = sb("split", [NB, 4, C])
        split_b = sb("split_b", [NB, 4, C], BF16)
        onehot = sb("onehot", [NB, NB, P])
        chosen = sb("chosen", [96, NB])
        condT = sb("condT", [P, CB, NB])
        bv4 = sb("bv4", [P, 2, CB, NB])
        siluT = sb("siluT", [P, CB, NB])
        tanhT = sb("tanhT", [P, CB, NB])

        psum = [stack.enter_context(nc.psum_tensor(f"bank{i}", [P, 512], F32)) for i in range(8)]

        full = [sem(f"full{i}") for i in range(8)]
        drained = [sem(f"drained{i}") for i in range(8)]
        x_loaded, y_ready, y_stored = sem("x_loaded"), sem("y_ready"), sem("y_stored")
        stats = [sem(f"ln_stats{i}") for i in range(4)]
        rstds = [sem(f"ln_rstd{i}") for i in range(4)]
        normed = [sem(f"normed{i}") for i in range(4)]
        row_max, probs = sem("row_max"), sem("probs")
        sums_inverted = sem("sums_inverted")
        topk, shifted, cross_exp, picked = sem("topk"), sem("shifted"), sem("cross_exp"), sem("picked")
        tanh_done, half_gated, gated = sem("tanh_done"), sem("half_gated"), sem("gated")
        proto_max, proto_exp, proto_steps = sem("proto_max"), sem("proto_exp"), sem("proto_steps")
        route_nx, route_steps, route_exp = sem("route_nx"), sem("route_steps"), sem("route_exp")
        mixed, gate_tanh = sem("mixed"), sem("gate_tanh")
        wm2_loaded, ctx_loaded = sem("wm2_loaded"), sem("ctx_loaded")
        cols_loaded, ada_loaded, rows_loaded, wa_loaded = sem("cols_loaded"), sem("ada_loaded"), sem("rows_loaded"), sem("wa_loaded")
        folded_loaded, anchor_loaded, ew2_loaded, wb_loaded = sem("folded_loaded"), sem("anchor_loaded"), sem("ew2_loaded"), sem("wb_loaded")
        consts, dve_step, init_full, init_read, init_tanh = sem("consts"), sem("dve_step"), sem("init_full"), sem("init_read"), sem("init_tanh")
        silu_ready, helpers_ready, prepared, prepared_b = sem("silu_ready"), sem("helpers_ready"), sem("prepared"), sem("prepared_b")
        fold_full, fold_read = sem("fold_full"), sem("fold_read")
        fullA, readA, doneA, gatedA = sem("prepA_full"), sem("prepA_read"), sem("prepA_done"), sem("gatedA")
        fullB, readB, doneB, gatedB = sem("prepB_full"), sem("prepB_read"), sem("prepB_done"), sem("gatedB")
        mod_ready = sem("mod_ready")
        q_half, ln2_half, q2_half, ln4_half = sem("q_half"), sem("ln2_half"), sem("q2_half"), sem("ln4_half")
        stepA, stepB = sem("prepA_step"), sem("prepB_step")

        passed = sem("passed")
        rrow = sb("rrow", [NB, E])

        def wait_full(eng, name, u):
            bank, i, n = JOB[name]
            eng.wait_ge(full[bank], u * n + (i + 1))

        def wait_drained(eng, name, u):
            bank, i, n = JOB[name]
            eng.wait_ge(drained[bank], u * n + (i + 2))

        def wait_free(eng, name, u):
            bank, i, n = JOB[name]
            eng.wait_ge(drained[bank], u * n + (i + 1))

        def alone(eng):
            eng.sem_inc(passed, 1)

        def bank_of(name):
            return psum[JOB[name][0]]

        HEADS = [(s, j, e) for s in range(SLOTS) for j in range(PAIR) for e in range(PAR)]

        def head(s, i):
            return 8 * (i // PAR) + 2 * s + i % PAR

        col_loads = [("ada", b_ada, 9 * CB), ("qkv", b_qkv, 3 * CB), ("q", b_q, CB), ("kv", b_kv, 2 * CB), ("m1", b_m1, 2 * HJ),
                     ("gamma", gamma, CB), ("beta", beta, CB), ("e_b1", e_b1.rearrange("e r -> (e r)"), E * RB),
                     ("gate_b1", gate_b1, CB), ("cond", cond.rearrange("b c -> (b c)"), NB * CB),
                     ("e_b2", e_b2.rearrange("e c -> (e c)"), E * CB)]

        def blocks(w):
            return w.rearrange("(k p) n -> p k n", p=P)

        def rank1(v):
            return v.rearrange("(a n) -> a n", a=1)

        ew1 = [e_w1[e].rearrange("(k p) n -> p k n", p=P) for e in range(E)]
        gw1 = blocks(gate_w1)

        def part_loads(dst, part):
            k = slice(part * CB, (part + 1) * CB)
            return [(dst[:, :, e * RH:(e + 1) * RH], ew1[e][:, k, :]) for e in range(E)] + \
                   [(dst[:, :, E * RH:W1N], gw1[:, k, :])]

        cols_loads = [(colrows[COLS[n]:COLS[n] + k, :], v.rearrange("(k p) -> k p", p=P)) for n, v, k in col_loads]
        ada_loads = [(Wada[k], w_ada[k * P:(k + 1) * P, :]) for k in range(CB)]

        def every_batch(dst, v):
            return dst, rank1(v).to_broadcast([NB, v.shape[0]])

        rows_loads = [every_batch(ada[:, :, :].rearrange("b s c -> b (s c)"), b_ada)] + \
                     [every_batch(rows[:, i, :], v) for i, v in enumerate((b_so, b_co, b_m2))]
        wa_loads = [(Wso[:, :, :], blocks(w_so)), (Wco[:, :, :], blocks(w_co)), (Wqkv[:, :, :], blocks(w_qkv)),
                    (Wkv[:, :, :], blocks(w_kv)), (Wq2[:, :, :], blocks(w_q))]
        folded_loads = [every_batch(rrow[:, :], router_b), (out_row[:, :], rank1(out_b)), (rows[0:1, BIAS.index("g2"), :], rank1(gate_b2)),
                        (Rw[:, :, :], blocks(router_w)), (outw, blocks(out_w)), (wk_sb, blocks(wk1)), (wq_sb, blocks(wq1))]
        anchor_loads = part_loads(W1an, 2)
        wb_loads = [(Wm1[:, :, :], blocks(w_m1)), (Wg2[:, :, :], blocks(gate_w2)), (Wv1[:, :, :], blocks(wv1))] + part_loads(W1nx, 0)
        evidence_loads = part_loads(W1ev, 1)
        e2_rows = e_w2.rearrange("e (k p) n -> p (e k) n", p=P)

        FOLD_JOBS = ["wk", "wq", "MT"] + [f"{x}{e}{i}" for e in range(E) for x in "tp" for i in range(CB)] + \
                    ["b01", "b2", "G1", "G2", "G3", "r0", "r1", "M0", "M1", "anchor"]
        assert RB // 2 == CB

        block = stack.enter_context(nc.Block())

        @block.sync
        def _(sp):
            for s in (*drained, mixed):
                sp.sem_inc(s, 1)
            sp.sem_inc(y_stored, 16)
            for loads, loaded in ((cols_loads, cols_loaded), (ada_loads, ada_loaded)):
                for dst, src in loads:
                    sp.dma_start(dst, src).then_inc(loaded, 16)

            def spans(u):
                at = ((u >> 2) & 3) * L
                uu = u & 3
                first = at + uu * UT + SHIFT
                return first, first + WIN, at + ((uu + 1) & 3) * UT

            def load_x(u):
                r0, r1, r2 = spans(u)
                sp.dma_start(xin[:, 0, :], x_rows[bass.ds(r0, WIN), :]).then_inc(x_loaded, 16)
                sp.dma_start(xin[0:SHIFT, 1, :], x_rows[bass.ds(r1, SHIFT), :]).then_inc(x_loaded, 16)
                sp.dma_start(xin[SHIFT:WIN, 1, :], x_rows[bass.ds(r2, SHIFT), :]).then_inc(x_loaded, 16)

            def store_y(u):
                r0, r1, r2 = spans(u)
                sp.wait_ge(y_ready, u + 1)
                alone(sp)
                sp.dma_start(out_rows[bass.ds(r0, WIN), :], acc[:, 0, :]).then_inc(y_stored, 16)
                sp.dma_start(out_rows[bass.ds(r1, SHIFT), :], acc[0:SHIFT, 1, :]).then_inc(y_stored, 16)
                sp.dma_start(out_rows[bass.ds(r2, SHIFT), :], acc[SHIFT:WIN, 1, :]).then_inc(y_stored, 16)

            def load_wm2():
                sp.dma_start(Wm2_g[:, :, :], blocks(w_m2)).then_inc(wm2_loaded, 16)

            def load_ctx(b):
                sp.dma_start(ctx_sb[:, :], ctx_rows[bass.ds((b & 3) * LC, LC), :]).then_inc(ctx_loaded, 16)

            load_x(0)
            for loads, loaded in ((rows_loads, rows_loaded), (wa_loads, wa_loaded)):
                for dst, src in loads:
                    sp.dma_start(dst, src).then_inc(loaded, 16)
            load_ctx(0)
            for dst, src in folded_loads:
                sp.dma_start(dst, src).then_inc(folded_loaded, 16)
            sp.dma_start(ew2[:, :, :], e2_rows[:, 0:2 * RB, :]).then_inc(ew2_loaded, 16)
            for loads, loaded in ((anchor_loads, anchor_loaded), (wb_loads, wb_loaded)):
                for dst, src in loads:
                    sp.dma_start(dst, src).then_inc(loaded, 16)
            sp.wait_ge(fold_read, FOLD_JOBS.index("t01") + 1)
            sp.dma_start(ew2[:, 0:RB, :], e2_rows[:, 2 * RB:3 * RB, :]).then_inc(ew2_loaded, 16)
            wait_drained(sp, "so", 0)
            load_x(1)
            sp.wait_ge(fold_read, FOLD_JOBS.index("b2") + 1)
            load_wm2()
            sp.wait_ge(fold_read, FOLD_JOBS.index("anchor") + 1)
            for dst, src in evidence_loads:
                sp.dma_start(dst, src).then_inc(wb_loaded, 16)
            with sp.Fori(0, NB) as b:
                sp.wait_ge(fullA, b * 3 + 1)
                alone(sp)
                load_ctx(b + 1)
                with sp.Fori(0, UNITS - 1) as r:
                    u = b * UNITS + r
                    wait_drained(sp, "so", u + 1)
                    alone(sp)
                    load_x(u + 2)
                    store_y(u)
                u = b * UNITS + (UNITS - 1)
                wait_full(sp, "mo", u)
                alone(sp)
                load_wm2()
                wait_drained(sp, "so", u + 1)
                alone(sp)
                load_x(u + 2)
                store_y(u)
            sp.wait_ge(wm2_loaded, 16 * (NB + 1))
            sp.wait_ge(y_stored, 48 * NB * UNITS + 16)
            sp.wait_ge(x_loaded, 48 * (NB * UNITS + 2))
            sp.wait_ge(ctx_loaded, 16 * (NB + 1))

        @block.tensor
        def _(pe):
            def prep_weights():
                pe.wait_ge(consts, 9)
                pe.wait_ge(cols_loaded, 16 * len(cols_loads))
                pe.transpose(psum[0][:, 0:NCOL], colrows[:, :], ident[0:NCOL, 0:NCOL]).then_inc(init_full, 1)
                pe.wait_ge(silu_ready, 1)
                pe.wait_ge(ada_loaded, 16 * CB)
                for n in range(5):
                    c0, c1 = n * 2 * C, min((n + 1) * 2 * C, 9 * C)
                    for k in range(CB):
                        m = pe.matmul(psum[1 + n][0:NB, 0:c1 - c0], siluT[:, k, :], Wada[k][:, c0:c1], start=(k == 0), stop=(k == CB - 1))
                    m.then_inc(init_full, 1)
                pe.wait_ge(helpers_ready, 1)
                pe.wait_ge(wa_loaded, 16 * len(wa_loads))
                for n, w in enumerate((Wso, Wco)):
                    for k in range(CB):
                        m = pe.matmul(psum[6][0:NB, n * C:(n + 1) * C], bv4[:, n, k, :], w[:, k, :], start=(k == 0), stop=(k == CB - 1))
                m.then_inc(init_full, 1)
                pe.wait_ge(init_read, 6)
                for n, sec in enumerate((1, 0, 4, 3, 7, 6)):
                    for f in range(CB):
                        m = pe.transpose(psum[7][:, (n * CB + f) * NB:(n * CB + f + 1) * NB], ada[:, sec, f * P:(f + 1) * P], ident[0:NB, 0:NB])
                m.then_inc(init_full, 1)
                for g in range(2):
                    m = pe.matmul(psum[0][:, g * C:(g + 1) * C], onehot[:, 0, :], ada[:, 3 * g + 2, :], start=True, stop=True)
                m.then_inc(init_full, 1)

            def fold_bank(name):
                n = FOLD_JOBS.index(name)
                if n == 0:
                    pe.wait_ge(init_read, 9)
                if n >= 3:
                    pe.wait_ge(fold_read, n - 2)
                return psum[5 + n % 3]

            def fold_gates(b):
                bk = fold_bank(f"G{b}")
                for g in range(2):
                    m = pe.matmul(bk[:, g * C:(g + 1) * C], onehot[:, b, :], ada[:, 3 * g + 2, :], start=True, stop=True)
                m.then_inc(fold_full, 1)

            def fold_mlp_gates(n):
                bk = fold_bank(f"M{n}")
                for i in range(2):
                    m = pe.matmul(bk[:, i * C:(i + 1) * C], onehot[:, 2 * n + i, :], ada[:, 8, :], start=True, stop=True)
                m.then_inc(fold_full, 1)

            def fold_router():
                bk = fold_bank("r0")
                for k in range(CB):
                    m = pe.matmul(bk[0:NB, 0:E], condT[:, k, :], Rw[:, 2 * CB + k, :], start=(k == 0), stop=(k == CB - 1))
                m.then_inc(fold_full, 1)
                bk = fold_bank("r1")
                pe.wait_ge(fold_read, FOLD_JOBS.index("r0") + 1)
                for b in range(NB):
                    m = pe.matmul(bk[:, b * E:(b + 1) * E], onehot[:, b, :], rrow[:, :], start=True, stop=True)
                m.then_inc(fold_full, 1)

            def fold_expert_biases():
                for name, es in (("b01", (0, 1)), ("b2", (2,))):
                    bk = fold_bank(name)
                    for e in es:
                        for k in range(CB):
                            col = COLS["e_b2"] + e * CB + k
                            m = pe.matmul(bk[0:1, (e % 2) * C:(e % 2 + 1) * C], cols[:, col:col + 1], outw[:, k, :],
                                          start=(k == 0), stop=(k == CB - 1))
                    m.then_inc(fold_full, 1)

            def fold_turn_qk():
                pe.wait_ge(folded_loaded, 16 * len(folded_loads))
                for name, w in (("wk", wk_sb), ("wq", wq_sb)):
                    bk = fold_bank(name)
                    for k in range(CB):
                        for h in range(CB):
                            m = pe.transpose(bk[:, h * C + k * P:h * C + (k + 1) * P], w[:, k, h * P:(h + 1) * P], ident[:, :])
                    m.then_inc(fold_full, 1)

            def fold_qk():
                bk = fold_bank("MT")
                pe.wait_ge(fold_read, FOLD_JOBS.index("wq") + 1)
                for c in range(CB):
                    for h in range(CB):
                        m = pe.matmul(bk[:, c * C:(c + 1) * C], wkT[:, h, c * P:(c + 1) * P], wqT[:, h, :], start=(h == 0), stop=(h == CB - 1))
                m.then_inc(fold_full, 1)

            def fold_anchor():
                bk = fold_bank("anchor")
                pe.wait_ge(anchor_loaded, 16 * len(anchor_loads))
                for n in range(W1B):
                    for k in range(CB):
                        m = pe.matmul(bk[:, n * NB:(n + 1) * NB], W1an[:, k, n * P:(n + 1) * P], condT[:, k, :],
                                      start=(k == 0), stop=(k == CB - 1))
                m.then_inc(fold_full, 1)

            def fold_turn_second(e):
                pe.wait_ge(ew2_loaded, 16 if e < 2 else 32)
                src = e * RB if e < 2 else 0
                for h in range(CB):
                    bk = fold_bank(f"t{e}{h}")
                    for k in range(RB):
                        m = pe.transpose(bk[:, k * P:(k + 1) * P], ew2[:, src + k, h * P:(h + 1) * P], ident[:, :])
                    m.then_inc(fold_full, 1)

            def fold_second(e):
                pe.wait_ge(fold_read, FOLD_JOBS.index(f"t{e}1") + 1)
                for k2 in range(RB // 2):
                    bk = fold_bank(f"p{e}{k2}")
                    for k in (2 * k2, 2 * k2 + 1):
                        for h in range(CB):
                            m = pe.matmul(bk[:, (k % 2) * C:(k % 2 + 1) * C], e2T[h][:, k * P:(k + 1) * P], outw[:, h, :],
                                          start=(h == 0), stop=(h == CB - 1))
                    m.then_inc(fold_full, 1)

            def context_turned(b):
                pe.wait_ge(ctx_loaded, b * 16 + 16)
                for k in range(CB):
                    m = pe.transpose(psum[3][:, k * LC:(k + 1) * LC], ctx_sb[:, k * P:(k + 1) * P], ident[0:LC, 0:LC])
                m.then_inc(fullA, 1)

            def context_keys(b):
                pe.wait_ge(readA, b * 3 + 1)
                for f in range(CB):
                    for k in range(CB):
                        m = pe.matmul(psum[3][:, f * LC:(f + 1) * LC], Wkv[:, k, f * P:(f + 1) * P], ctxT[:, k, :],
                                      start=(k == 0), stop=(k == CB - 1))
                m.then_inc(fullA, 1)

            def context_values(b):
                pe.wait_ge(readA, b * 3 + 2)
                for k in range(CB):
                    m = pe.matmul(psum[3][0:LC, 0:C], ctxT[:, k, :], Wkv[:, k, C:2 * C], start=(k == 0), stop=(k == CB - 1))
                m.then_inc(fullA, 1)

            def prep_b_context(b):
                for h in range(CB):
                    for k in range(CB):
                        m = pe.matmul(psum[3][:, h * LC:(h + 1) * LC], Wv1[:, k, h * P:(h + 1) * P], ctxT[:, k, :],
                                      start=(k == 0), stop=(k == CB - 1))
                for c in range(CB):
                    for k in range(CB):
                        m = pe.matmul(psum[3][:, C + c * LC:C + (c + 1) * LC], MT[:, k, c * P:(c + 1) * P], ctxT[:, k, :],
                                      start=(k == 0), stop=(k == CB - 1))
                m.then_inc(fullB, 1)

            def prep_b_evidence(b, n):
                if n == 0:
                    pe.wait_ge(readB, b * 5 + 1)
                c0, c1 = n * 512, min((n + 1) * 512, W1N)
                bk = psum[(7, 6, 5, 3)[n]]
                for h in range(CB):
                    m = pe.matmul(bk[0:LC, 0:c1 - c0], vT1[:, h, :], W1ev[:, h, c0:c1], start=(h == 0), stop=(h == CB - 1))
                if n == 3:
                    for h in range(CB):
                        m = pe.matmul(bk[0:LC, c1 - c0:c1 - c0 + E], vT1[:, h, :], Rw[:, CB + h, :],
                                      start=(h == 0), stop=(h == CB - 1))
                m.then_inc(fullB, 1)

            def turn(name, src, u, sem_, per):
                wait_free(pe, name, u)
                bk = bank_of(name)
                for t in range(TILES):
                    pe.wait_ge(sem_, u * per + (t + 1))
                    for f in range(CB):
                        m = pe.transpose(bk[:, f * UT + t * P:f * UT + (t + 1) * P], src[:, t, f * P:(f + 1) * P], ident[:, :])
                m.then_inc(full[JOB[name][0]], 1)

            def feature_major(name, w, c0, src, u, half=None, whole=None):
                wait_free(pe, name, u)
                bk = bank_of(name)
                for f in range(CB):
                    for k in range(CB):
                        if half is not None and f == 0:
                            if k == 0:
                                pe.wait_ge(half, u + 1)
                            elif k == CB - 1:
                                wait_drained(pe, whole, u)
                        m = pe.matmul(bk[:, f * UT:(f + 1) * UT], w[:, k, c0 + f * P:c0 + (f + 1) * P], src[:, k, :],
                                      start=(k == 0), stop=(k == CB - 1))
                m.then_inc(full[JOB[name][0]], 1)

            def bias_first(name, which):
                i = BIAS.index(which)
                lhsT = ones3 if i >= 3 else chooseB if which == "mo" else chooseA
                pe.matmul(bank_of(name)[:, :], lhsT[:, :], bias3[:, i:i + 1, :].to_broadcast([96, TILES, C]),
                          start=True, stop=False, skip_group_check=True)

            def token_major(name, src, w, nk, last=True):
                bk = bank_of(name)
                for k in range(nk):
                    for t in range(TILES):
                        m = pe.matmul(bk[:, t * C:(t + 1) * C], src[:, k, t * P:(t + 1) * P], w[:, k, :],
                                      start=False, stop=(k == nk - 1), skip_group_check=True)
                m.then_inc(full[JOB[name][0]], 1)

            def a_turn_input(u):
                turn("ln1", xnA, u, normed[0], TILES)

            def a_k(u):
                wait_drained(pe, "ln1", u)
                feature_major("k", Wqkv, C, hA, u)

            def a_q(u):
                feature_major("q", Wqkv, 0, hA, u)

            def a_v(t, u):
                if t == 0:
                    wait_free(pe, "v", u)
                for k in range(CB):
                    m = pe.matmul(bank_of("v")[:, t * C:(t + 1) * C], hA[:, k, t * P:(t + 1) * P], Wqkv[:, k, 2 * C:3 * C],
                                  start=(k == 0), stop=(k == CB - 1))
                if t == TILES - 1:
                    m.then_inc(full[JOB["v"][0]], 1)

            def a_scores(t, slots, u):
                if t == 0 and 0 in slots:
                    wait_drained(pe, "k", u)
                    pe.wait_ge(q_half, u + 1)
                for s in slots:
                    wait_free(pe, f"s{t}{s}", u)
                for j in range(PAIR):
                    if t == 0 and 0 in slots and j == 1:
                        wait_drained(pe, "q", u)
                    for s in slots:
                        r, w = slice(32 * s, 32 * s + 32), slice(t * P, (t + 1) * P)
                        m = pe.matmul(psum[s][:, j * PAR * P:(j + 1) * PAR * P].rearrange("p (e k) -> p e k", e=PAR),
                                      qT[r, j, w], km[r, :, j, w], start=True, stop=True)
                        if j == PAIR - 1:
                            m.then_inc(full[s], 1)

            def a_turn_probs(t, s, u):
                pe.wait_ge(probs, u * (TILES * SLOTS) + (t * SLOTS + s + 1))
                wait_free(pe, f"p{t}{s}", u)
                for i in range(HPS):
                    m = pe.transpose(psum[s][:, i * P:(i + 1) * P], prob[:, s, i, :], ident[:, :])
                m.then_inc(full[s], 1)

            def a_values(t, s, u):
                if s == 0:
                    wait_free(pe, f"pv{t}", u)
                wait_drained(pe, f"p{t}{s}", u)
                for i in range(HPS):
                    h = head(s, i)
                    m = pe.matmul(psum[4][:, h * DV:(h + 1) * DV], probT[:, s, i, :], va[:, t, h, :], start=True, stop=True)
                if s == SLOTS - 1:
                    m.then_inc(full[4], 1)

            def a_turn_outputs(name, src, pv, u):
                wait_drained(pe, pv, u)
                wait_free(pe, name, u)
                bk = bank_of(name)
                for f in range(CB):
                    for t in range(TILES):
                        m = pe.transpose(bk[:, f * UT + t * P:f * UT + (t + 1) * P], src[:, t, f * P:(f + 1) * P], ident[:, :])
                m.then_inc(full[JOB[name][0]], 1)

            def a_project(turn_name, src, name, w, u):
                wait_free(pe, name, u)
                bias_first(name, name)
                wait_drained(pe, turn_name, u)
                token_major(name, src, w, CB)

            def a_turn_query(u):
                turn("ln2", xnA, u, normed[1], TILES)

            def a_query(u):
                feature_major("q2", Wq2, 0, hA, u, ln2_half, "ln2")

            def a_cross_scores(t, slots, u):
                if t == 0 and 0 in slots:
                    pe.wait_ge(q2_half, u + 1)
                for s in slots:
                    wait_free(pe, f"c{t}{s}", u)
                for j in range(PAIR):
                    if t == 0 and 0 in slots and j == 1:
                        wait_drained(pe, "q2", u)
                    for s in slots:
                        r = slice(32 * s, 32 * s + 32)
                        m = pe.matmul(psum[s][:, j * PAR * LC:(j + 1) * PAR * LC].rearrange("p (e k) -> p e k", e=PAR),
                                      q2T[r, j, t * P:(t + 1) * P], kc[r, :, j, :], start=True, stop=True)
                        if j == PAIR - 1:
                            m.then_inc(full[s], 1)

            def a_turn_picked(t, s, u):
                if s % 2 == 0:
                    pe.wait_ge(picked, u * (TILES * 2) + (2 * t + s // 2 + 1))
                wait_free(pe, f"y{t}{s}", u)
                for i in range(HPS):
                    m = pe.transpose(psum[s][0:LC, i * P:(i + 1) * P], Dx[:, t, s * HPS + i, :], ident[:, :])
                m.then_inc(full[s], 1)

            def a_cross_values(t, s, u):
                if s == 0:
                    wait_free(pe, f"xv{t}", u)
                wait_drained(pe, f"y{t}{s}", u)
                for i in range(HPS):
                    h = head(s, i)
                    m = pe.matmul(psum[4][:, h * DV:(h + 1) * DV], probT[0:LC, s, i, :], vc[:, h, :], start=True, stop=True)
                if s == SLOTS - 1:
                    m.then_inc(full[4], 1)

            def b_hidden(j, u):
                name = f"m{j}"
                if j == 0:
                    wait_drained(pe, "ln3", u)
                wait_free(pe, name, u)
                for half in range(2):
                    for k in range(CB):
                        c = half * HID + j * P
                        m = pe.matmul(bank_of(name)[:, half * UT:(half + 1) * UT], Wm1[:, k, c:c + P], hB[:, k, :],
                                      start=(k == 0), stop=(k == CB - 1))
                m.then_inc(full[JOB[name][0]], 1)

            def b_down(j, u):
                if j == 0:
                    wait_free(pe, "mo", u)
                    bias_first("mo", "mo")
                wait_drained(pe, f"m{j}", u)
                for t in range(TILES):
                    m = pe.matmul(psum[7][:, t * C:(t + 1) * C], gT[:, j, t * P:(t + 1) * P], Wm2_g[:, j, :],
                                  start=False, stop=(j == HJ - 1), skip_group_check=True)
                if j == HJ - 1:
                    m.then_inc(full[7], 1)

            def b_turn_normed(u):
                turn("ln4", xnB, u, normed[3], TILES)

            def b_proto_scores(u):
                pe.wait_ge(ln4_half, u + 1)
                wait_free(pe, "ps", u)
                for t in range(TILES):
                    for k in range(CB):
                        if t == 0 and k == CB - 1:
                            wait_drained(pe, "ln4", u)
                        m = pe.matmul(psum[7][:, t * (LC + E):(t + 1) * (LC + E)], nxT[:, k, t * P:(t + 1) * P], GpR[:, k, :],
                                      start=(k == 0), stop=(k == CB - 1))
                m.then_inc(full[7], 1)

            def b_turn_weights(u):
                pe.wait_ge(proto_steps, u * 3 + 3)
                wait_free(pe, "wt", u)
                for t in range(TILES):
                    m = pe.transpose(bank_of("wt")[0:LC, t * P:(t + 1) * P], pw[:, t, :], ident[:, :])
                m.then_inc(full[JOB["wt"][0]], 1)

            def b_router(u):
                wait_free(pe, "rt", u)
                for t in range(TILES):
                    m = pe.matmul(psum[7][:, t * E:(t + 1) * E], wT[:, t * P:(t + 1) * P], Vp[:, W1N:W1N + E], start=True, stop=True)
                m.then_inc(full[7], 1)

            def b_first_nx(name, c0, u):
                wait_free(pe, name, u)
                for n in range(2):
                    for k in range(CB):
                        pe.matmul(bank_of(name)[:, n * UT:(n + 1) * UT], W1nx[:, k, c0 + n * P:c0 + (n + 1) * P], nxT[:, k, :],
                                  start=(n == 0 and k == 0), stop=False, skip_group_check=True)

            def b_first_evidence(name, c0, u):
                if name == FIRST_ORDER[0]:
                    wait_drained(pe, "wt", u)
                for n in range(2):
                    m = pe.matmul(bank_of(name)[:, n * UT:(n + 1) * UT], Vp[:, c0 + n * P:c0 + (n + 1) * P], wT[:, :],
                                  start=False, stop=True, skip_group_check=True)
                m.then_inc(full[JOB[name][0]], 1)

            def b_first(name, c0, u):
                b_first_nx(name, c0, u)
                b_first_evidence(name, c0, u)

            def b_second(e, blocks_, u):
                name = f"e{e}"
                for k in blocks_:
                    if k == 0:
                        wait_free(pe, name, u)
                        bias_first(name, name)
                    if k % 2 == 0:
                        pe.wait_ge(gated, u * len(FIRST_ORDER) + (2 * e + k // 2 + 1))
                    for t in range(TILES):
                        m = pe.matmul(psum[7][:, t * C:(t + 1) * C], hE[:, e % 2, k, t * P:(t + 1) * P], W2p[:, e * RB + k, :],
                                      start=False, stop=(k == RB - 1), skip_group_check=True)
                    if k == RB - 1:
                        m.then_inc(full[7], 1)

            def b_gate(u):
                wait_free(pe, "g2", u)
                bias_first("g2", "g2")
                pe.wait_ge(gated, u * len(FIRST_ORDER) + len(FIRST_ORDER))
                token_major("g2", gs, Wg2, CB)

            def first_unit(u):
                pe.wait_ge(init_read, 9)
                a_turn_input(u)
                a_k(u)
                context_turned(0)
                a_q(u)
                context_keys(0)
                a_v(0, u)
                a_v(1, u)
                context_values(0)
                pe.wait_ge(readA, 3)
                for s in range(SLOTS):
                    a_scores(0, (s,), u)
                fold_turn_qk()
                for s in range(SLOTS):
                    a_turn_probs(0, s, u)
                fold_qk()
                for s in range(SLOTS):
                    a_scores(1, (s,), u)
                fold_turn_second(0)
                a_values(0, 0, u)
                a_values(0, 1, u)
                fold_second(0)
                a_values(0, 2, u)
                a_values(0, 3, u)
                fold_turn_second(1)
                for s in range(SLOTS):
                    a_turn_probs(1, s, u)
                fold_second(1)
                a_values(1, 0, u)
                a_values(1, 1, u)
                fold_turn_second(2)
                a_values(1, 2, u)
                a_values(1, 3, u)
                fold_second(2)
                a_turn_outputs("o1", on, "pv1", u)
                fold_expert_biases()
                pe.wait_ge(prepared, 1)
                pe.wait_ge(gatedA, 4)
                a_project("o1", oT, "so", Wso_g, u)
                for b in range(1, NB):
                    fold_gates(b)
                a_turn_query(u)
                fold_router()
                a_query(u)
                for n in range(2):
                    fold_mlp_gates(n)
                a_cross_scores(0, range(SLOTS), u)
                a_cross_scores(1, range(SLOTS), u)
                fold_anchor()
                for t in range(TILES):
                    for s in range(SLOTS):
                        a_turn_picked(t, s, u)
                    for s in range(SLOTS):
                        a_cross_values(t, s, u)
                a_turn_input(u + 1)
                a_turn_outputs("o2", on2, "xv1", u)
                a_project("o2", oT2, "co", Wco_g, u)
                pe.wait_ge(wb_loaded, 16 * (len(wb_loads) + len(evidence_loads)))
                pe.wait_ge(prepared_b, 1)

            def both(ua, ub, first=None, last=None):
                a_k(ua)
                if first is not None:
                    for name in ("hg", "h21", "g2"):
                        wait_drained(pe, name, ub - 1)
                    alone(pe)
                    prep_b_context(first)
                if last is not None:
                    context_turned(last)
                a_q(ua)
                if first is not None:
                    prep_b_evidence(first, 0)
                    prep_b_evidence(first, 1)
                a_v(0, ua)
                if last is not None:
                    context_keys(last)
                if first is not None:
                    prep_b_evidence(first, 2)
                    prep_b_evidence(first, 3)
                a_scores(0, (0, 1), ua)
                if first is not None:
                    pe.wait_ge(readB, first * 5 + 5)
                turn("ln3", xnB, ub, normed[2], TILES)
                if last is not None:
                    context_values(last)
                a_v(1, ua)
                if last is not None:
                    pe.wait_ge(readA, last * 3 + 3)
                a_scores(0, (2, 3), ua)
                b_hidden(0, ub)
                a_turn_probs(0, 0, ua)
                a_turn_probs(0, 1, ua)
                b_hidden(1, ub)
                a_turn_probs(0, 2, ua)
                a_turn_probs(0, 3, ua)
                a_scores(1, (0,), ua)
                b_hidden(2, ub)
                a_scores(1, (1,), ua)
                if first is not None:
                    pe.wait_ge(gatedB, first * HJ + HJ)
                b_down(0, ub)
                a_scores(1, (2, 3), ua)
                b_down(1, ub)
                b_hidden(3, ub)
                a_values(0, 0, ua)
                a_values(0, 1, ua)
                b_hidden(4, ub)
                a_values(0, 2, ua)
                a_values(0, 3, ua)
                a_turn_probs(1, 0, ua)
                a_turn_probs(1, 1, ua)
                b_down(2, ub)
                a_turn_probs(1, 2, ua)
                a_turn_probs(1, 3, ua)
                a_values(1, 0, ua)
                a_values(1, 1, ua)
                b_hidden(5, ub)
                a_values(1, 2, ua)
                a_values(1, 3, ua)
                b_down(3, ub)
                a_turn_outputs("o1", on, "pv1", ua)
                b_down(4, ub)
                if last is not None:
                    pe.wait_ge(gatedA, last * 4 + 4)
                a_project("o1", oT, "so", Wso_g, ua)
                b_hidden(6, ub)
                b_down(5, ub)
                b_hidden(7, ub)
                a_turn_query(ua)
                b_down(6, ub)
                a_query(ua)
                b_down(7, ub)
                a_cross_scores(0, (0, 1), ua)
                a_cross_scores(0, (2, 3), ua)
                a_cross_scores(1, (0, 1), ua)
                b_turn_normed(ub)
                a_cross_scores(1, (2, 3), ua)
                b_proto_scores(ub)
                b_first_nx("h00", 0, ub)
                b_first_nx("h01", 2 * P, ub)
                b_turn_weights(ub)
                b_first_nx("h10", RH, ub)
                b_first_evidence("h00", 0, ub)
                b_router(ub)
                b_first_evidence("h01", 2 * P, ub)
                b_first_evidence("h10", RH, ub)
                b_second(0, (0, 1), ub)
                b_first("h11", RH + 2 * P, ub)
                b_second(0, (2, 3), ub)
                for s in range(SLOTS):
                    a_turn_picked(0, s, ua)
                b_first("h20", 2 * RH, ub)
                a_cross_values(0, 0, ua)
                a_cross_values(0, 1, ua)
                b_second(1, (0, 1), ub)
                a_cross_values(0, 2, ua)
                a_cross_values(0, 3, ua)
                b_second(1, (2, 3), ub)
                b_first("h21", 2 * RH + 2 * P, ub)
                for s in range(SLOTS):
                    a_turn_picked(1, s, ua)
                b_second(2, (0, 1), ub)
                a_cross_values(1, 0, ua)
                a_cross_values(1, 1, ua)
                b_first("hg", 3 * RH, ub)
                a_cross_values(1, 2, ua)
                a_cross_values(1, 3, ua)
                b_second(2, (2, 3), ub)
                a_turn_input(ua + 1)
                a_turn_outputs("o2", on2, "xv1", ua)
                b_gate(ub)
                a_project("o2", oT2, "co", Wco_g, ua)

            prep_weights()
            first_unit(0)
            with pe.Fori(0, NB) as b:
                both(b * UNITS + 1, b * UNITS, first=b)
                with pe.Fori(1, UNITS - 1) as r:
                    u = b * UNITS + r
                    both(u + 1, u)
                both(b * UNITS + UNITS, b * UNITS + (UNITS - 1), last=b + 1)

        @block.scalar
        def _(act):
            def copy_job(dst, name, u, view=None):
                wait_full(act, name, u)
                act.activation(dst, bank_of(name)[:, :] if view is None else view, ACT.Copy).then_inc(drained[JOB[name][0]], 1)

            def modulate(dst, name, u, scale, shift, half=None):
                wait_full(act, name, u)
                for f in range(CB):
                    i = act.activation(dst[:, f, :], bank_of(name)[:, f * UT:(f + 1) * UT], ACT.Identity,
                                       bias=shift(f), scale=scale(f))
                    if f == 0 and half is not None:
                        i.then_inc(half, 1)
                i.then_inc(drained[JOB[name][0]], 1)

            def add_bias(dst, name, u, c0, half):
                wait_full(act, name, u)
                for f in range(CB):
                    i = act.activation(dst[:, f, :], bank_of(name)[:, f * UT:(f + 1) * UT], ACT.Identity,
                                       bias=cols[:, c0 + f:c0 + f + 1])
                    if f == 0:
                        i.then_inc(half, 1)
                i.then_inc(drained[JOB[name][0]], 1)

            def a_modulate(name, mod, u):
                if name == "ln1":
                    act.wait_ge(mod_ready, u + 1)
                modulate(hA, name, u, lambda f: mod[:, f:f + 1], lambda f: mod[:, CB + f:CB + f + 1],
                         ln2_half if name == "ln2" else None)

            def a_keys(u):
                wait_full(act, "k", u)
                for e, m in enumerate((maskE, maskO)):
                    for f in range(CB):
                        i = act.activation(km[:, e, f, :], bank_of("k")[:, f * UT:(f + 1) * UT], ACT.Identity,
                                           bias=kbias[:, e, f:f + 1], scale=m[:, 0:1])
                i.then_inc(drained[JOB["k"][0]], 1)

            def a_copy_values(u):
                wait_full(act, "v", u)
                act.activation(va[:, :, :, 0:D], bank_of("v")[:, :].rearrange("p (t h d) -> p t h d", t=TILES, h=H), ACT.Copy)\
                   .then_inc(drained[JOB["v"][0]], 1)

            def a_exp(t, s, u):
                wait_drained(act, f"s{t}{s}", u)
                act.activation(prob[:, s], prob[:, s], ACT.Exp, scale=float(D) ** -0.5).then_inc(probs, 1)

            def a_copy_turned(t, s, u, kind, np_=P):
                name = f"{kind}{t}{s}"
                wait_full(act, name, u)
                act.activation(probT[0:np_, s], psum[s][0:np_, :].rearrange("p (i q) -> p i q", i=HPS), ACT.Copy)\
                   .then_inc(drained[s], 1)

            def a_copy_outputs(name, dst, u):
                copy_job(dst[:, :, :].rearrange("p f t -> p (f t)"), name, u)

            def a_copy_scores(t, s, u):
                wait_full(act, f"c{t}{s}", u)
                act.activation(S[:, t, s * HPS:(s + 1) * HPS, :], psum[s][:, 0:HPS * LC].rearrange("p (i c) -> p i c", i=HPS),
                               ACT.Copy).then_inc(drained[s], 1)

            def a_cross_exp(t, half, u):
                act.wait_ge(shifted, u * (TILES * SLOTS) + (2 * (2 * t + half) + 2))
                g = slice(half * (H // 2), (half + 1) * (H // 2))
                act.activation(Dx[:, t, g], Dx[:, t, g], ACT.Exp, scale=float(D) ** -0.5).then_inc(cross_exp, 1)

            def b_tanh_mlp(j, u):
                name = f"m{j}"
                if j == 0:
                    act.wait_ge(mixed, u + 1)
                wait_full(act, name, u)
                act.activation(tb[tb_of(name)][:, 0:UT], bank_of(name)[:, 0:UT], ACT.Tanh, bias=b1half[:, j:j + 1], scale=0.5)
                c = COLS["m1"] + j
                act.activation(gT[:, j, :], bank_of(name)[:, 0:UT], ACT.Identity, bias=cols[:, c:c + 1]).then_inc(tanh_done, 1)

            def b_tanh_first(name, dst, d0, n0, u):
                i = FIRST_ORDER.index(name)
                if i >= 2:
                    act.wait_ge(gated, u * len(FIRST_ORDER) + (i - 1))
                wait_full(act, name, u)
                for n in range(2):
                    act.activation(tb[tb_of(name)][:, n * UT:(n + 1) * UT], bank_of(name)[:, n * UT:(n + 1) * UT], ACT.Tanh,
                                   bias=betaH[:, n0 + n:n0 + n + 1], scale=0.5)
                for n in range(2):
                    o = dst[:, d0 + n, :]
                    if n == 0:
                        act.activation(o, bank_of(name)[:, 0:UT], ACT.Identity, bias=betaF[:, n0:n0 + 1]).then_inc(tanh_done, 1)
                    else:
                        act.activation(o, bank_of(name)[:, UT:2 * UT], ACT.Identity, bias=betaF[:, n0 + 1:n0 + 2])\
                           .then_inc(drained[JOB[name][0]], 1)

            def b_modulate(u):
                modulate(hB, "ln3", u, lambda f: modB[:, f:f + 1], lambda f: modB[:, CB + f:CB + f + 1])

            def b_affine(u):
                g, c = COLS["gamma"], COLS["beta"]
                modulate(nxT, "ln4", u, lambda f: cols[:, g + f:g + f + 1], lambda f: cols[:, c + f:c + f + 1], ln4_half)

            def b_proto_exp(u):
                wait_drained(act, "ps", u)
                act.activation(pw[:, :, :], pw[:, :, :], ACT.Exp, scale=float(C) ** -0.5).then_inc(proto_exp, 1)

            def b_copy_weights(u):
                wait_full(act, "wt", u)
                act.activation(wT[:, :], bank_of("wt")[0:LC, 0:UT], ACT.Copy).then_inc(drained[JOB["wt"][0]], 1)

            def b_route_exp(u):
                act.wait_ge(route_steps, u * 5 + 2)
                act.activation(rl[:, :, :], rl[:, :, :], ACT.Exp).then_inc(route_exp, 1)

            def b_gate_tanh(u):
                wait_full(act, "g2", u)
                act.activation(tg[:, :], psum[7][:, :], ACT.Tanh, scale=0.5).then_inc(drained[7], 1)

            def stage_a(u):
                a_modulate("ln1", modS, u)
                a_keys(u)
                a_copy_values(u)
                for s in range(SLOTS):
                    a_exp(0, s, u)
                for s in range(SLOTS):
                    a_copy_turned(0, s, u, "p")
                for s in range(SLOTS):
                    a_exp(1, s, u)
                for s in range(SLOTS):
                    a_copy_turned(1, s, u, "p")
                a_copy_outputs("o1", oT, u)
                a_modulate("ln2", modC, u)
                add_bias(q2T, "q2", u, COLS["q"], q2_half)
                for t in range(TILES):
                    for s in range(SLOTS):
                        a_copy_scores(t, s, u)
                for t in range(TILES):
                    a_cross_exp(t, 0, u)
                    a_cross_exp(t, 1, u)
                    for s in range(SLOTS):
                        a_copy_turned(t, s, u, "y", LC)
                a_copy_outputs("o2", oT2, u)

            def both(ua, ub, first=None, last=None):
                a_modulate("ln1", modS, ua)
                a_keys(ua)
                if first is not None:
                    act.wait_ge(doneB, first + 1)
                b_modulate(ub)
                a_exp(0, 0, ua)
                a_exp(0, 1, ua)
                a_copy_turned(0, 0, ua, "p")
                a_exp(0, 2, ua)
                b_tanh_mlp(0, ub)
                a_exp(0, 3, ua)
                a_copy_values(ua)
                a_copy_turned(0, 1, ua, "p")
                b_tanh_mlp(1, ub)
                a_copy_turned(0, 2, ua, "p")
                a_copy_turned(0, 3, ua, "p")
                b_tanh_mlp(2, ub)
                for s in range(SLOTS):
                    a_exp(1, s, ua)
                b_tanh_mlp(3, ub)
                b_tanh_mlp(4, ub)
                a_copy_turned(1, 0, ua, "p")
                a_copy_turned(1, 1, ua, "p")
                a_copy_turned(1, 2, ua, "p")
                a_copy_turned(1, 3, ua, "p")
                b_tanh_mlp(5, ub)
                a_copy_outputs("o1", oT, ua)
                b_tanh_mlp(6, ub)
                if last is not None:
                    act.wait_ge(doneA, last + 1)
                b_tanh_mlp(7, ub)
                a_modulate("ln2", modC, ua)
                add_bias(q2T, "q2", ua, COLS["q"], q2_half)
                for s in range(SLOTS):
                    a_copy_scores(0, s, ua)
                a_copy_scores(1, 0, ua)
                a_copy_scores(1, 1, ua)
                b_affine(ub)
                a_copy_scores(1, 2, ua)
                a_copy_scores(1, 3, ua)
                b_proto_exp(ub)
                b_copy_weights(ub)
                b_tanh_first("h00", hE[:, 0], 0, 0, ub)
                b_route_exp(ub)
                b_tanh_first("h01", hE[:, 0], 2, 2, ub)
                a_cross_exp(0, 0, ua)
                b_tanh_first("h10", hE[:, 1], 0, 4, ub)
                a_cross_exp(0, 1, ua)
                b_tanh_first("h11", hE[:, 1], 2, 6, ub)
                for s in range(SLOTS):
                    a_copy_turned(0, s, ua, "y", LC)
                b_tanh_first("h20", hE[:, 0], 0, 8, ub)
                a_cross_exp(1, 0, ua)
                a_cross_exp(1, 1, ua)
                b_tanh_first("h21", hE[:, 0], 2, 10, ub)
                for s in range(SLOTS):
                    a_copy_turned(1, s, ua, "y", LC)
                b_tanh_first("hg", gs, 0, 12, ub)
                a_copy_outputs("o2", oT2, ua)
                b_gate_tanh(ub)

            act.wait_ge(init_read, 1)
            act.activation(tanhT[:, :, :], cols[:, COLS["cond"]:COLS["cond"] + NB * CB].rearrange("p (b k) -> p k b", k=CB),
                           ACT.Tanh, scale=0.5).then_inc(init_tanh, 1)
            act.wait_ge(doneA, 1)
            stage_a(0)
            act.wait_ge(prepared_b, 1)
            with act.Fori(0, NB) as b:
                both(b * UNITS + 1, b * UNITS, first=b)
                with act.Fori(1, UNITS - 1) as r:
                    u = b * UNITS + r
                    both(u + 1, u)
                both(b * UNITS + UNITS, b * UNITS + (UNITS - 1), last=b + 1)

        @block.gpsimd
        def _(pool):
            def rstd_of(i, eps, u):
                pool.wait_ge(stats[i], u * 4 + 4)
                alone(pool)
                pool.tensor_scalar(vare[i][:, :], mv[i][:, :, 1], eps, None, ALU.add).then_inc(rstds[i], 1)
                pool.wait_ge(rstds[i], u * 2 + 1)
                pool.tensor_tensor(rstd[i][:, :], vare[i][:, :], neghalf[:, :], ALU.pow).then_inc(rstds[i], 1)

            def a_shift(t, s, u):
                pool.wait_ge(topk, u * TOPK_PER_UNIT + (topk_base(t, s) + HPS))
                g = slice(s * HPS, (s + 1) * HPS)
                pool.tensor_tensor(Dx[:, t, g, :], S[:, t, g, :], M1[:, t, g, 0:1].to_broadcast([P, HPS, LC]), ALU.subtract)\
                    .then_inc(shifted, 1)

            def gate_a(b):
                for n, (dst, w) in enumerate(((Wso_g, Wso), (Wco_g, Wco))):
                    for k in range(CB):
                        pool.tensor_tensor(dst[:, k, :], w[:, k, :], Gall[:, bass.ds((b & 3) * 3 + n, 1), :]
                                           .rearrange("p a c -> p (a c)"), ALU.mult).then_inc(gatedA, 1)

            def gate_b(b):
                pool.wait_ge(wm2_loaded, b * 16 + 16)
                for k in range(HJ):
                    pool.tensor_tensor(Wm2_g[:, k, :], Wm2_g[:, k, :], Gall[:, bass.ds((b & 3) * 3 + 2, 1), :]
                                       .rearrange("p a c -> p (a c)"), ALU.mult).then_inc(gatedB, 1)

            def cross(u):
                for t in range(TILES):
                    for s in range(SLOTS):
                        a_shift(t, s, u)
                        if (t, s) == (1, 1):
                            rstd_of(0, EPS0, u + 1)

            def stage_a(u):
                rstd_of(1, EPS0, u)
                cross(u)

            def both(ua, ub, first=None, last=None):
                rstd_of(2, EPS0, ub)
                if first is not None:
                    gate_b(first)
                if last is not None:
                    wait_full(pool, "co", ub)
                    alone(pool)
                    gate_a(last)
                rstd_of(1, EPS0, ua)
                rstd_of(3, EPS1, ub)
                cross(ua)

            pool.memset(ident[:, :], 0.0).then_inc(consts, 1)
            pool.memset(maskE[:, :], 0.0).then_inc(consts, 1)
            pool.memset(maskO[:, :], 0.0).then_inc(consts, 1)
            pool.memset(neghalf[:, :], -0.5).then_inc(consts, 1)
            pool.memset(ones3[:, :], 1.0).then_inc(consts, 1)
            pool.memset(va[:, :, :, :], 1.0).then_inc(consts, 1)
            pool.memset(vc[:, :, :], 1.0).then_inc(consts, 1)
            pool.memset(bias3[:, :, :], 0.0).then_inc(consts, 1)
            pool.wait_ge(consts, 8)
            pool.affine_select(out=ident[:, :], in_=ident[:, :], compare_op=ALU.not_equal, fill=1.0, base=0,
                               pattern=[[-1, P]], channel_multiplier=1).then_inc(consts, 1)
            pool.wait_ge(consts, 9)
            rstd_of(0, EPS0, 0)
            pool.wait_ge(init_read, 9)
            gate_a(0)
            stage_a(0)
            pool.wait_ge(prepared_b, 1)
            with pool.Fori(0, NB) as b:
                both(b * UNITS + 1, b * UNITS, first=b)
                with pool.Fori(1, UNITS - 1) as r:
                    u = b * UNITS + r
                    both(u + 1, u)
                both(b * UNITS + UNITS, b * UNITS + (UNITS - 1), last=b + 1)

        @block.vector
        def _(dve):
            step = [0]

            def chain(i):
                step[0] += 1
                i.then_inc(dve_step, 1)
                dve.wait_ge(dve_step, step[0])

            def read_job(k, *ops):
                dve.wait_ge(init_full, k + 1)
                for o in ops[:-1]:
                    o()
                ops[-1]().then_inc(init_read, 1)

            def three_parts(np_, r0, r1):
                n = r1 - r0
                cur = rows[0:np_, r0:r1, :]
                part, rest = split_b[0:np_, 0:n, :], split[0:np_, 0:n, :]
                for p in range(3):
                    chain(dve.tensor_copy(part, cur))
                    chain(dve.tensor_copy(bias3[32 * p:32 * p + np_, r0:r1, :], part))
                    if p < 2:
                        chain(dve.tensor_tensor(rest, cur, part, ALU.subtract))
                        cur = rest

            def prep_weights():
                dve.wait_ge(consts, 9)
                for m, o in ((maskE, 0), (maskO, D)):
                    cv = ident[:, :].rearrange("p (s d) -> p s d", d=32)[:, :, o:o + D]
                    dve.tensor_reduce(m[:, :], cv, AX.XY, ALU.add).then_inc(dve_step, 1)
                step[0] += 2
                chain(dve.tensor_copy(onehot[:, :, :], ident[0:NB, 0:NB].rearrange("p (b a) -> p b a", a=1).to_broadcast([NB, NB, P])))
                chain(dve.tensor_tensor(chosen[:, :], ident[0:96, 0:NB], ident[0:96, 32:32 + NB], ALU.add))
                chain(dve.tensor_tensor(chosen[:, :], chosen[:, :], ident[0:96, 64:64 + NB], ALU.add))
                chain(dve.tensor_copy(choose[:, :, :], chosen[:, :].rearrange("p (b a) -> p b a", a=1).to_broadcast([96, NB, P])))
                read_job(0, lambda: dve.tensor_copy(cols[:, :], psum[0][:, 0:NCOL]))
                dve.wait_ge(init_tanh, 1)
                dve.wait_ge(init_read, 1)
                cond_cols = cols[:, COLS["cond"]:COLS["cond"] + NB * CB].rearrange("p (b k) -> p k b", k=CB)
                chain(dve.scalar_tensor_tensor(siluT[:, :, :], tanhT[:, :, :], 1.0, cond_cols, ALU.add, ALU.mult))
                dve.tensor_scalar(siluT[:, :, :], siluT[:, :, :], 0.5, None, ALU.mult).then_inc(silu_ready, 1)
                for n, col in enumerate((COLS["qkv"] + 2 * CB, COLS["kv"] + CB)):
                    chain(dve.tensor_copy(bv4[:, n], cols[:, col:col + CB].rearrange("p (k a) -> p k a", a=1).to_broadcast([P, CB, NB])))
                chain(dve.tensor_scalar(b1half[:, :], cols[:, COLS["m1"]:COLS["m1"] + HJ], 0.5, None, ALU.mult))
                for e, m in enumerate((maskE, maskO)):
                    chain(dve.tensor_scalar(kbias[:, e, :], cols[:, COLS["qkv"] + CB:COLS["qkv"] + 2 * CB], m[:, 0:1], None, ALU.mult))
                dve.tensor_copy(condT[:, :, :], cond_cols).then_inc(helpers_ready, 1)
                a_load(0)
                ln_stats(0, xin, 0)
                ln_apply(0, xin, xnA, 0)
                dve.wait_ge(rows_loaded, 16 * len(rows_loads))
                for n in range(5):
                    s0, s1 = 2 * n, min(2 * n + 2, 9)
                    v = ada[:, s0:s1, :].rearrange("b s c -> b (s c)")
                    read_job(1 + n, lambda: dve.tensor_tensor(v, psum[1 + n][0:NB, 0:(s1 - s0) * C], v, ALU.add))
                so_co = rows[:, 0:2, :].rearrange("b n c -> b (n c)")
                read_job(6, lambda: dve.tensor_tensor(so_co, psum[6][0:NB, :], so_co, ALU.add))

                def read_mods():
                    v = psum[7][:, 0:12 * NB].rearrange("p (n b) -> p b n", b=NB)
                    for n, one in enumerate((1.0, 0.0, 1.0, 0.0, 1.0, 0.0)):
                        i = dve.tensor_scalar(mods[:, :, n * CB:(n + 1) * CB], v[:, :, n * CB:(n + 1) * CB], one, None, ALU.add)
                    return i

                read_job(7, read_mods)
                read_job(8, lambda: dve.tensor_copy(Gall[:, 0:2, :].rearrange("p g c -> p (g c)"), psum[0][:, :]))
                dve.wait_ge(init_read, 9)
                for i in range(3):
                    chain(dve.tensor_tensor(rows[:, i, :], rows[:, i, :], ada[:, 3 * i + 2, :], ALU.mult))
                prep_a(0)

            def prep_bias_rows():
                three_parts(NB, 0, 3)
                dve.tensor_copy(M2[0:1, 2, 0:1], rows[0:1, 0, 0:1]).then_inc(prepared, 1)

            def read_fold(name, *ops):
                n = FOLD_JOBS.index(name)
                dve.wait_ge(fold_full, n + 1)
                for o in ops[:-1]:
                    o(psum[5 + n % 3])
                ops[-1](psum[5 + n % 3]).then_inc(fold_read, 1)

            def fold_gates(b):
                read_fold(f"G{b}", lambda bk: dve.tensor_copy(Gall[:, b * 3:b * 3 + 2, :].rearrange("p g c -> p (g c)"), bk[:, :]))

            def fold_mlp_gates(n):
                read_fold(f"M{n}", *[lambda bk, i=i: dve.tensor_scalar(Gall[:, (2 * n + i) * 3 + 2, :], bk[:, i * C:(i + 1) * C], 0.5, None, ALU.mult)
                                     for i in range(2)])

            def fold_router():
                dve.wait_ge(folded_loaded, 16 * len(folded_loads))
                dve.tensor_copy(GpR[:, :, LC:LC + E], Rw[:, 0:CB, :])
                read_fold("r0", lambda bk: dve.tensor_tensor(rrow[:, :], bk[0:NB, 0:E], rrow[:, :], ALU.add))
                read_fold("r1", lambda bk: dve.tensor_copy(rbias_all[:, :, :].rearrange("p b e -> p (b e)"), bk[:, 0:NB * E]))

            def fold_expert_biases():
                dve.wait_ge(folded_loaded, 16 * len(folded_loads))
                e0 = BIAS.index("e0")
                read_fold("b01", *[lambda bk, e=e: dve.tensor_tensor(rows[0:1, e0 + e, :], bk[0:1, e * C:(e + 1) * C], out_row[:, :], ALU.add)
                                   for e in range(2)])
                read_fold("b2", lambda bk: dve.tensor_tensor(rows[0:1, e0 + 2, :], bk[0:1, 0:C], out_row[:, :], ALU.add))
                dve.wait_ge(fold_read, FOLD_JOBS.index("b2") + 1)
                chain(dve.tensor_scalar(rows[0:1, e0:e0 + E, :], rows[0:1, e0:e0 + E, :], 0.5, None, ALU.mult))

            def fold_turn_qk():
                for name, w in (("wk", wkT), ("wq", wqT)):
                    read_fold(name, lambda bk: dve.tensor_copy(w[:, :, :].rearrange("p h c -> p (h c)"), bk[:, :]))

            def fold_qk():
                read_fold("MT", lambda bk: dve.tensor_copy(MT[:, :, :].rearrange("p h c -> p (h c)"), bk[:, :]))

            def fold_anchor():
                def read(bk):
                    v = bk[:, 0:W1B * NB].rearrange("p (n b) -> p b n", b=NB)
                    b1 = cols[:, COLS["e_b1"]:COLS["e_b1"] + W1B]
                    for b in range(NB):
                        i = dve.tensor_tensor(betas[:, b, :], v[:, b, :], b1, ALU.add)
                    return i

                read_fold("anchor", read)

            def fold_turn_second(e):
                for h in range(CB):
                    read_fold(f"t{e}{h}", lambda bk: dve.tensor_copy(e2T[h], bk[:, :]))

            def fold_second(e):
                for k2 in range(RB // 2):
                    k = e * RB + 2 * k2
                    read_fold(f"p{e}{k2}", lambda bk: dve.tensor_scalar(W2p[:, k:k + 2, :].rearrange("p k c -> p (k c)"), bk[:, :], 0.25, None, ALU.mult))

            def prepared_for_b():
                dve.wait_ge(wb_loaded, 16 * (len(wb_loads) + len(evidence_loads)))
                dve.tensor_scalar(Wg2[:, :, :], Wg2[:, :, :], 0.5, None, ALU.mult).then_inc(prepared_b, 1)

            def prep_a(b):
                bb = b & 3
                dve.tensor_copy(modC[:, :], mods[:, bass.ds(bb, 1), 4:8].rearrange("p a n -> p (a n)")).then_inc(stepA, 1)
                dve.tensor_copy(chooseA[:, :], choose[:, bass.ds(bb, 1), :].rearrange("p a n -> p (a n)")).then_inc(doneA, 1)

            def context_turned(b):
                dve.wait_ge(fullA, b * 3 + 1)
                alone(dve)
                dve.tensor_copy(ctxT[:, :, :].rearrange("p k c -> p (k c)"), psum[3][:, 0:CB * LC]).then_inc(readA, 1)

            def context_keys(b):
                dve.wait_ge(fullA, b * 3 + 2)
                alone(dve)
                for f in range(CB):
                    for e, m in enumerate((maskE, maskO)):
                        c = COLS["kv"] + f
                        i = dve.tensor_scalar(kc[:, e, f, :], psum[3][:, f * LC:(f + 1) * LC], cols[:, c:c + 1], m[:, 0:1],
                                              ALU.add, ALU.mult)
                i.then_inc(readA, 1)

            def context_values(b):
                dve.wait_ge(fullA, b * 3 + 3)
                alone(dve)
                dve.tensor_copy(vc[:, :, 0:D], psum[3][0:LC, 0:C].rearrange("p (h d) -> p h d", h=H)).then_inc(readA, 1)

            def prep_b(b):
                dve.tensor_copy(modB[:, :], mods[:, bass.ds(b, 1), 8:12].rearrange("p a n -> p (a n)")).then_inc(stepB, 1)
                dve.tensor_copy(chooseB[:, :], choose[:, bass.ds(b, 1), :].rearrange("p a n -> p (a n)")).then_inc(stepB, 1)
                dve.tensor_copy(rbias[:, :], rbias_all[:, bass.ds(b, 1), :].rearrange("p a n -> p (a n)")).then_inc(stepB, 1)
                dve.tensor_copy(betaF[:, :], betas[:, bass.ds(b, 1), :].rearrange("p a n -> p (a n)")).then_inc(stepB, 1)
                dve.wait_ge(stepB, b * 4 + 4)
                alone(dve)
                dve.tensor_scalar(betaH[:, :], betaF[:, :], 0.5, None, ALU.mult).then_inc(doneB, 1)

            def prep_b_context(b):
                dve.wait_ge(fullB, b * 5 + 1)
                alone(dve)
                dve.tensor_copy(vT1[:, :, :].rearrange("p k c -> p (k c)"), psum[3][:, 0:CB * LC])
                dve.tensor_copy(GpR[:, :, 0:LC], psum[3][:, C:C + CB * LC].rearrange("p (k c) -> p k c", k=CB)).then_inc(readB, 1)

            def prep_b_evidence(b, k):
                dve.wait_ge(fullB, b * 5 + 2 + k)
                alone(dve)
                c0, c1 = k * 512, min((k + 1) * 512, W1N + E)
                dve.tensor_copy(Vp[:, c0:c1], psum[(7, 6, 5, 3)[k]][0:LC, 0:c1 - c0]).then_inc(readB, 1)

            def ln_stats(i, src, u):
                for t in range(TILES):
                    dve.bn_stats(stat[i][:, t, :], src[:, t, :]).then_inc(stats[i], 1)
                dve.wait_ge(stats[i], u * 4 + 2)
                alone(dve)
                for t in range(TILES):
                    dve.bn_aggr(mv[i][:, t, :], stat[i][:, t, :]).then_inc(stats[i], 1)

            def ln_apply(i, src, dst, u):
                dve.wait_ge(rstds[i], u * 2 + 2)
                dve.wait_ge(stats[i], u * 4 + 4)
                for t in range(TILES):
                    dve.tensor_scalar(dst[:, t, :], src[:, t, :], mv[i][:, t, 0:1], rstd[i][:, t:t + 1], ALU.subtract, ALU.mult)\
                       .then_inc(normed[i], 1)

            def a_bias_queries(u):
                wait_full(dve, "q", u)
                for f in range(CB):
                    c = COLS["qkv"] + f
                    i = dve.tensor_scalar(qT[:, f, :], bank_of("q")[:, f * UT:(f + 1) * UT], cols[:, c:c + 1], None, ALU.add)
                    if f == 0:
                        i.then_inc(q_half, 1)
                i.then_inc(drained[JOB["q"][0]], 1)

            def slot_scores(s):
                return psum[s][:, :].rearrange("p (i k) -> p i k", i=HPS)

            def a_max(t, s, u):
                wait_full(dve, f"s{t}{s}", u)
                dve.tensor_reduce(rmax[:, t, s * HPS:(s + 1) * HPS], slot_scores(s), AX.X, ALU.max).then_inc(row_max, 1)

            def a_subtract(t, s, u):
                dve.wait_ge(row_max, u * (TILES * SLOTS) + (t * SLOTS + s + 1))
                dve.tensor_tensor(prob[:, s], slot_scores(s), rmax[:, t, s * HPS:(s + 1) * HPS].rearrange("p (i a) -> p i a", a=1)
                                  .to_broadcast([P, HPS, P]), ALU.subtract).then_inc(drained[s], 1)

            def a_softmax(t, slots, u):
                for n, s in enumerate(slots):
                    a_max(t, s, u)
                    if n:
                        a_subtract(t, slots[n - 1], u)
                a_subtract(t, slots[-1], u)

            def a_normalise(n, name, dst, t, u):
                wait_full(dve, name, u)
                v = psum[4][:, 0:H * DV].rearrange("p (h d) -> p h d", h=H)
                dve.reciprocal(rsum[:, t, :], v[:, :, D]).then_inc(sums_inverted, 1)
                dve.wait_ge(sums_inverted, u * 4 + n + 1)
                dve.tensor_tensor(dst[:, t, :].rearrange("p (h d) -> p h d", h=H), v[:, :, 0:D],
                                  rsum[:, t, :].rearrange("p (h a) -> p h a", a=1).to_broadcast([P, H, D]), ALU.mult)\
                   .then_inc(drained[4], 1)

            def a_residual(dst, src, name, u):
                wait_full(dve, name, u)
                dve.tensor_tensor(dst[:, :, :].rearrange("p t c -> p (t c)"), src[:, :, :].rearrange("p t c -> p (t c)"),
                                  bank_of(name)[:, :], ALU.add).then_inc(drained[JOB[name][0]], 1)

            def a_topk(t, s, u, steps=(0, 1, 2, 3)):
                if 0 in steps:
                    wait_drained(dve, f"c{t}{s}", u)
                base = u * TOPK_PER_UNIT + topk_base(t, s)
                if 0 in steps:
                    alone(dve)

                def phase(n, one):
                    if n not in steps:
                        return
                    for i in range(HPS):
                        if n and i % 2 == 0:
                            dve.wait_ge(topk, base + ((n - 1) * HPS + i + 2))
                            alone(dve)
                        one(s * HPS + i).then_inc(topk, 1)

                phase(0, lambda h: dve.max(M1[:, t, h, :], S[:, t, h, :]))
                phase(1, lambda h: dve.match_replace(K[:, h, :], M1[:, t, h, :], S[:, t, h, :], KNOCKED))
                phase(2, lambda h: dve.max(M2[:, h, :], K[:, h, :]))
                phase(3, lambda h: dve.match_replace(K[:, h, :], M2[:, h, :], K[:, h, :], KNOCKED))

            def a_pick(t, half, u):
                dve.wait_ge(cross_exp, u * (TILES * 2) + (2 * t + half + 1))
                dve.wait_ge(topk, u * TOPK_PER_UNIT + topk_base(t, 2 * half + 1) + 4 * HPS)
                g = slice(half * (H // 2), (half + 1) * (H // 2))
                dve.scalar_tensor_tensor(Dx[:, t, g].rearrange("p h c -> p (h c)"), K[:, g, :].rearrange("p h c -> p (h c)"), KNOCKED_BELOW,
                                         Dx[:, t, g].rearrange("p h c -> p (h c)"), ALU.is_lt, ALU.mult).then_inc(picked, 1)

            def b_swiglu(j, u):
                name = f"m{j}"
                w = tb_of(name)
                dve.wait_ge(tanh_done, u * len(TANH_ORDER) + (TANH_ORDER.index(name) + 1))
                dve.scalar_tensor_tensor(gT[:, j, :], tb[w][:, 0:UT], 1.0, gT[:, j, :], ALU.add, ALU.mult).then_inc(half_gated, 1)
                dve.wait_ge(half_gated, u * HJ + (j + 1))
                c = COLS["m1"] + HJ + j
                dve.scalar_tensor_tensor(gT[:, j, :], bank_of(name)[:, UT:2 * UT], cols[:, c:c + 1], gT[:, j, :], ALU.add, ALU.mult)\
                   .then_inc(drained[JOB[name][0]], 1)

            def b_silu(name, dst, d0, u):
                wait_drained(dve, name, u)
                o = dst[:, d0:d0 + 2, :].rearrange("p k t -> p (k t)")
                dve.scalar_tensor_tensor(o, tb[tb_of(name)][:, :], 1.0, o, ALU.add, ALU.mult).then_inc(gated, 1)

            def b_proto_shift(u):
                wait_full(dve, "ps", u)
                both = psum[7][:, 0:TILES * (LC + E)].rearrange("p (t c) -> p t c", t=TILES)
                v = both[:, :, 0:LC]
                dve.tensor_reduce(pm[:, :], v, AX.X, ALU.max).then_inc(proto_max, 1)
                dve.tensor_tensor(rn[:, :, :], both[:, :, LC:LC + E], rbias[:, :].rearrange("p (a e) -> p a e", a=1).to_broadcast([P, TILES, E]), ALU.add)\
                   .then_inc(route_nx, 1)
                dve.wait_ge(proto_max, u + 1)
                dve.tensor_tensor(pw[:, :, :], v, pm[:, :].rearrange("p (t a) -> p t a", a=1).to_broadcast([P, TILES, LC]),
                                  ALU.subtract).then_inc(drained[7], 1)

            def b_proto_norm(u):
                dve.wait_ge(proto_exp, u + 1)
                dve.tensor_reduce(psu[:, :], pw[:, :, :], AX.X, ALU.add).then_inc(proto_steps, 1)
                dve.wait_ge(proto_steps, u * 3 + 1)
                dve.reciprocal(psu[:, :], psu[:, :]).then_inc(proto_steps, 1)
                dve.wait_ge(proto_steps, u * 3 + 2)
                dve.tensor_tensor(pw[:, :, :], pw[:, :, :], psu[:, :].rearrange("p (t a) -> p t a", a=1).to_broadcast([P, TILES, LC]),
                                  ALU.mult).then_inc(proto_steps, 1)

            def b_route_shift(u):
                wait_full(dve, "rt", u)
                v = psum[7][:, 0:TILES * E].rearrange("p (t c) -> p t c", t=TILES)
                dve.wait_ge(route_nx, u + 1)
                dve.tensor_tensor(rl[:, :, :], v, rn[:, :, :], ALU.add)\
                   .then_inc(drained[7], 1)
                wait_drained(dve, "rt", u)
                dve.tensor_reduce(rm[:, :], rl[:, :, :], AX.X, ALU.max).then_inc(route_steps, 1)
                dve.wait_ge(route_steps, u * 5 + 1)
                dve.tensor_tensor(rl[:, :, :], rl[:, :, :], rm[:, :].rearrange("p (t a) -> p t a", a=1).to_broadcast([P, TILES, E]),
                                  ALU.subtract).then_inc(route_steps, 1)

            def b_route_norm(u):
                dve.wait_ge(route_exp, u + 1)
                dve.tensor_reduce(rs[:, :], rl[:, :, :], AX.X, ALU.add).then_inc(route_steps, 1)
                dve.wait_ge(route_steps, u * 5 + 3)
                dve.reciprocal(rs[:, :], rs[:, :]).then_inc(route_steps, 1)
                dve.wait_ge(route_steps, u * 5 + 4)
                dve.tensor_tensor(rp[:, :, :], rl[:, :, :], rs[:, :].rearrange("p (t a) -> p t a", a=1).to_broadcast([P, TILES, E]),
                                  ALU.mult).then_inc(route_steps, 1)

            def b_mix(e, u):
                wait_full(dve, f"e{e}", u)
                if e == 0:
                    dve.wait_ge(route_steps, u * 5 + 5)
                    dve.wait_ge(y_stored, u * 48 + 16)
                else:
                    wait_drained(dve, f"e{e - 1}", u)
                for t in range(TILES):
                    o, v = acc[:, t, :], psum[7][:, t * C:(t + 1) * C]
                    if e == 0:
                        i = dve.tensor_scalar(o, v, rp[:, t, 0:1], None, ALU.mult)
                    else:
                        i = dve.scalar_tensor_tensor(o, v, rp[:, t, e:e + 1], o, ALU.mult, ALU.add)
                i.then_inc(drained[7], 1)

            def b_finish(u):
                wait_drained(dve, "g2", u)
                flat = lambda a: a[:, :, :].rearrange("p t c -> p (t c)")
                dve.scalar_tensor_tensor(flat(acc), tg[:, :], 1.0, flat(acc), ALU.add, ALU.mult).then_inc(mixed, 1)
                dve.wait_ge(mixed, u + 2)
                dve.tensor_tensor(flat(acc), flat(x2), flat(acc), ALU.add).then_inc(y_ready, 1)

            def a_load(u):
                dve.wait_ge(x_loaded, u * 48 + 48)

            def a_norm_input(u):
                a_load(u)
                ln_stats(0, xin, u)
                wait_drained(dve, "ln1", u - 1)
                alone(dve)
                dve.tensor_copy(modS[:, :], mods[:, bass.ds((u >> 2) & 3, 1), 0:4].rearrange("p a n -> p (a n)")).then_inc(mod_ready, 1)

            def first_unit(u):
                dve.tensor_copy(modS[:, :], mods[:, 0, 0:4]).then_inc(mod_ready, 1)
                prep_bias_rows()
                context_turned(0)
                a_bias_queries(u)
                context_keys(0)
                context_values(0)
                a_softmax(0, range(SLOTS), u)
                fold_turn_qk()
                fold_qk()
                a_softmax(1, range(SLOTS), u)
                fold_turn_second(0)
                fold_second(0)
                a_normalise(0, "pv0", on, 0, u)
                fold_turn_second(1)
                fold_second(1)
                fold_turn_second(2)
                a_normalise(1, "pv1", on, 1, u)
                wait_drained(dve, "pv1", u)
                for count in (full[4], drained[4]):
                    dve.sem_inc(count, 1)
                fold_second(2)
                fold_expert_biases()
                a_residual(x1, xin, "so", u)
                wait_drained(dve, "so", u)
                ln_stats(1, x1, u)
                for b in range(1, NB):
                    fold_gates(b)
                ln_apply(1, x1, xnA, u)
                fold_router()
                for n in range(2):
                    fold_mlp_gates(n)
                for s in range(SLOTS):
                    a_topk(0, s, u)
                a_pick(0, 0, u)
                a_topk(1, 0, u)
                a_pick(0, 1, u)
                a_topk(1, 1, u)
                fold_anchor()
                a_norm_input(u + 1)
                a_topk(1, 2, u)
                wait_full(dve, "ln2", u)
                ln_apply(0, xin, xnA, u + 1)
                a_topk(1, 3, u)
                a_pick(1, 0, u)
                a_pick(1, 1, u)
                a_normalise(2, "xv0", on2, 0, u)
                three_parts(1, BIAS.index("e0"), len(BIAS))
                a_normalise(3, "xv1", on2, 1, u)
                prepared_for_b()
                a_residual(x2, x1, "co", u)
                wait_drained(dve, "co", u)

            def both(ua, ub, first=None, last=None):
                ln_stats(2, x2, ub)
                if first is not None:
                    prep_b_context(first)
                if last is not None:
                    context_turned(last)
                a_bias_queries(ua)
                ln_apply(2, x2, xnB, ub)
                if first is not None:
                    prep_b(first)
                if last is not None:
                    prep_a(last)
                if first is not None:
                    prep_b_evidence(first, 0)
                    prep_b_evidence(first, 1)
                if last is not None:
                    context_keys(last)
                if first is not None:
                    prep_b_evidence(first, 2)
                    prep_b_evidence(first, 3)
                if last is not None:
                    context_values(last)
                a_softmax(0, range(SLOTS), ua)
                b_swiglu(0, ub)
                b_swiglu(1, ub)
                a_softmax(1, (0, 1), ua)
                b_swiglu(2, ub)
                a_softmax(1, (2, 3), ua)
                b_swiglu(3, ub)
                b_swiglu(4, ub)
                a_normalise(0, "pv0", on, 0, ua)
                b_swiglu(5, ub)
                a_normalise(1, "pv1", on, 1, ua)
                a_residual(x1, xin, "so", ua)
                wait_drained(dve, "so", ua)
                ln_stats(1, x1, ua)
                b_swiglu(6, ub)
                ln_apply(1, x1, xnA, ua)
                b_swiglu(7, ub)
                a_residual(x2, x2, "mo", ub)
                wait_drained(dve, "mo", ub)
                ln_stats(3, x2, ub)
                a_topk(0, 0, ua, (0,))
                ln_apply(3, x2, xnB, ub)
                a_topk(0, 0, ua, (1, 2, 3))
                a_topk(0, 1, ua, (0, 1))
                b_proto_shift(ub)
                a_topk(0, 1, ua, (2, 3))
                b_proto_norm(ub)
                a_topk(0, 2, ua)
                b_route_shift(ub)
                a_topk(0, 3, ua, (0, 1))
                b_silu("h00", hE[:, 0], 0, ub)
                b_route_norm(ub)
                a_topk(0, 3, ua, (2, 3))
                b_silu("h01", hE[:, 0], 2, ub)
                a_pick(0, 0, ua)
                a_topk(1, 0, ua)
                a_pick(0, 1, ua)
                a_topk(1, 1, ua)
                b_silu("h10", hE[:, 1], 0, ub)
                b_mix(0, ub)
                a_norm_input(ua + 1)
                b_silu("h11", hE[:, 1], 2, ub)
                a_topk(1, 2, ua)
                wait_full(dve, "ln2", ua)
                ln_apply(0, xin, xnA, ua + 1)
                a_topk(1, 3, ua)
                b_silu("h20", hE[:, 0], 0, ub)
                a_pick(1, 0, ua)
                a_pick(1, 1, ua)
                a_normalise(2, "xv0", on2, 0, ua)
                b_mix(1, ub)
                b_silu("h21", hE[:, 0], 2, ub)
                b_silu("hg", gs, 0, ub)
                a_normalise(3, "xv1", on2, 1, ua)
                b_mix(2, ub)
                b_finish(ub)
                dve.wait_ge(y_ready, ub + 1)
                a_residual(x2, x1, "co", ua)
                wait_drained(dve, "co", ua)
                alone(dve)

            prep_weights()
            first_unit(0)
            with dve.Fori(0, NB) as b:
                both(b * UNITS + 1, b * UNITS, first=b)
                with dve.Fori(1, UNITS - 1) as r:
                    u = b * UNITS + r
                    both(u + 1, u)
                both(b * UNITS + UNITS, b * UNITS + (UNITS - 1), last=b + 1)


_INS = ["x", "cond_1024", "ctx_1024"] + \
       ["L0_xcond_" + n for n in ("w_ada", "b_ada", "w_qkv", "b_qkv", "w_so", "b_so", "w_q", "b_q", "w_kv", "b_kv", "w_co", "b_co",
                                  "w_m1", "b_m1", "w_m2", "b_m2")] + \
       ["L1_xcond_" + n for n in ("ln_gamma", "ln_beta", "Wq", "Wk", "Wv", "router_W", "router_b", "e_w1", "e_b1", "e_w2", "e_b2",
                                  "gate_w1", "gate_b1", "gate_w2", "gate_b2", "out_w", "out_b")]
_OUT = (NB, L, C)


def kernel(**inputs):
    import numpy as _np
    import concourse.bacc as _bacc
    from concourse import mybir as _mybir
    from concourse.bass_utils import run_bass_kernel_spmd as _run

    nc = _bacc.Bacc("TRN2", target_bir_lowering=False, num_devices=1)
    arrays, args = {}, []
    for name in _INS:
        a = _np.ascontiguousarray(inputs[name])
        arrays[f"in_{name}_dram"] = a
        args.append(nc.dram_tensor(f"in_{name}_dram", a.shape, _mybir.dt.from_np(a.dtype), kind="ExternalInput").ap())
    args.append(nc.dram_tensor("out_dram", _OUT, _mybir.dt.float32, kind="ExternalOutput").ap())
    bass_pixart_experts(nc, *args)
    r = _run(nc, [arrays], core_ids=[0])
    return r.results[0]["out_dram"]
```
